# Optimizing a Trainium2 kernel written in Bass

```python
import numpy as np
import jax
import jax.numpy as jnp

def _softmax(x, axis=-1):
    return jax.nn.softmax(x, axis=axis)

def _gelu(x):
    return jax.nn.gelu(x, approximate=True)

def _silu(x):
    return jax.nn.silu(x)

def _sigmoid(x):
    return jax.nn.sigmoid(x)

def _layernorm(x, axis=-1, eps=1e-05):
    m = jnp.mean(x, axis=axis, keepdims=True)
    v = jnp.var(x, axis=axis, keepdims=True)
    return (x - m) / jnp.sqrt(v + eps)

def _scatter_add(tgt, idx, src, axis=0):
    return tgt.at[idx].add(src)

def _segment_sum(src, seg, n):
    return jax.ops.segment_sum(src, seg, n)
kernel_name = 'mk_adaln_d2_jaxref_r8_18d290'

def setup_inputs(seed: int=0):
    np.random.seed(seed)
    _w = jnp.asarray

    def _L0_attn_setup():
        import jax, jax.numpy as jnp
        import numpy as np
        B, N, EMBED, HEADS = (1, 256, 128, 16)
        HD = EMBED // HEADS
        BASE = 10000.0
        EPS = 1e-05

        def _rope(t):
            d = t.shape[-1]
            n = t.shape[-2]
            inv_freq = 1.0 / BASE ** (jnp.arange(0, d, 2, dtype=jnp.float32) / d)
            pos = jnp.arange(n, dtype=jnp.float32)
            ang = pos[:, None] * inv_freq[None, :]
            cos = jnp.concatenate([jnp.cos(ang), jnp.cos(ang)], axis=-1)
            sin = jnp.concatenate([jnp.sin(ang), jnp.sin(ang)], axis=-1)
            t1, t2 = (t[..., :d // 2], t[..., d // 2:])
            rot = jnp.concatenate([-t2, t1], axis=-1)
            return t * cos + rot * sin
        key = jax.random.key(seed)
        ks = jax.random.split(key, 7)
        s = EMBED ** (-0.5)
        return {'x': jax.random.normal(ks[0], (B, N, EMBED), dtype=jnp.float32), 'Wq': jax.random.normal(ks[1], (EMBED, EMBED), dtype=jnp.float32) * s, 'Wk': jax.random.normal(ks[2], (EMBED, EMBED), dtype=jnp.float32) * s, 'Wv': jax.random.normal(ks[3], (EMBED, EMBED), dtype=jnp.float32) * s, 'Wo': jax.random.normal(ks[4], (EMBED, EMBED), dtype=jnp.float32) * s, 'Wg1': jax.random.normal(ks[5], (EMBED, HD), dtype=jnp.float32) * s, 'Wg2': jax.random.normal(ks[6], (HD, EMBED), dtype=jnp.float32) * HD ** (-0.5), 'ln_w': jnp.ones((EMBED,), dtype=jnp.float32), 'ln_b': jnp.zeros((EMBED,), dtype=jnp.float32)}
    _L0_attn_in = _L0_attn_setup()

    def _L0_ffn_setup():
        import jax, jax.numpy as jnp
        import numpy as np
        B, S, H = (2, 256, 128)
        E_DYN, E_FIX = (8, 1)
        I_DYN, I_FIX = (64, 256)
        TOP_K = 4
        TOP_P = 0.75
        JITTER_EPS = 0.1
        CAPACITY_FACTOR = 1.25
        MIN_CAPACITY = 4

        def _sparse_mixer(scores):
            T = scores.shape[0]
            rows = jnp.arange(T)
            masked_scores = scores
            mults, sels = ([], [])
            for _ in range(TOP_K):
                thr = jnp.max(masked_scores, axis=-1, keepdims=True)
                sel = jnp.argmax(masked_scores, axis=-1)
                factor = jnp.maximum(jnp.abs(scores), jnp.abs(thr))
                jmask = (thr - scores) / factor > 2.0 * JITTER_EPS
                gates = jax.nn.softmax(jnp.where(jmask, -jnp.inf, masked_scores), axis=-1)
                mult = jnp.take_along_axis(gates, sel[:, None], axis=-1)[:, 0]
                masked_scores = masked_scores.at[rows, sel].set(-jnp.inf)
                mults.append(mult)
                sels.append(sel)
            return (jnp.stack(mults, axis=-1), jnp.stack(sels, axis=-1))
        key = jax.random.key(seed)
        k = jax.random.split(key, 8)
        sc = 0.02
        return {'hidden_states': jax.random.normal(k[0], (B, S, H), jnp.float32), 'gate_w': jax.random.normal(k[1], (E_DYN + E_FIX, H), jnp.float32) * sc, 'dyn_gate_w': jax.random.normal(k[2], (E_DYN, I_DYN, H), jnp.float32) * sc, 'dyn_up_w': jax.random.normal(k[3], (E_DYN, I_DYN, H), jnp.float32) * sc, 'dyn_down_w': jax.random.normal(k[4], (E_DYN, H, I_DYN), jnp.float32) * sc, 'sh_gate_w': jax.random.normal(k[5], (E_FIX, I_FIX, H), jnp.float32) * sc, 'sh_up_w': jax.random.normal(k[6], (E_FIX, I_FIX, H), jnp.float32) * sc, 'sh_down_w': jax.random.normal(k[7], (E_FIX, H, I_FIX), jnp.float32) * sc}
    _L0_ffn_in = _L0_ffn_setup()
    _L0_c = _w((lambda *s: np.random.randn(*s).astype(np.float32) * 0.05)(8, 128))
    _L0_wmod = _w((lambda *s: np.random.randn(*s).astype(np.float32) * 0.05)(128, 6 * 128) * 128 ** (-0.5))

    def _L1_attn_setup():
        import jax, jax.numpy as jnp
        import numpy as np
        import math
        D_MODEL, N_HEADS, D_K, D_C, D_HR = (128, 8, 128, 32, 32)
        B, S = (4, 256)
        key = jax.random.key(seed)
        ks = jax.random.split(key, 17)

        def lin(k, fan_in, fan_out):
            lim = 1.0 / math.sqrt(fan_in)
            kw, kb = jax.random.split(k)
            W = jax.random.uniform(kw, (fan_in, fan_out), jnp.float32, -lim, lim)
            b = jax.random.uniform(kb, (fan_out,), jnp.float32, -lim, lim)
            return (W, b)
        W_DQ, b_DQ = lin(ks[0], D_MODEL, D_C)
        W_UQ, b_UQ = lin(ks[1], D_C, N_HEADS * D_K)
        W_DKV, b_DKV = lin(ks[2], D_MODEL, D_C)
        W_UK, b_UK = lin(ks[3], D_C, N_HEADS * D_K)
        W_UV, b_UV = lin(ks[4], D_C, N_HEADS * D_K)
        W_QR, b_QR = lin(ks[5], D_C, N_HEADS * D_HR)
        W_KR, b_KR = lin(ks[6], D_MODEL, D_HR)
        W_O, b_O = lin(ks[7], N_HEADS * D_K, D_MODEL)
        h_t = jax.random.normal(ks[8], (B, S, D_MODEL), jnp.float32)
        return {'h_t': h_t, 'W_DQ': W_DQ, 'b_DQ': b_DQ, 'W_UQ': W_UQ, 'b_UQ': b_UQ, 'W_DKV': W_DKV, 'b_DKV': b_DKV, 'W_UK': W_UK, 'b_UK': b_UK, 'W_UV': W_UV, 'b_UV': b_UV, 'W_QR': W_QR, 'b_QR': b_QR, 'W_KR': W_KR, 'b_KR': b_KR, 'W_O': W_O, 'b_O': b_O}
    _L1_attn_in = _L1_attn_setup()

    def _L1_ffn_setup():
        import jax, jax.numpy as jnp
        import numpy as np

        def _binarize(w):
            alpha = jax.lax.stop_gradient(jnp.mean(jnp.abs(w), axis=1, keepdims=True))
            bw = alpha * jnp.sign(w)
            return w + jax.lax.stop_gradient(bw - w)
        key = jax.random.key(seed)
        k1, k2, k3, k4, k5 = jax.random.split(key, 5)
        D, H = (128, 512)
        x = jax.random.normal(k1, (64, 196, D), dtype=jnp.float32)
        w1 = jax.random.normal(k2, (H, D), dtype=jnp.float32) * 0.02
        b1 = jax.random.normal(k3, (H,), dtype=jnp.float32) * 0.02
        w2 = jax.random.normal(k4, (D, H), dtype=jnp.float32) * 0.02
        b2 = jax.random.normal(k5, (D,), dtype=jnp.float32) * 0.02
        return {'x': x, 'w1': w1, 'b1': b1, 'w2': w2, 'b2': b2}
    _L1_ffn_in = _L1_ffn_setup()
    _L1_c = _w((lambda *s: np.random.randn(*s).astype(np.float32) * 0.05)(8, 128))
    _L1_wmod = _w((lambda *s: np.random.randn(*s).astype(np.float32) * 0.05)(128, 6 * 128) * 128 ** (-0.5))
    _d = {'L0_attn_x': _L0_attn_in['x'], 'L0_attn_Wq': _L0_attn_in['Wq'], 'L0_attn_Wk': _L0_attn_in['Wk'], 'L0_attn_Wv': _L0_attn_in['Wv'], 'L0_attn_Wo': _L0_attn_in['Wo'], 'L0_attn_Wg1': _L0_attn_in['Wg1'], 'L0_attn_Wg2': _L0_attn_in['Wg2'], 'L0_attn_ln_w': _L0_attn_in['ln_w'], 'L0_attn_ln_b': _L0_attn_in['ln_b'], 'L0_ffn_gate_w': _L0_ffn_in['gate_w'], 'L0_ffn_dyn_gate_w': _L0_ffn_in['dyn_gate_w'], 'L0_ffn_dyn_up_w': _L0_ffn_in['dyn_up_w'], 'L0_ffn_dyn_down_w': _L0_ffn_in['dyn_down_w'], 'L0_ffn_sh_gate_w': _L0_ffn_in['sh_gate_w'], 'L0_ffn_sh_up_w': _L0_ffn_in['sh_up_w'], 'L0_ffn_sh_down_w': _L0_ffn_in['sh_down_w'], 'L0_c': _L0_c, 'L0_wmod': _L0_wmod, 'L1_attn_W_DQ': _L1_attn_in['W_DQ'], 'L1_attn_b_DQ': _L1_attn_in['b_DQ'], 'L1_attn_W_UQ': _L1_attn_in['W_UQ'], 'L1_attn_b_UQ': _L1_attn_in['b_UQ'], 'L1_attn_W_DKV': _L1_attn_in['W_DKV'], 'L1_attn_b_DKV': _L1_attn_in['b_DKV'], 'L1_attn_W_UK': _L1_attn_in['W_UK'], 'L1_attn_b_UK': _L1_attn_in['b_UK'], 'L1_attn_W_UV': _L1_attn_in['W_UV'], 'L1_attn_b_UV': _L1_attn_in['b_UV'], 'L1_attn_W_QR': _L1_attn_in['W_QR'], 'L1_attn_b_QR': _L1_attn_in['b_QR'], 'L1_attn_W_KR': _L1_attn_in['W_KR'], 'L1_attn_b_KR': _L1_attn_in['b_KR'], 'L1_attn_W_O': _L1_attn_in['W_O'], 'L1_attn_b_O': _L1_attn_in['b_O'], 'L1_ffn_w1': _L1_ffn_in['w1'], 'L1_ffn_b1': _L1_ffn_in['b1'], 'L1_ffn_w2': _L1_ffn_in['w2'], 'L1_ffn_b2': _L1_ffn_in['b2'], 'L1_c': _L1_c, 'L1_wmod': _L1_wmod}
    _x0 = _d['L0_attn_x']
    _d['L0_attn_x'] = jax.random.normal(jax.random.fold_in(jax.random.key(seed), 1), (8, 512, 128), dtype=_x0.dtype)
    del _x0
    return _d

def reference(L0_attn_x, L0_attn_Wq, L0_attn_Wk, L0_attn_Wv, L0_attn_Wo, L0_attn_Wg1, L0_attn_Wg2, L0_attn_ln_w, L0_attn_ln_b, L0_ffn_gate_w, L0_ffn_dyn_gate_w, L0_ffn_dyn_up_w, L0_ffn_dyn_down_w, L0_ffn_sh_gate_w, L0_ffn_sh_up_w, L0_ffn_sh_down_w, L0_c, L0_wmod, L1_attn_W_DQ, L1_attn_b_DQ, L1_attn_W_UQ, L1_attn_b_UQ, L1_attn_W_DKV, L1_attn_b_DKV, L1_attn_W_UK, L1_attn_b_UK, L1_attn_W_UV, L1_attn_b_UV, L1_attn_W_QR, L1_attn_b_QR, L1_attn_W_KR, L1_attn_b_KR, L1_attn_W_O, L1_attn_b_O, L1_ffn_w1, L1_ffn_b1, L1_ffn_w2, L1_ffn_b2, L1_c, L1_wmod):

    def _L0_attn_ref(x, Wq, Wk, Wv, Wo, Wg1, Wg2, ln_w, ln_b):
        import jax, jax.numpy as jnp
        import numpy as np
        B, N, EMBED, HEADS = (1, 256, 128, 16)
        HD = EMBED // HEADS
        BASE = 10000.0
        EPS = 1e-05

        def _rope(t):
            d = t.shape[-1]
            n = t.shape[-2]
            inv_freq = 1.0 / BASE ** (jnp.arange(0, d, 2, dtype=jnp.float32) / d)
            pos = jnp.arange(n, dtype=jnp.float32)
            ang = pos[:, None] * inv_freq[None, :]
            cos = jnp.concatenate([jnp.cos(ang), jnp.cos(ang)], axis=-1)
            sin = jnp.concatenate([jnp.sin(ang), jnp.sin(ang)], axis=-1)
            t1, t2 = (t[..., :d // 2], t[..., d // 2:])
            rot = jnp.concatenate([-t2, t1], axis=-1)
            return t * cos + rot * sin
        b, n, _ = x.shape
        q = jax.nn.silu(x @ Wq)
        k = jax.nn.silu(x @ Wk)
        v = x @ Wv
        split = lambda t: t.reshape(b, n, HEADS, HD).transpose(0, 2, 1, 3)
        q, k, v = (split(q), split(k), split(v))
        q = _rope(q)
        k = _rope(k)
        energy = jnp.einsum('bhnd,bhmd->bhnm', q, k)
        mask = jnp.tril(jnp.ones((n, n), dtype=energy.dtype))
        energy = energy * mask
        out = jnp.einsum('bhnm,bhmd->bhnd', energy, v)
        out = out.transpose(0, 2, 1, 3).reshape(b, n, EMBED)
        gate = jax.nn.sigmoid(x @ Wg1 @ Wg2)
        out = out * gate
        mu = out.mean(axis=-1, keepdims=True)
        var = ((out - mu) ** 2).mean(axis=-1, keepdims=True)
        out = (out - mu) / jnp.sqrt(var + EPS) * ln_w + ln_b
        return out @ Wo

    def _L0_ffn_ref(hidden_states, gate_w, dyn_gate_w, dyn_up_w, dyn_down_w, sh_gate_w, sh_up_w, sh_down_w):
        import jax, jax.numpy as jnp
        import numpy as np
        B, S, H = (2, 256, 128)
        E_DYN, E_FIX = (8, 1)
        I_DYN, I_FIX = (64, 256)
        TOP_K = 4
        TOP_P = 0.75
        JITTER_EPS = 0.1
        CAPACITY_FACTOR = 1.25
        MIN_CAPACITY = 4

        def _sparse_mixer(scores):
            T = scores.shape[0]
            rows = jnp.arange(T)
            masked_scores = scores
            mults, sels = ([], [])
            for _ in range(TOP_K):
                thr = jnp.max(masked_scores, axis=-1, keepdims=True)
                sel = jnp.argmax(masked_scores, axis=-1)
                factor = jnp.maximum(jnp.abs(scores), jnp.abs(thr))
                jmask = (thr - scores) / factor > 2.0 * JITTER_EPS
                gates = jax.nn.softmax(jnp.where(jmask, -jnp.inf, masked_scores), axis=-1)
                mult = jnp.take_along_axis(gates, sel[:, None], axis=-1)[:, 0]
                masked_scores = masked_scores.at[rows, sel].set(-jnp.inf)
                mults.append(mult)
                sels.append(sel)
            return (jnp.stack(mults, axis=-1), jnp.stack(sels, axis=-1))
        Bv, Sv, Hv = hidden_states.shape
        T = Bv * Sv
        x = hidden_states.reshape(T, Hv)
        full_logits = x @ gate_w.T
        dyn_logits = full_logits[:, :E_DYN]
        probs = jax.nn.softmax(dyn_logits, axis=-1)
        sorted_p = jnp.sort(probs, axis=-1)[:, ::-1]
        csum = jnp.cumsum(sorted_p, axis=-1)
        dyn_k = jnp.minimum(jnp.sum(csum < TOP_P, axis=-1) + 1, TOP_K)
        mult, sel = _sparse_mixer(dyn_logits)
        slot_valid = jnp.arange(TOP_K)[None, :] < dyn_k[:, None]
        mult = jnp.where(slot_valid, mult, 0.0)
        rows = jnp.arange(T)
        rw = jnp.zeros((T, E_DYN), x.dtype).at[rows[:, None], sel].add(mult)
        rw = rw / jnp.sum(rw, axis=-1, keepdims=True)
        mask_dyn = (rw > 0).astype(jnp.int32)
        cap = max(int(np.ceil(T / E_DYN * CAPACITY_FACTOR)), MIN_CAPACITY)
        mask_dyn = mask_dyn * (jnp.cumsum(mask_dyn, axis=0) <= cap)
        expert_mask = jnp.concatenate([mask_dyn, jnp.ones((T, E_FIX), jnp.int32)], axis=-1)
        maskf = expert_mask.astype(x.dtype)
        gw = jax.nn.softmax(jnp.where(expert_mask == 0, -jnp.inf, full_logits), axis=-1)
        gd = rw * jnp.sum(gw[:, :E_DYN], axis=-1, keepdims=True)
        global_w = jnp.concatenate([gd, gw[:, E_DYN:]], axis=-1) * maskf
        g = jnp.einsum('th,eih->tei', x, dyn_gate_w)
        u = jnp.einsum('th,eih->tei', x, dyn_up_w)
        y_dyn = jnp.einsum('tei,ehi->teh', jax.nn.silu(g) * u, dyn_down_w)
        out = jnp.einsum('te,teh->th', global_w[:, :E_DYN], y_dyn)
        gs = jnp.einsum('th,fih->tfi', x, sh_gate_w)
        us = jnp.einsum('th,fih->tfi', x, sh_up_w)
        y_sh = jnp.einsum('tfi,fhi->tfh', jax.nn.silu(gs) * us, sh_down_w)
        out = out + jnp.einsum('tf,tfh->th', global_w[:, E_DYN:], y_sh)
        return out.reshape(Bv, Sv, Hv)

    def _L1_attn_ref(h_t, W_DQ, b_DQ, W_UQ, b_UQ, W_DKV, b_DKV, W_UK, b_UK, W_UV, b_UV, W_QR, b_QR, W_KR, b_KR, W_O, b_O):
        import jax, jax.numpy as jnp
        import numpy as np
        import math
        D_MODEL, N_HEADS, D_K, D_C, D_HR = (128, 8, 128, 32, 32)
        B, S = (4, 256)
        b, s, _ = h_t.shape
        c_q = h_t @ W_DQ + b_DQ
        c_kv = h_t @ W_DKV + b_DKV
        q_c = (c_q @ W_UQ + b_UQ).reshape(b, s, N_HEADS, D_K).transpose(0, 2, 1, 3)
        k_c = (c_kv @ W_UK + b_UK).reshape(b, s, N_HEADS, D_K).transpose(0, 2, 1, 3)
        v_c = (c_kv @ W_UV + b_UV).reshape(b, s, N_HEADS, D_K).transpose(0, 2, 1, 3)
        q_r = (c_q @ W_QR + b_QR).reshape(b, s, N_HEADS, D_HR).transpose(0, 2, 1, 3)
        k_r = (h_t @ W_KR + b_KR)[:, None, :, :]
        k_r = jnp.broadcast_to(k_r, (b, N_HEADS, s, D_HR))
        q = jnp.concatenate([q_c, q_r], axis=-1)
        k = jnp.concatenate([k_c, k_r], axis=-1)
        scale = 1.0 / math.sqrt(D_K + D_HR)
        scores = jnp.einsum('bhsd,bhtd->bhst', q, k) * scale
        attn = jax.nn.softmax(scores, axis=-1)
        o = jnp.einsum('bhst,bhtd->bhsd', attn, v_c)
        o = o.transpose(0, 2, 1, 3).reshape(b, s, N_HEADS * D_K)
        return o @ W_O + b_O

    def _L1_ffn_ref(x, w1, b1, w2, b2):
        import jax, jax.numpy as jnp
        import numpy as np

        def _binarize(w):
            alpha = jax.lax.stop_gradient(jnp.mean(jnp.abs(w), axis=1, keepdims=True))
            bw = alpha * jnp.sign(w)
            return w + jax.lax.stop_gradient(bw - w)
        bw1 = _binarize(w1)
        h = jnp.einsum('bsd,hd->bsh', x, bw1) + b1
        h = jax.nn.gelu(h, approximate=False)
        bw2 = _binarize(w2)
        out = jnp.einsum('bsh,dh->bsd', h, bw2) + b2
        return out
    x = L0_attn_x
    mod = (_silu(L0_c) @ L0_wmod).reshape(L0_c.shape[0], 6, 1, -1)
    sa, ca, ga, sb, cb, gb = (mod[:, 0], mod[:, 1], mod[:, 2], mod[:, 3], mod[:, 4], mod[:, 5])
    ga = (2 * (ga >= 0) - 1) * jnp.maximum(jnp.abs(ga), 0.25)
    gb = (2 * (gb >= 0) - 1) * jnp.maximum(jnp.abs(gb), 0.25)
    h = _layernorm(x, axis=-1) * (1 + ca) + sa
    x = x + ga * _L0_attn_ref(h, L0_attn_Wq, L0_attn_Wk, L0_attn_Wv, L0_attn_Wo, L0_attn_Wg1, L0_attn_Wg2, L0_attn_ln_w, L0_attn_ln_b)
    h = _layernorm(x, axis=-1) * (1 + cb) + sb
    x = x + gb * _L0_ffn_ref(h, L0_ffn_gate_w, L0_ffn_dyn_gate_w, L0_ffn_dyn_up_w, L0_ffn_dyn_down_w, L0_ffn_sh_gate_w, L0_ffn_sh_up_w, L0_ffn_sh_down_w)
    mod = (_silu(L1_c) @ L1_wmod).reshape(L1_c.shape[0], 6, 1, -1)
    sa, ca, ga, sb, cb, gb = (mod[:, 0], mod[:, 1], mod[:, 2], mod[:, 3], mod[:, 4], mod[:, 5])
    ga = (2 * (ga >= 0) - 1) * jnp.maximum(jnp.abs(ga), 0.25)
    gb = (2 * (gb >= 0) - 1) * jnp.maximum(jnp.abs(gb), 0.25)
    h = _layernorm(x, axis=-1) * (1 + ca) + sa
    x = x + ga * _L1_attn_ref(h, L1_attn_W_DQ, L1_attn_b_DQ, L1_attn_W_UQ, L1_attn_b_UQ, L1_attn_W_DKV, L1_attn_b_DKV, L1_attn_W_UK, L1_attn_b_UK, L1_attn_W_UV, L1_attn_b_UV, L1_attn_W_QR, L1_attn_b_QR, L1_attn_W_KR, L1_attn_b_KR, L1_attn_W_O, L1_attn_b_O)
    h = _layernorm(x, axis=-1) * (1 + cb) + sb
    x = x + gb * _L1_ffn_ref(h, L1_ffn_w1, L1_ffn_b1, L1_ffn_w2, L1_ffn_b2)
    return x

_drawn_inputs = setup_inputs


def setup_inputs(seed=0):
    import zlib

    import numpy as np

    out = dict(_drawn_inputs(seed))
    spreads = {'L0_attn_ln_w': (1.0, 0.2), 'L0_attn_ln_b': (0.0, 0.335)}
    factors = {'L0_ffn_gate_w': 8.0,
     'L0_ffn_dyn_gate_w': 8.0,
     'L0_ffn_dyn_up_w': 8.0,
     'L0_ffn_dyn_down_w': 8.0,
     'L0_ffn_sh_gate_w': 8.0,
     'L0_ffn_sh_up_w': 8.0,
     'L0_ffn_sh_down_w': 8.0,
     'L1_attn_W_DQ': 8.0,
     'L1_attn_b_DQ': 8.0,
     'L1_attn_W_UQ': 8.0,
     'L1_attn_b_UQ': 8.0,
     'L1_attn_W_DKV': 8.0,
     'L1_attn_b_DKV': 8.0,
     'L1_attn_W_UK': 8.0,
     'L1_attn_b_UK': 64.0,
     'L1_attn_W_UV': 8.0,
     'L1_attn_b_UV': 12.939,
     'L1_attn_W_QR': 8.0,
     'L1_attn_b_QR': 8.0,
     'L1_attn_W_KR': 8.0,
     'L1_attn_b_KR': 64.0,
     'L1_attn_W_O': 3.6,
     'L1_attn_b_O': 64.0,
     'L1_ffn_w1': 6.936,
     'L1_ffn_b1': 64.0,
     'L1_ffn_w2': 6.728,
     'L1_ffn_b2': 64.0,
     'L1_c': 2.916,
     'L1_wmod': 2.885}
    for name, (base, spread) in spreads.items():
        noise = np.random.default_rng([zlib.crc32(name.encode()), seed]).standard_normal(out[name].shape)
        drawn = base * np.exp(spread * noise) if base else spread * noise
        out[name] = jnp.asarray(drawn.astype(out[name].dtype))
    for name, factor in factors.items():
        out[name] = (out[name] * factor).astype(out[name].dtype)
    return out
```

```python
from contextlib import ExitStack

import numpy as np

import concourse.bass as bass
from concourse import mybir

F32 = mybir.dt.float32
F32R = mybir.dt.float32r
ALU = mybir.AluOpType
ACT = mybir.ActivationFunctionType
AX = mybir.AxisListType

P = 128
B, N, D = 8, 512, 128
T = N // P
HEADS0, HD0 = 16, 8
G0, J0 = 4, 4
EPS = 1e-5
SA, CA, SB, CB = range(4)


def steps(eng, step, late):
    step(0, 1, None, 0)
    with eng.Fori(0, (B - 2) // 2) as i:
        step(2 * i + 1, 2 * i + 2, 2 * i, 1)
        step(2 * i + 2, 2 * i + 3, 2 * i + 1, 0)
    step(B - 1, None, B - 2, 1)
    late(B - 1)


def apart(eng, passed):
    eng.sem_inc(passed, 1)


class Memory:

    def __init__(self, nc, stack):
        self.nc, self.stack = nc, stack

    def sb(self, name, shape, dt=F32):
        return self.stack.enter_context(self.nc.sbuf_tensor(name, shape, dt))

    def ps(self, name):
        return self.stack.enter_context(self.nc.psum_tensor(name, [P, 512], F32))

    def sem(self, name):
        handle = self.nc.alloc_semaphore(name=name)

        def give_back():
            self.nc.gpsimd.sem_clear(handle)
            self.nc.release_semaphore(handle)

        self.stack.callback(give_back)
        return handle


def prepare(nc, a, k):
    with ExitStack() as stack:
        m = Memory(nc, stack)
        c_rows = m.sb("c_rows", [B, 2, D])
        cT = m.sb("cT", [P, 2, B])
        silu_cT = m.sb("silu_cT", [P, 2, B])
        wmod = m.sb("wmod", [P, 2, 6 * D])
        gate_raw = m.sb("gate_raw", [B, 4, D])
        gate_sign = m.sb("gate_sign", [B, 4, D])
        gate_neg = m.sb("gate_neg", [B, 4, D])
        gate_abs = m.sb("gate_abs", [B, 4, D])
        gate_rows = m.sb("gate_rows", [B, 4, D])
        spread_raw = m.sb("spread_raw", [P, 4, G0, P])
        spread_in = m.sem("spread_in")
        ps_c, ps_col, ps_row = m.ps("ps_c"), m.ps("ps_col"), m.ps("ps_row")
        ident_in, c_in, wmod_in = m.sem("ident_in"), m.sem("c_in"), m.sem("wmod_in")
        c_turned, c_copied, silu_done = m.sem("c_turned"), m.sem("c_copied"), m.sem("silu_done")
        cols_done, rows_done = m.sem("cols_done"), m.sem("rows_done")
        step, rows_ready = m.sem("gate_step"), m.sem("rows_ready")
        rows_stored, rows_spread = m.sem("rows_stored"), m.sem("rows_spread")
        with nc.Block() as block:

            @block.sync
            def _(eng):
                eng.dma_start(k.ident[:, :], a["ident"]).then_inc(ident_in, 16)
                for l in range(2):
                    eng.dma_start(c_rows[:, l, :], a[f"L{l}_c"]).then_inc(c_in, 16)
                for l in range(2):
                    eng.dma_start(wmod[:, l, :], a[f"L{l}_wmod"]).then_inc(wmod_in, 16)
                eng.dma_start(spread_raw[:, :, :, :].rearrange("p a g n -> p (a g n)"), a["spread"]).then_inc(spread_in, 16)
                eng.wait_ge(rows_ready, 1)
                eng.dma_start(k.scratch, gate_rows[:, :, :].rearrange("b k d -> b (k d)")).then_inc(rows_stored, 16)
                eng.wait_ge(rows_stored, 16)
                eng.dma_start(k.gates[:, :, :, :].rearrange("p b k d -> p (b k d)"),
                              k.scratch.rearrange("b n -> (b n)").partition_broadcast(P)).then_inc(rows_spread, 16)
                eng.wait_ge(rows_spread, 16)

            @block.tensor
            def _(eng):
                eng.wait_ge(ident_in, 16)
                eng.wait_ge(c_in, 32)
                for l in range(2):
                    last = eng.transpose(ps_c[:, B * l:B * l + B], c_rows[:, l, :], k.ident[0:B, 0:B])
                last.then_inc(c_turned, 1)
                eng.wait_ge(silu_done, 1)
                eng.wait_ge(wmod_in, 32)
                for l in range(2):
                    for n, chunk in enumerate((0, 1, 3, 4)):
                        at = (4 * l + n) * B
                        last = eng.matmul(ps_col[:, at:at + B], wmod[:, l, chunk * D:(chunk + 1) * D],
                                          silu_cT[:, l, :], start=True, stop=True)
                last.then_inc(cols_done, 1)
                for l in range(2):
                    for n, chunk in enumerate((2, 5)):
                        at = (2 * l + n) * D
                        last = eng.matmul(ps_row[0:B, at:at + D], silu_cT[:, l, :],
                                          wmod[:, l, chunk * D:(chunk + 1) * D], start=True, stop=True)
                last.then_inc(rows_done, 1)

            @block.scalar
            def _(eng):
                eng.wait_ge(c_turned, 1)
                eng.activation(silu_cT[:, :, :].rearrange("p l b -> p (l b)"), ps_c[:, 0:2 * B], ACT.Silu).then_inc(silu_done, 1)

            @block.vector
            def _(eng):
                cols = ps_col[:, 0:8 * B].rearrange("p (l c b) -> p l c b", l=2, c=4)
                eng.wait_ge(cols_done, 1)
                for n, plus in ((SA, 0.0), (CA, 1.0), (SB, 0.0), (CB, 1.0)):
                    eng.tensor_scalar(k.mods[:, :, n, :], cols[:, :, n, :], plus, None, ALU.add)
                eng.wait_ge(rows_done, 1)
                rows = ps_row[0:B, :].rearrange("b (k d) -> b k d", k=4)
                eng.tensor_scalar(gate_sign[:, :, :], rows, 0.0, 2.0, ALU.is_ge, ALU.mult)
                eng.tensor_scalar(gate_neg[:, :, :], rows, -1.0, None, ALU.mult).then_inc(step, 1)
                eng.wait_ge(step, 1)
                eng.scalar_tensor_tensor(gate_abs[:, :, :], rows, 0.25, gate_neg[:, :, :], ALU.max, ALU.max).then_inc(step, 1)
                eng.wait_ge(step, 2)
                eng.scalar_tensor_tensor(gate_rows[:, :, :], gate_sign[:, :, :], -1.0, gate_abs[:, :, :],
                                         ALU.add, ALU.mult).then_inc(rows_ready, 1)
                eng.wait_ge(spread_in, 16)
                eng.tensor_copy(k.spread[:, :, :, :], spread_raw[:, :, :, :])


def layer_norm_stats(eng, rows, stats, moments, stats_done, moments_done, passed, s):
    for t in range(T):
        last = eng.bn_stats(stats[:, t, :], rows(t))
    last.then_inc(stats_done, 1)
    eng.wait_ge(stats_done, s + 1)
    apart(eng, passed)
    for t in range(T):
        last = eng.bn_aggr(moments[:, t, :], stats[:, t, :])
    last.then_inc(moments_done, 1)


def linear_attention(nc, a, k):
    with ExitStack() as stack:
        m = Memory(nc, stack)
        wq, wk, wv, wo = (m.sb(n, [P, D]) for n in ("wq", "wk", "wv", "wo"))
        wq_rot, wk_rot = m.sb("wq_rot", [P, D]), m.sb("wk_rot", [P, D])
        wg1, wg1T, wg2, wg = m.sb("wg1", [P, 8]), m.sb("wg1T", [8, P]), m.sb("wg2", [8, D]), m.sb("wg", [P, D])
        lnw, lnb = m.sb("lnw", [P, 1]), m.sb("lnb", [P, 1])
        cos, sin = m.sb("cos", [P, N]), m.sb("sin", [P, N])
        causal, own_head = m.sb("causal", [P, P]), m.sb("own_head", [P, P])
        head_rows = m.sb("head_rows", [P, J0])
        spread = k.spread
        minus_half = m.sb("minus_half", [P, T])
        stats, moments = m.sb("stats", [P, T, 6]), m.sb("moments", [P, T, 2])
        var_eps, rstd = m.sb("var_eps", [P, T]), m.sb("rstd", [P, T])
        xn, hT = m.sb("xn", [P, T, D]), m.sb("hT", [P, N])
        act = {n: m.sb("act_" + n, [P, N]) for n in ("q", "q_rot", "k", "k_rot")}
        qr = [m.sb(f"qr{p}", [P, N]) for p in (0, 1)]
        kr = m.sb("kr", [P, N])
        hi = {n: m.sb("hi_" + n, [P, N], F32R) for n in "qk"}
        lo = {n: m.sb("lo_" + n, [P, N], F32R) for n in "qk"}
        q_stack = m.sb("q_stack", [P, G0, N])
        q_heads = m.sb("q_heads", [P, 2, G0, J0, N // 1], F32R)
        k_stack = m.sb("k_stack", [P, 2, G0, N], F32R)
        k_tok, v_tok = m.sb("k_tok", [P, 2, T, D]), m.sb("v_tok", [P, 2, T, D])
        v_heads = m.sb("v_heads", [P, 2, T, J0, D])
        gate = m.sb("gate", [P, 2, N])
        masked = m.sb("masked", [P, 4, 4 * P])
        state = m.sb("state", [P, D])
        gated = m.sb("gated", [P, N])
        stats2, moments2 = m.sb("stats2", [P, T, 6]), m.sb("moments2", [P, T, 2])
        var_eps2, rstd2, shift2 = m.sb("var_eps2", [P, T]), m.sb("rstd2", [P, T]), m.sb("shift2", [P, T])
        on, oT, wo_g = m.sb("on", [P, T, D]), m.sb("oT", [P, N]), m.sb("wo_g", [P, D])
        ps_t, ps_e, ps_o, ps_s, ps_y = m.ps("ps_t"), [m.ps("ps_e0"), m.ps("ps_e1")], m.ps("ps_o"), m.ps("ps_s"), m.ps("ps_y")
        ps_p = [m.ps("ps_p0"), m.ps("ps_p1")]
        S = m.sem
        w_in, x_in, x_in2 = S("w_in"), S("x_in"), S("x_in2")
        consts, wrot, wg_t, wg_c, wg_m, w_ready, w_pool = (S("consts"), S("wrot"), S("wg_t"), S("wg_c"), S("wg_m"),
                                                       S("w_ready"), S("w_pool"))
        stats_done, moments_done, ve_done, rstd_done = S("stats_done"), S("moments_done"), S("ve_done"), S("rstd_done")
        xn_done, turned, hT_done, kT_turned, k_tok_done = S("xn_done"), S("turned"), S("hT_done"), S("kT_turned"), S("k_tok_done")
        filled, emptied = [S("filled0"), S("filled1")], [S("emptied0"), S("emptied1")]
        cos_done, sin_done, rot_done, hi_done, lo_done = S("cos_done"), S("sin_done"), S("rot_done"), S("hi_done"), S("lo_done")
        q_heads_v, q_heads_a, v_heads_done = S("q_heads_v"), S("q_heads_a"), S("v_heads_done")
        energy_done, masked_done, av_done = S("energy_done"), S("masked_done"), S("av_done")
        state_sum, state_done, o_done, gated_done = S("state_sum"), S("state_done"), S("o_done"), S("gated_done")
        o_turned, stats2_done, moments2_done, ve2_done, rstd2_done, shift2_done = (
            S("o_turned"), S("stats2_done"), S("moments2_done"), S("ve2_done"), S("rstd2_done"), S("shift2_done"))
        on_done, on_turned, oT_done, wo_g_done, y_done, x_done = (
            S("on_done"), S("on_turned"), S("oT_done"), S("wo_g_done"), S("y_done"), S("x_done"))
        USES = (6 + 2 * G0) // 2
        Q, Q_ROT, K, K_ROT, V, GATE, QS, KS = 0, 1, 2, 3, 4, 5, 6, 6 + G0

        def nth(n, s):
            return s * USES + n // 2 + 1

        with nc.Block() as block:

            @block.sync
            def _(eng):
                for dst, name in ((wq, "L0_attn_Wq"), (wk, "L0_attn_Wk"), (wv, "L0_attn_Wv"), (wo, "L0_attn_Wo"),
                                  (wg1, "L0_attn_Wg1"), (wg2, "L0_attn_Wg2"), (cos, "cos"), (sin, "sin"),
                                  (causal, "causal"), (own_head, "own_head"), (head_rows, "head_rows")):
                    eng.dma_start(dst[:, :], a[name]).then_inc(w_in, 16)
                for dst, name in ((lnw, "L0_attn_ln_w"), (lnb, "L0_attn_ln_b")):
                    eng.dma_start(dst[:, :], a[name].rearrange("(d o) -> d o", o=1)).then_inc(w_in, 16)

                def load(s):
                    eng.dma_start(k.x[:, s, :, :], a["L0_attn_x"][s, :, :].rearrange("(t p) d -> p t d", p=P)).then_inc(x_in, 16)

                load(0)
                with eng.Fori(1, B) as s:
                    eng.wait_ge(x_in, s * 16)
                    load(s)
            W_IN = 13 * 16

            @block.gpsimd
            def _(eng):
                eng.memset(minus_half[:, :], -0.5)
                eng.memset(v_heads[:, :, :, :, :].rearrange("p a t j d -> p (a t j d)"), 0.0).then_inc(w_pool, 1)
                eng.wait_ge(w_pool, 1)
                eng.wait_ge(w_in, W_IN)

                def norm_rstd(s):
                    eng.wait_ge(moments_done, s + 1)
                    apart(eng, k.passed)
                    eng.tensor_scalar(var_eps[:, :], moments[:, :, 1], EPS, None, ALU.add).then_inc(ve_done, 1)
                    eng.wait_ge(ve_done, s + 1)
                    eng.tensor_tensor(rstd[:, :], var_eps[:, :], minus_half[:, :], ALU.pow).then_inc(rstd_done, 1)

                def front(s, p):
                    norm_rstd(s)
                    for i, n in enumerate("qk"):
                        bank = 2 * i
                        eng.wait_ge(emptied[0], nth(bank, s))
                        eng.tensor_tensor(act[n][:, :], act[n][:, :], cos[:, :], ALU.mult).then_inc(cos_done, 1)
                    for i, n in enumerate("qk"):
                        eng.wait_ge(hi_done, 2 * s + i + 1)
                        rot = qr[p] if n == "q" else kr
                        eng.tensor_tensor(lo[n][:, :], rot[:, :], hi[n][:, :].bitcast(F32), ALU.subtract).then_inc(lo_done, 1)
                    eng.wait_ge(emptied[0], nth(V, s))
                    apart(eng, k.passed)
                    for j in range(J0):
                        cols = lambda t: t.rearrange("p t (g j c) -> p t g j c", g=G0, j=J0)[:, :, :, j, :]
                        last = eng.tensor_copy(cols(v_heads[:, p, :, j, :]), cols(v_tok[:, p, :, :]))
                    last.then_inc(v_heads_done, 1)

                def step(s, front_of, late_of, p):
                    if front_of is not None:
                        front(front_of, 1 - p)
                    eng.wait_ge(y_done, s)
                    eng.tensor_tensor(wo_g[:, :], wo[:, :], k.gates[:, s, 0, :], ALU.mult).then_inc(wo_g_done, 1)
                    eng.wait_ge(moments2_done, s + 1)
                    apart(eng, k.passed)
                    eng.tensor_scalar(var_eps2[:, :], moments2[:, :, 1], 4 * EPS, None, ALU.add).then_inc(ve2_done, 1)
                    eng.wait_ge(ve2_done, s + 1)
                    eng.tensor_tensor(rstd2[:, :], var_eps2[:, :], minus_half[:, :], ALU.pow).then_inc(rstd2_done, 1)

                front(0, 0)
                steps(eng, step, lambda s: None)

            @block.tensor
            def _(eng):
                eng.wait_ge(w_in, W_IN)
                eng.transpose(ps_t[0:8, 0:P], wg1[:, :], k.ident[:, :]).then_inc(wg_t, 1)
                eng.wait_ge(wg_c, 1)
                eng.matmul(ps_t[:, 0:D], wg1T[:, :], wg2[:, :], start=True, stop=True).then_inc(wg_m, 1)
                eng.wait_ge(w_ready, 2)

                def turn(s):
                    eng.wait_ge(xn_done, s + 1)
                    eng.wait_ge(k_tok_done, s)
                    for t in range(T):
                        last = eng.transpose(ps_t[:, t * P:(t + 1) * P], xn[:, t, :], k.ident[:, :])
                    last.then_inc(turned, 1)

                def project(s, n):
                    eng.wait_ge(hT_done, s + 1)
                    eng.wait_ge(emptied[n % 2], s * USES + n // 2)
                    if n == V:
                        for t in range(T):
                            last = eng.matmul(ps_p[0][:, t * P:(t + 1) * P], hT[:, t * P:(t + 1) * P], wv[:, :], start=True, stop=True)
                    else:
                        last = eng.matmul(ps_p[n % 2][:, :], {Q: wq, Q_ROT: wq_rot, K: wk, K_ROT: wk_rot, GATE: wg}[n][:, :], hT[:, :],
                                          start=True, stop=True)
                    last.then_inc(filled[n % 2], 1)

                def spread_parts(s, i):
                    name, first = (("q", QS), ("k", KS))[i]
                    eng.wait_ge(lo_done, 2 * s + i + 1)
                    for g in range(G0):
                        n = first + g
                        eng.wait_ge(emptied[n % 2], s * USES + n // 2)
                        eng.matmul(ps_p[n % 2][:, :], spread[:, 2 * i, g, :], hi[name][:, :], start=True, stop=False)
                        eng.matmul(ps_p[n % 2][:, :], spread[:, 2 * i + 1, g, :], lo[name][:, :],
                                   start=False, stop=True).then_inc(filled[n % 2], 1)

                def turn_k(s):
                    for t in range(T):
                        last = eng.transpose(ps_t[:, t * P:(t + 1) * P], kr[:, t * P:(t + 1) * P], k.ident[:, :])
                    last.then_inc(kT_turned, 1)

                def energy(s, p, n):
                    c, g = divmod(n, G0)
                    if c == 0:
                        eng.wait_ge((q_heads_v, q_heads_a)[g // 2], 2 * s + g % 2 + 1)
                        eng.wait_ge(emptied[(KS + g) % 2], nth(KS + g, s))
                    eng.wait_ge(masked_done, s * 16 + max(n - 1, 0))
                    eng.matmul(ps_e[n % 2][:, :], k_stack[:, p, g, c * P:(c + 1) * P],
                               q_heads[:, p, g, :, c * P:(c + 1) * P],
                               start=True, stop=True).then_inc(energy_done, 1)

                def values(s, p, n):
                    c, g = divmod(n, G0)
                    out = slice(c * P, (c + 1) * P)
                    if n == 0:
                        eng.wait_ge(gated_done, s)
                        eng.wait_ge(v_heads_done, s + 1)
                        eng.wait_ge(k_tok_done, s + 1)
                    if g == 0 and c > 0:
                        eng.wait_ge(state_done, s * 3 + c)
                        eng.matmul(ps_o[:, out], state[:, :], qr[p][:, out], start=True, stop=False,
                                   skip_group_check=True)
                    if g == 0 and c < T - 1:
                        eng.wait_ge(state_done, s * 3 + c)
                        eng.matmul(ps_s[:, 0:D], k_tok[:, p, c, :], v_tok[:, p, c, :], start=(c == 0),
                                   stop=(c == T - 2), skip_group_check=True).then_inc(state_sum, 1)
                    eng.wait_ge(masked_done, s * 16 + n + 1)
                    for j in range(J0):
                        last = eng.matmul(ps_o[32 * g:32 * g + 32, out], v_heads[:, p, c, j, 32 * g:32 * g + 32],
                                          masked[:, n % 4, j * P:(j + 1) * P], start=(c == 0 and j == 0),
                                          stop=(j == J0 - 1), skip_group_check=True)
                    last.then_inc(av_done, 1)

                def turn_gated(s):
                    eng.wait_ge(gated_done, s + 1)
                    eng.wait_ge(x_done, s)
                    for t in range(T):
                        last = eng.transpose(ps_y[:, t * P:(t + 1) * P], gated[:, t * P:(t + 1) * P], k.ident[:, :])
                    last.then_inc(o_turned, 1)

                def turn_normed(s):
                    eng.wait_ge(on_done, s + 1)
                    for t in range(T):
                        last = eng.transpose(ps_y[:, t * P:(t + 1) * P], on[:, t, :], k.ident[:, :])
                    last.then_inc(on_turned, 1)

                def product_out(s):
                    eng.wait_ge(oT_done, s + 1)
                    eng.wait_ge(wo_g_done, s + 1)
                    for t in range(T):
                        last = eng.matmul(ps_y[:, t * P:(t + 1) * P], oT[:, t * P:(t + 1) * P], wo_g[:, :],
                                          start=True, stop=True)
                    last.then_inc(y_done, 1)

                def step(s, front, late, p):
                    energy(s, p, 0)
                    energy(s, p, 1)
                    for n in range(16):
                        if n + 2 < 16:
                            energy(s, p, n + 2)
                        values(s, p, n)
                        if late is not None and n == 4:
                            turn_normed(late)
                        if late is not None and n == 6:
                            product_out(late)
                        if front is not None and n == 5:
                            turn(front)
                        if front is not None and 7 <= n < 13:
                            project(front, n - 7)
                    if front is not None:
                        spread_parts(front, 0)
                    turn_gated(s)
                    if front is not None:
                        spread_parts(front, 1)
                        turn_k(front)

                def late(s):
                    turn_normed(s)
                    product_out(s)

                turn(0)
                for n in range(6):
                    project(0, n)
                spread_parts(0, 0)
                spread_parts(0, 1)
                turn_k(0)
                steps(eng, step, late)

            @block.scalar
            def _(eng):
                eng.wait_ge(wg_t, 1)
                eng.activation(wg1T[:, :], ps_t[0:8, 0:P], ACT.Copy).then_inc(wg_c, 1)
                eng.wait_ge(wg_m, 1)
                eng.activation(wg[:, :], ps_t[:, 0:D], ACT.Copy).then_inc(w_ready, 1)

                def front(s, p):
                    eng.wait_ge(turned, s + 1)
                    eng.wait_ge(filled[1], s * USES)
                    eng.activation(hT[:, :], ps_t[:, :], ACT.Identity,
                                   scale=k.mods[:, 0, CA, bass.ds(s, 1)], bias=k.mods[:, 0, SA, bass.ds(s, 1)]).then_inc(hT_done, 1)

                    def split(i):
                        eng.wait_ge(rot_done, 2 * s + i + 1)
                        rot = (qr[p], kr)[i]
                        eng.activation(hi["qk"[i]][:, :], rot[:, :], ACT.Copy).then_inc(hi_done, 1)

                    for n, name in enumerate(("q", "q_rot", "k", "k_rot")):
                        eng.wait_ge(filled[n % 2], nth(n, s))
                        eng.wait_ge(rot_done, 2 * s)
                        eng.activation(act[name][:, :], ps_p[n % 2][:, :], ACT.Silu).then_inc(emptied[n % 2], 1)
                    eng.wait_ge(filled[0], nth(V, s))
                    eng.activation(v_tok[:, p, :, :].rearrange("p t d -> p (t d)"), ps_p[0][:, :], ACT.Copy).then_inc(emptied[0], 1)
                    split(0)
                    eng.wait_ge(filled[1], nth(GATE, s))
                    eng.activation(gate[:, p, :], ps_p[1][:, :], ACT.Tanh, scale=0.5).then_inc(emptied[1], 1)
                    split(1)
                    eng.wait_ge(q_heads_v, 2 * s)
                    for g in range(G0):
                        n = QS + g
                        eng.wait_ge(filled[n % 2], nth(n, s))
                        if g == 2:
                            eng.wait_ge(q_heads_a, 2 * s)
                        eng.activation(q_stack[:, g, :], ps_p[n % 2][:, :], ACT.Copy).then_inc(emptied[n % 2], 1)
                    for g in range(G0):
                        n = KS + g
                        eng.wait_ge(filled[n % 2], nth(n, s))
                        eng.activation(k_stack[:, p, g, :], ps_p[n % 2][:, :], ACT.Copy).then_inc(emptied[n % 2], 1)
                    eng.wait_ge(kT_turned, s + 1)
                    eng.activation(k_tok[:, p, :, :].rearrange("p t d -> p (t d)"), ps_t[:, :], ACT.Copy).then_inc(k_tok_done, 1)
                    eng.wait_ge(emptied[1], nth(QS + 3, s))
                    eng.wait_ge(emptied[0], nth(QS + 2, s))
                    for g in (2, 3):
                        for j in range(J0):
                            last = eng.activation(q_heads[:, p, g, j, :], q_stack[:, g, :], ACT.Copy, scale=head_rows[:, j:j + 1])
                        last.then_inc(q_heads_a, 1)

                def late(s):
                    eng.wait_ge(shift2_done, s + 1)
                    eng.wait_ge(rstd2_done, s + 1)
                    for t in range(T):
                        last = eng.activation(on[:, t, :], ps_y[:, t * P:(t + 1) * P], ACT.Identity,
                                              scale=rstd2[:, t:t + 1], bias=shift2[:, t:t + 1])
                    last.then_inc(on_done, 1)
                    eng.wait_ge(on_turned, s + 1)
                    eng.activation(oT[:, :], ps_y[:, :], ACT.Identity, scale=lnw[:, :], bias=lnb[:, :]).then_inc(oT_done, 1)

                def step(s, front_of, late_of, p):
                    if late_of is not None:
                        late(late_of)
                    if front_of is not None:
                        front(front_of, 1 - p)

                front(0, 0)
                steps(eng, step, late)

            @block.vector
            def _(eng):
                eng.wait_ge(w_in, W_IN)
                for w, rot in ((wq, wq_rot), (wk, wk_rot)):
                    for half in (0, 1):
                        of = lambda t, h: t[:, :].rearrange("p (n h r) -> p n h r", h=2, r=4)[:, :, h, :]
                        last = eng.tensor_copy(of(rot, half), of(w, 1 - half))
                last.then_inc(w_ready, 1)

                def norm_stats(s):
                    eng.wait_ge(x_in, s * 16 + 16)
                    layer_norm_stats(eng, lambda t: k.x[:, s, t, :], stats, moments, stats_done, moments_done, k.passed, s)

                def normalise(s):
                    eng.wait_ge(rstd_done, s + 1)
                    eng.wait_ge(turned, s)
                    for t in range(T):
                        last = eng.tensor_scalar(xn[:, t, :], k.x[:, s, t, :], moments[:, t, 0:1], rstd[:, t:t + 1],
                                                 ALU.subtract, ALU.mult)
                    last.then_inc(xn_done, 1)

                def times_sine(s, i):
                    name = "qk"[i]
                    eng.wait_ge(emptied[1], nth(2 * i + 1, s))
                    eng.tensor_tensor(act[name + "_rot"][:, :], act[name + "_rot"][:, :], sin[:, :], ALU.mult).then_inc(sin_done, 1)

                def rotate(s, p, i):
                    name = "qk"[i]
                    eng.wait_ge(sin_done, 2 * s + i + 1)
                    eng.wait_ge(cos_done, 2 * s + i + 1)
                    if name == "k":
                        eng.wait_ge(kT_turned, s)
                        eng.wait_ge(lo_done, 2 * s)
                    rot = qr[p] if name == "q" else kr
                    eng.tensor_tensor(rot[:, :], act[name][:, :], act[name + "_rot"][:, :], ALU.add).then_inc(rot_done, 1)

                def split_heads(s, p):
                    for g in range(2):
                        eng.wait_ge(emptied[g % 2], nth(QS + g, s))
                        for j in range(J0):
                            last = eng.tensor_scalar(q_heads[:, p, g, j, :], q_stack[:, g, :], head_rows[:, j:j + 1],
                                                     None, ALU.mult)
                        last.then_inc(q_heads_v, 1)

                def mask(s, n):
                    c, g = divmod(n, G0)
                    eng.wait_ge(energy_done, s * 16 + n + 1)
                    if n >= 4:
                        eng.wait_ge(av_done, s * 16 + n - 3)
                    eng.tensor_tensor(masked[:, n % 4, :].rearrange("p (j n) -> p j n", j=J0),
                                      ps_e[n % 2][:, :].rearrange("p (j n) -> p j n", j=J0),
                                      causal[:, :].unsqueeze(1).to_broadcast([P, J0, P]), ALU.mult).then_inc(masked_done, 1)
                    if g == 1 and c < T - 1:
                        eng.wait_ge(state_sum, s * 3 + c + 1)
                        eng.tensor_tensor(state[:, :], ps_s[:, 0:D], own_head[:, :], ALU.mult).then_inc(state_done, 1)

                def gate_out(s, p):
                    eng.wait_ge(av_done, s * 16 + 16)
                    eng.wait_ge(o_turned, s)
                    eng.scalar_tensor_tensor(gated[:, :], gate[:, p, :], 1.0, ps_o[:, :], ALU.add, ALU.mult).then_inc(gated_done, 1)

                def late_shift(s):
                    eng.wait_ge(rstd2_done, s + 1)
                    eng.scalar_tensor_tensor(shift2[:, :], moments2[:, :, 0], -1.0, rstd2[:, :], ALU.mult, ALU.mult).then_inc(shift2_done, 1)

                def add_out(s):
                    eng.wait_ge(y_done, s + 1)
                    xs = k.x[:, s, :, :].rearrange("p t d -> p (t d)")
                    eng.tensor_tensor(xs, ps_y[:, :], xs, ALU.add).then_inc(x_done, 1)

                def step(s, front, late, p):
                    for n in range(16):
                        mask(s, n)
                        if late is not None and n == 0:
                            late_shift(late)
                        if front is not None and n == 1:
                            norm_stats(front)
                        if front is not None and n == 4:
                            normalise(front)
                        if late is not None and n == 8:
                            add_out(late)
                        if front is not None and n in (10, 13):
                            times_sine(front, n // 13)
                        if front is not None and n in (12, 15):
                            rotate(front, 1 - p, n // 15)
                    gate_out(s, p)
                    if front is not None:
                        split_heads(front, 1 - p)
                    eng.wait_ge(o_turned, s + 1)
                    layer_norm_stats(eng, lambda t: ps_y[:, t * P:(t + 1) * P], stats2, moments2, stats2_done, moments2_done, k.passed, s)

                def late(s):
                    late_shift(s)
                    add_out(s)

                norm_stats(0)
                normalise(0)
                for i in range(2):
                    times_sine(0, i)
                    rotate(0, 0, i)
                split_heads(0, 0)
                steps(eng, step, late)


def pairs_of(eng, body):
    body(0, 0)
    with eng.Fori(0, (B - 2) // 2) as i:
        body(2 * i + 1, 1)
        body(2 * i + 2, 0)
    body(B - 1, 1)


class Norm:

    def __init__(self, m, k, layer, shift, scale):
        tag = f"n{layer}{shift}_"
        self.k, self.layer, self.shift, self.scale = k, layer, shift, scale
        self.stats, self.moments = m.sb(tag + "stats", [P, 2, T, 6]), m.sb(tag + "moments", [P, 2, T, 2])
        self.var_eps, self.rstd = m.sb(tag + "var_eps", [P, 2, T]), m.sb(tag + "rstd", [P, 2, T])
        self.minus_half = m.sb(tag + "minus_half", [P, T])
        self.xn = m.sb(tag + "xn", [P, 2, T, D])
        self.power_ready = m.sem(tag + "power_ready")
        self.stats_done, self.moments_done = m.sem(tag + "stats_done"), m.sem(tag + "moments_done")
        self.ve_done, self.rstd_done = m.sem(tag + "ve_done"), m.sem(tag + "rstd_done")
        self.xn_done, self.turned, self.h_done = m.sem(tag + "xn_done"), m.sem(tag + "turned"), m.sem(tag + "h_done")

    def pool_setup(self, eng):
        eng.memset(self.minus_half[:, :], -0.5).then_inc(self.power_ready, 1)
        eng.wait_ge(self.power_ready, 1)

    def pool_rstd(self, eng, s, p):
        eng.wait_ge(self.moments_done, s + 1)
        apart(eng, self.k.passed)
        eng.tensor_scalar(self.var_eps[:, p, :], self.moments[:, p, :, 1], EPS, None, ALU.add).then_inc(self.ve_done, 1)
        eng.wait_ge(self.ve_done, s + 1)
        eng.tensor_tensor(self.rstd[:, p, :], self.var_eps[:, p, :], self.minus_half[:, :], ALU.pow).then_inc(self.rstd_done, 1)

    def vector_stats(self, eng, s, p):
        for t in range(T):
            last = eng.bn_stats(self.stats[:, p, t, :], self.k.x[:, s, t, :])
        last.then_inc(self.stats_done, 1)
        eng.wait_ge(self.stats_done, s + 1)
        apart(eng, self.k.passed)
        for t in range(T):
            last = eng.bn_aggr(self.moments[:, p, t, :], self.stats[:, p, t, :])
        last.then_inc(self.moments_done, 1)

    def vector_normalise(self, eng, s, p):
        eng.wait_ge(self.rstd_done, s + 1)
        for t in range(T):
            last = eng.tensor_scalar(self.xn[:, p, t, :], self.k.x[:, s, t, :], self.moments[:, p, t, 0:1],
                                     self.rstd[:, p, t:t + 1], ALU.subtract, ALU.mult)
        last.then_inc(self.xn_done, 1)

    def tensor_turn(self, eng, bank, s, p):
        eng.wait_ge(self.xn_done, s + 1)
        for t in range(T):
            last = eng.transpose(bank[:, t * P:(t + 1) * P], self.xn[:, p, t, :], self.k.ident[:, :])
        last.then_inc(self.turned, 1)

    def scalar_modulate(self, eng, bank, out, s):
        eng.wait_ge(self.turned, s + 1)
        return eng.activation(out, bank[:, :], ACT.Identity,
                              scale=self.k.mods[:, self.layer, self.scale, bass.ds(s, 1)],
                              bias=self.k.mods[:, self.layer, self.shift, bass.ds(s, 1)])


E_DYN, I_DYN, I_FIX = 8, 64, 256
E_ALL = E_DYN + 1
TOP_K, TOP_P, JITTER = 4, 0.75, 0.1
TILES = B * T
CAPACITY = max(int(np.ceil(B * N / E_DYN * 1.25)), 4)
UNITS = (E_DYN * I_DYN + I_FIX) // P
DYN_UNITS = E_DYN * I_DYN // P


def routing(nc, a, k, r):
    with ExitStack() as stack:
        m = Memory(nc, stack)
        norm = Norm(m, k, 0, SB, CB)
        gate_rows, gateT = m.sb("r_gate_rows", [E_ALL, D]), m.sb("r_gateT", [P, E_ALL])
        hT = m.sb("r_hT", [P, 2, N])
        raw = {n: m.sb("r_raw_" + n, [P, UNITS, P]) for n in ("gate", "up", "down")}
        ps_t, ps_l, ps_w = [m.ps("r_ps_t0"), m.ps("r_ps_t1")], m.ps("r_ps_l"), [m.ps("r_ps_w0"), m.ps("r_ps_w1")]
        g_in, w_in, g_turned, g_done = m.sem("r_g_in"), m.sem("r_w_in"), m.sem("r_g_turned"), m.sem("r_g_done")
        w_turned, w_done = m.sem("r_w_turned"), m.sem("r_w_done")
        h_done, h_kept, logits_done = m.sem("r_h_done"), m.sem("r_h_kept"), m.sem("r_logits_done")
        logits = m.sb("r_logits", [P, TILES, E_ALL])
        batches = [(raw[n], dst, u, min(u + 4, UNITS)) for n, dst in (("gate", r.gate), ("up", r.up), ("down", r.down)) for u in (0, 4)]
        with nc.Block() as block:

            @block.sync
            def _(eng):
                eng.dma_start(gate_rows[:, :], a["L0_ffn_gate_w"]).then_inc(g_in, 16)
                for n in ("gate", "up"):
                    eng.dma_start(raw[n][:, 0:DYN_UNITS, :],
                                  a[f"L0_ffn_dyn_{n}_w"].rearrange("e i h -> (e i) h").rearrange("(u p) h -> p u h", p=P)).then_inc(w_in, 16)
                    eng.dma_start(raw[n][:, DYN_UNITS:UNITS, :],
                                  a[f"L0_ffn_sh_{n}_w"].rearrange("f i h -> (f i) h").rearrange("(u p) h -> p u h", p=P)).then_inc(w_in, 16)
                eng.dma_start(raw["down"][:, 0:DYN_UNITS, :].rearrange("p u i -> p (u i)").rearrange("p (e i) -> p e i", e=E_DYN),
                              a["L0_ffn_dyn_down_w"].rearrange("e h i -> h e i")).then_inc(w_in, 16)
                eng.dma_start(raw["down"][:, DYN_UNITS:UNITS, :].rearrange("p u i -> p (u i)"),
                              a["L0_ffn_sh_down_w"].rearrange("f h i -> (f h) i")).then_inc(w_in, 16)

            @block.gpsimd
            def _(eng):
                norm.pool_setup(eng)
                pairs_of(eng, lambda s, p: norm.pool_rstd(eng, s, p))

            @block.tensor
            def _(eng):
                eng.wait_ge(g_in, 16)
                eng.transpose(ps_l[:, 0:E_ALL], gate_rows[:, :], k.ident[0:E_ALL, 0:E_ALL]).then_inc(g_turned, 1)
                eng.wait_ge(g_done, 1)

                def body(s, p):
                    eng.wait_ge(h_kept, s)
                    norm.tensor_turn(eng, ps_t[p], s, p)
                    eng.wait_ge(h_done, s + 1)
                    for t in range(T):
                        last = eng.matmul(ps_l[:, bass.ds((s * T + t) * E_ALL, E_ALL)], hT[:, p, t * P:(t + 1) * P], gateT[:, :],
                                          start=True, stop=True)
                    last.then_inc(logits_done, 1)

                pairs_of(eng, body)
                eng.wait_ge(w_in, 6 * 16)
                for b, (src, _dst, u0, u1) in enumerate(batches):
                    if b >= 2:
                        eng.wait_ge(w_done, b - 1)
                    for u in range(u0, u1):
                        last = eng.transpose(ps_w[b % 2][:, (u - u0) * P:(u - u0 + 1) * P], src[:, u, :], k.ident[:, :])
                    last.then_inc(w_turned, 1)

            @block.scalar
            def _(eng):
                eng.wait_ge(g_turned, 1)
                eng.activation(gateT[:, :], ps_l[:, 0:E_ALL], ACT.Copy).then_inc(g_done, 1)

                def body(s, p):
                    eng.wait_ge(logits_done, s)
                    norm.scalar_modulate(eng, ps_t[p], hT[:, p, :], s).then_inc(h_done, 1)
                    norm.scalar_modulate(eng, ps_t[p], r.h[:, s, :], s).then_inc(h_kept, 1)

                pairs_of(eng, body)
                for b, (_src, dst, u0, u1) in enumerate(batches):
                    eng.wait_ge(w_turned, b + 1)
                    eng.activation(dst[:, u0:u1, :].rearrange("p u i -> p (u i)"), ps_w[b % 2][:, 0:(u1 - u0) * P],
                                   ACT.Copy).then_inc(w_done, 1)

            @block.vector
            def _(eng):
                def body(s, p):
                    norm.vector_stats(eng, s, p)
                    eng.wait_ge(norm.turned, s)
                    norm.vector_normalise(eng, s, p)

                pairs_of(eng, body)
                eng.wait_ge(logits_done, B)
                eng.tensor_copy(logits[:, :, :].rearrange("p t e -> p (t e)"), ps_l[:, 0:TILES * E_ALL])

        route(nc, a, k, r, m, logits)


def route(nc, a, k, r, m, logits):
    S8 = [P, TILES, E_DYN]
    SKJ = [P, TILES, TOP_K, E_DYN]
    best, index, index_f = m.sb("r_best", S8), m.sb("r_index", S8, mybir.dt.uint32), m.sb("r_index_f", S8)
    negated, size = m.sb("r_negated", S8), m.sb("r_size", S8)
    apart, larger, close, expo = (m.sb(n, SKJ) for n in ("r_apart", "r_larger", "r_close", "r_expo"))
    kept_sum, slot_w = m.sb("r_kept_sum", [P, TILES, TOP_K]), m.sb("r_slot_w", [P, TILES, TOP_K])
    head_sum, whole, valid = m.sb("r_head_sum", [P, TILES, 3]), m.sb("r_whole", [P, TILES]), m.sb("r_valid", [P, TILES, 3])
    total, total_inv = m.sb("r_total", [P, TILES]), m.sb("r_total_inv", [P, TILES])
    experts = m.sb("r_experts", [P, E_DYN])
    chosen, weighed, rw = m.sb("r_chosen", SKJ), m.sb("r_weighed", SKJ), m.sb("r_rw", S8)
    mask, causal, ones = m.sb("r_mask", S8), m.sb("r_causal", [P, P]), m.sb("r_ones", [P, P])
    before = [m.sb("r_before0", [P, TILES + 1, E_DYN]), m.sb("r_before1", [P, TILES + 1, E_DYN])]
    count, fits, masked_l, penalty = m.sb("r_count", S8), m.sb("r_fits", S8), m.sb("r_masked_l", S8), m.sb("r_penalty", S8)
    top, shifted, expo9 = m.sb("r_top", [P, TILES]), m.sb("r_shifted", [P, TILES, E_ALL]), m.sb("r_expo9", [P, TILES, E_ALL])
    dyn_sum, all_sum, all_inv, dyn_share = (m.sb(n, [P, TILES]) for n in ("r_dyn_sum", "r_all_sum", "r_all_inv", "r_dyn_share"))
    ps_in, ps_all = m.ps("r_ps_in"), m.ps("r_ps_all")
    consts_in, pool_done = m.sem("r_consts_in"), m.sem("r_pool_done")
    step = m.sem("r_step")
    apart_done, expo_done, mask_done, counted = m.sem("r_apart_done"), m.sem("r_expo_done"), m.sem("r_mask_done"), m.sem("r_counted")
    shifted_done, expo9_done = m.sem("r_shifted_done"), m.sem("r_expo9_done")

    def over_j(t):
        return t.unsqueeze(3).to_broadcast([P, TILES, TOP_K, E_DYN])

    def over_k(t):
        return t.unsqueeze(2).to_broadcast([P, TILES, TOP_K, E_DYN])

    def over_e(t, n=E_DYN):
        return t.unsqueeze(2).to_broadcast([P, TILES, n])

    with nc.Block() as block:

        @block.sync
        def _(eng):
            eng.dma_start(causal[:, :], a["causal"]).then_inc(consts_in, 16)
            eng.dma_start(experts[:, :], a["experts"]).then_inc(consts_in, 16)

        @block.gpsimd
        def _(eng):
            eng.memset(ones[:, :], 1.0)
            for b in before:
                last = eng.memset(b[:, :, :].rearrange("p t e -> p (t e)"), 0.0)
            last.then_inc(pool_done, 1)

        @block.tensor
        def _(eng):
            eng.wait_ge(consts_in, 32)
            eng.wait_ge(pool_done, 1)
            eng.wait_ge(mask_done, 1)
            flat = mask[:, :, :].rearrange("p t e -> p (t e)")
            eng.matmul(ps_in[:, 0:TILES * E_DYN], causal[:, :], flat, start=True, stop=True)
            eng.matmul(ps_all[:, 0:TILES * E_DYN], ones[:, :], flat, start=True, stop=True).then_inc(counted, 1)

        @block.scalar
        def _(eng):
            eng.wait_ge(apart_done, 1)
            eng.activation(expo[:, :, :, :].rearrange("p t k j -> p (t k j)"),
                           apart[:, :, :, :].rearrange("p t k j -> p (t k j)"), ACT.Exp).then_inc(expo_done, 1)
            eng.wait_ge(shifted_done, 1)
            eng.activation(expo9[:, :, :].rearrange("p t e -> p (t e)"),
                           shifted[:, :, :].rearrange("p t e -> p (t e)"), ACT.Exp).then_inc(expo9_done, 1)

        @block.vector
        def _(eng):
            steps = [0]

            def then(ins):
                steps[0] += 1
                ins.then_inc(step, 1)
                eng.wait_ge(step, steps[0])

            for t in range(TILES):
                last = eng.max(best[:, t, :], logits[:, t, 0:E_DYN])
            then(last)
            eng.tensor_tensor(apart[:, :, :, :], over_k(best[:, :, :]), over_j(best[:, :, 0:TOP_K]), ALU.subtract).then_inc(apart_done, 1)
            for t in range(TILES):
                last = eng.max_index(index[:, t, :], best[:, t, :], logits[:, t, 0:E_DYN])
            then(last)
            eng.tensor_copy(index_f[:, :, :], index[:, :, :])
            then(eng.tensor_scalar(negated[:, :, :], best[:, :, :], -1.0, None, ALU.mult))
            then(eng.tensor_tensor(size[:, :, :], best[:, :, :], negated[:, :, :], ALU.max))
            then(eng.tensor_tensor(larger[:, :, :, :], over_k(size[:, :, :]), over_j(size[:, :, 0:TOP_K]), ALU.max))
            flat4 = lambda t: t[:, :, :, :].rearrange("p t k j -> p (t k j)")
            then(eng.scalar_tensor_tensor(flat4(close), flat4(larger), 2.0 * JITTER, flat4(apart), ALU.mult, ALU.add))
            eng.wait_ge(expo_done, 1)
            then(eng.scalar_tensor_tensor(flat4(larger), flat4(close), 0.0, flat4(expo), ALU.is_ge, ALU.mult))
            for j in range(TOP_K):
                last = eng.tensor_reduce(kept_sum[:, :, j], larger[:, :, j, j:E_DYN], AX.X, ALU.add)
            eng.tensor_reduce(whole[:, :], expo[:, :, 0, :], AX.X, ALU.add)
            for j in range(3):
                last = eng.tensor_reduce(head_sum[:, :, j], expo[:, :, 0, 0:j + 1], AX.X, ALU.add)
            then(last)
            eng.reciprocal(slot_w[:, :, :], kept_sum[:, :, :])
            then(eng.scalar_tensor_tensor(valid[:, :, :], over_e(whole[:, :], 3), TOP_P, head_sum[:, :, :], ALU.mult, ALU.is_gt))
            then(eng.tensor_tensor(slot_w[:, :, 1:TOP_K], slot_w[:, :, 1:TOP_K], valid[:, :, :], ALU.mult))
            then(eng.tensor_reduce(total[:, :], slot_w[:, :, :], AX.X, ALU.add))
            then(eng.reciprocal(total_inv[:, :], total[:, :]))
            then(eng.tensor_tensor(slot_w[:, :, :], slot_w[:, :, :], over_e(total_inv[:, :], TOP_K), ALU.mult))
            eng.wait_ge(consts_in, 32)
            then(eng.tensor_tensor(chosen[:, :, :, :], over_j(index_f[:, :, 0:TOP_K]),
                                   experts[:, :].unsqueeze(1).unsqueeze(1).to_broadcast(SKJ), ALU.is_equal))
            then(eng.tensor_tensor(weighed[:, :, :, :], chosen[:, :, :, :], over_j(slot_w[:, :, :]), ALU.mult))
            then(eng.tensor_reduce(rw[:, :, :], weighed[:, :, :, :].rearrange("p t k e -> p t e k"), AX.X, ALU.add))
            eng.tensor_scalar(mask[:, :, :], rw[:, :, :], 0.0, None, ALU.is_gt).then_inc(mask_done, 1)
            eng.wait_ge(counted, 1)
            eng.wait_ge(pool_done, 1)
            then(eng.tensor_copy(before[0][:, 1:TILES + 1, :], ps_all[:, 0:TILES * E_DYN].rearrange("p (t e) -> p t e", e=E_DYN)))
            reach, cur = 1, 0
            while reach < TILES:
                src, dst = before[cur], before[1 - cur]
                eng.tensor_copy(dst[:, 1:reach + 1, :], src[:, 1:reach + 1, :])
                then(eng.tensor_tensor(dst[:, reach + 1:TILES + 1, :], src[:, reach + 1:TILES + 1, :],
                                       src[:, 1:TILES + 1 - reach, :], ALU.add))
                reach, cur = 2 * reach, 1 - cur
            then(eng.tensor_tensor(count[:, :, :], ps_in[:, 0:TILES * E_DYN].rearrange("p (t e) -> p t e", e=E_DYN),
                                   before[cur][:, 0:TILES, :], ALU.add))
            then(eng.scalar_tensor_tensor(fits[:, :, :], count[:, :, :], float(CAPACITY), mask[:, :, :], ALU.is_le, ALU.mult))
            eng.tensor_tensor(masked_l[:, :, :], logits[:, :, 0:E_DYN], fits[:, :, :], ALU.mult)
            then(eng.tensor_scalar(penalty[:, :, :], fits[:, :, :], -1.0, 1e30, ALU.add, ALU.mult))
            then(eng.tensor_tensor(masked_l[:, :, :], masked_l[:, :, :], penalty[:, :, :], ALU.add))
            then(eng.tensor_reduce(top[:, :], masked_l[:, :, :], AX.X, ALU.max))
            then(eng.tensor_tensor(top[:, :], top[:, :], logits[:, :, E_DYN], ALU.max))
            eng.tensor_tensor(shifted[:, :, 0:E_DYN], masked_l[:, :, :], over_e(top[:, :]), ALU.subtract)
            eng.tensor_tensor(shifted[:, :, E_DYN], logits[:, :, E_DYN], top[:, :], ALU.subtract).then_inc(shifted_done, 1)
            eng.wait_ge(expo9_done, 1)
            eng.tensor_reduce(dyn_sum[:, :], expo9[:, :, 0:E_DYN], AX.X, ALU.add)
            then(eng.tensor_reduce(all_sum[:, :], expo9[:, :, :], AX.X, ALU.add))
            then(eng.reciprocal(all_inv[:, :], all_sum[:, :]))
            then(eng.tensor_tensor(dyn_share[:, :], dyn_sum[:, :], all_inv[:, :], ALU.mult))
            then(eng.tensor_tensor(rw[:, :, :], rw[:, :, :], fits[:, :, :], ALU.mult))
            eng.tensor_tensor(r.weights[:, :, 0:E_DYN], rw[:, :, :], over_e(dyn_share[:, :]), ALU.mult)
            eng.tensor_tensor(r.weights[:, :, E_DYN], expo9[:, :, E_DYN], all_inv[:, :], ALU.mult)


class Router:

    def __init__(self, m):
        self.h = m.sb("moe_h", [P, B, N])
        self.weights = m.sb("moe_weights", [P, TILES, E_ALL])
        self.gate, self.up, self.down = (m.sb("moe_" + n, [P, UNITS, P]) for n in ("gate", "up", "down"))


def expert_layers(nc, a, k, r):
    with ExitStack() as stack:
        m = Memory(nc, stack)
        pair = m.sb("e_pair", [P, 2, T, 64])
        rounded = m.sb("e_rounded", [64, 2, N], F32R)
        stacked = m.sb("e_stacked", [64, 2, N], F32R)
        low_rows = m.sb("e_low_rows", [64, 1])
        pick_raw, pick = m.sb("e_pick_raw", [64, DYN_UNITS + 1, P]), m.sb("e_pick", [64, DYN_UNITS + 1, P], F32R)
        silu_g, product, hidden = m.sb("e_silu_g", [P, 2, N]), m.sb("e_product", [P, 2, N]), m.sb("e_hidden", [P, 2, N])
        scaled = m.sb("e_scaled", [P, 2, N])
        ps_g, ps_u, ps_w = ([m.ps(f"e_ps_{n}{i}") for i in (0, 1)] for n in "guw")
        ps_y, ps_t = m.ps("e_ps_y"), m.ps("e_ps_t")
        S = m.sem
        consts_in, pool_ready, ready = S("e_consts_in"), S("e_pool_ready"), S("e_ready")
        pair_done, turned, rounded_done, stacked_done = S("e_pair_done"), S("e_turned"), S("e_rounded_done"), S("e_stacked_done")
        g_done, u_done, w_done, silu_done = S("e_g_done"), S("e_u_done"), S("e_w_done"), S("e_silu_done")
        product_done, hidden_done, down_done = S("e_product_done"), S("e_hidden_done"), S("e_down_done")
        scaled_done, x_done = S("e_scaled_done"), S("e_x_done")
        with nc.Block() as block:

            @block.sync
            def _(eng):
                eng.dma_start(pick_raw[:, :, :].rearrange("p u n -> p (u n)"), a["pick"]).then_inc(consts_in, 16)
                eng.dma_start(low_rows[:, :], a["low_rows"]).then_inc(consts_in, 16)

            @block.gpsimd
            def _(eng):
                eng.memset(pair[:, :, :, :].rearrange("p a t n -> p (a t n)"), 0.0).then_inc(pool_ready, 1)
                eng.wait_ge(pool_ready, 1)

                def copy_pair(s, p):
                    eng.wait_ge(turned, s)
                    for at in (0, 32):
                        last = eng.tensor_copy(pair[:, p, :, at:at + E_ALL], r.weights[:, bass.ds(s * T, T), :])
                    last.then_inc(pair_done, 1)

                def body(s, p):
                    copy_pair(s, p)
                    eng.wait_ge(scaled_done, s + 1)
                    xs = k.x[:, s, :, :].rearrange("p t d -> p (t d)")
                    eng.tensor_tensor(xs, scaled[:, p, :], xs, ALU.add).then_inc(x_done, 1)

                pairs_of(eng, body)

            @block.tensor
            def _(eng):
                eng.wait_ge(ready, 1)

                def body(s, p):
                    h = r.h[:, s, :]

                    def gate_up(u):
                        if u >= 2:
                            eng.wait_ge(silu_done, s * UNITS + u - 1)
                        else:
                            eng.wait_ge(silu_done, s * UNITS)
                        eng.matmul(ps_g[u % 2][:, :], r.gate[:, u, :], h, start=True, stop=True).then_inc(g_done, 1)
                        eng.wait_ge(product_done, s * UNITS + max(u - 1, 0))
                        eng.matmul(ps_u[u % 2][:, :], r.up[:, u, :], h, start=True, stop=True).then_inc(u_done, 1)

                    def weigh(u):
                        if u <= DYN_UNITS:
                            eng.wait_ge(stacked_done, s + 1)
                            eng.wait_ge(hidden_done, s * UNITS + max(u - 1, 0))
                            eng.matmul(ps_w[u % 2][:, :], pick[:, u, :], stacked[:, p, :], start=True, stop=True).then_inc(w_done, 1)

                    def down(u):
                        eng.wait_ge(hidden_done, s * UNITS + u + 1)
                        if u == 0:
                            eng.wait_ge(scaled_done, s)
                        for t in range(T):
                            last = eng.matmul(ps_y[:, t * P:(t + 1) * P], hidden[:, u % 2, t * P:(t + 1) * P], r.down[:, u, :],
                                              start=(u == 0 and t == 0), stop=(u == UNITS - 1), skip_group_check=True)
                        last.then_inc(down_done, 1)

                    gate_up(0)
                    eng.wait_ge(pair_done, s + 1)
                    eng.wait_ge(stacked_done, s)
                    apart(eng, k.passed)
                    for t in range(T):
                        last = eng.transpose(ps_t[0:64, t * P:(t + 1) * P], pair[:, p, t, :], k.ident[:, :])
                    last.then_inc(turned, 1)
                    gate_up(1)
                    weigh(0)
                    for u in range(UNITS):
                        if u + 2 < UNITS:
                            gate_up(u + 2)
                        if u + 1 < UNITS:
                            weigh(u + 1)
                        down(u)

                pairs_of(eng, body)

            @block.scalar
            def _(eng):
                def body(s, p):
                    for u in range(UNITS):
                        eng.wait_ge(g_done, s * UNITS + u + 1)
                        eng.wait_ge(product_done, s * UNITS + max(u - 1, 0))
                        eng.activation(silu_g[:, u % 2, :], ps_g[u % 2][:, :], ACT.Silu).then_inc(silu_done, 1)
                        if u == 1:
                            eng.wait_ge(turned, s + 1)
                            eng.wait_ge(stacked_done, s)
                            eng.activation(rounded[:, p, :], ps_t[0:64, :], ACT.Copy).then_inc(rounded_done, 1)

                pairs_of(eng, body)

            @block.vector
            def _(eng):
                eng.wait_ge(consts_in, 32)
                eng.tensor_copy(pick[:, :, :], pick_raw[:, :, :]).then_inc(ready, 1)

                def body(s, p):
                    def stack():
                        eng.wait_ge(rounded_done, s + 1)
                        eng.wait_ge(w_done, s * (DYN_UNITS + 1))
                        eng.scalar_tensor_tensor(stacked[:, p, :], rounded[:, p, :].bitcast(F32), low_rows[:, :], ps_t[0:64, :],
                                                 ALU.mult, ALU.add).then_inc(stacked_done, 1)

                    for u in range(UNITS):
                        eng.wait_ge(silu_done, s * UNITS + u + 1)
                        eng.wait_ge(u_done, s * UNITS + u + 1)
                        eng.wait_ge(hidden_done, s * UNITS + max(u - 1, 0))
                        eng.tensor_tensor(product[:, u % 2, :], silu_g[:, u % 2, :], ps_u[u % 2][:, :], ALU.mult).then_inc(product_done, 1)
                        if u == 0:
                            stack()
                        eng.wait_ge(product_done, s * UNITS + u + 1)
                        eng.wait_ge(w_done, s * (DYN_UNITS + 1) + min(u, DYN_UNITS) + 1)
                        eng.wait_ge(down_done, s * UNITS + max(u - 1, 0))
                        eng.tensor_tensor(hidden[:, u % 2, :], product[:, u % 2, :], ps_w[min(u, DYN_UNITS) % 2][:, :],
                                          ALU.mult).then_inc(hidden_done, 1)
                    eng.wait_ge(down_done, s * UNITS + UNITS)
                    eng.wait_ge(x_done, s)
                    eng.tensor_tensor(scaled[:, p, :].rearrange("p (t d) -> p t d", t=T), ps_y[:, :].rearrange("p (t d) -> p t d", t=T),
                                      k.gates[:, s, 1, :].unsqueeze(1).to_broadcast([P, T, D]), ALU.mult).then_inc(scaled_done, 1)

                pairs_of(eng, body)


H1, DK, DC = 8, 128, 32
DKV = 2 * DC
SCALE = float(1.0 / np.sqrt(DK + DC))


def rounds(eng, body):
    body(0, None, 1, 0)
    with eng.Fori(0, (B - 2) // 2) as i:
        body(2 * i + 1, 2 * i, 2 * i + 2, 1)
        body(2 * i + 2, 2 * i + 1, 2 * i + 3, 0)
    body(B - 1, B - 2, None, 1)
    body(None, B - 1, None, 0)


class Latent:

    def __init__(self, m):
        self.q_lat = m.sb("l_q_lat", [P, P])
        self.kv_lat = m.sb("l_kv_lat", [P, P])
        self.bias = m.sb("l_bias", [2, 2, P], F32R)
        self.ones2 = m.sb("l_ones2", [2, N], F32R)
        self.query = m.sb("l_query", [P, H1, 2, DKV], F32R)
        self.out = m.sb("l_out", [P, 2, D])
        self.const = m.sb("l_const", [P, D])
        self.kv_bias = m.sb("l_kv_bias", [P, DC])
        self.q_low, self.upper_low = m.sb("l_q_low", [P, 1]), m.sb("l_upper_low", [P, 1])


def fold_latent(nc, a, k, w):
    with ExitStack() as stack:
        m = Memory(nc, stack)
        uq, uk, uv = m.sb("f_uq", [DC + 1, H1, DK]), m.sb("f_uk", [DC, H1, DK]), m.sb("f_uv", [DC, H1, DK])
        qr, wo = m.sb("f_qr", [DC + 1, H1, DC]), m.sb("f_wo", [P, H1, D])
        b_uv_rows = m.sb("f_b_uv_rows", [H1, DK])
        b_uv, b_uv_wide, b_o = m.sb("f_b_uv", [P, H1]), m.sb("f_b_uv_wide", [P, H1, P]), m.sb("f_b_o", [P, D])
        uqT, ukT, uvT = m.sb("f_uqT", [P, H1, DC + 1]), m.sb("f_ukT", [P, H1, DC]), m.sb("f_uvT", [P, H1, DC])
        met = m.sb("f_met", [DC + 1, H1, DKV])
        place, low_w, low2 = m.sb("f_place", [DC + 1, P]), m.sb("f_low_w", [P, 1]), m.sb("f_low2", [2, 1])
        rounded = m.sb("f_rounded", [P, H1 * DKV], F32R)
        bias2, bias2_hi = m.sb("f_bias2", [2, 2, P]), m.sb("f_bias2_hi", [2, 2, P], F32R)
        ps = {n: m.ps("f_ps_" + n) for n in ("uq", "uk", "uv", "met", "query", "out", "const")}
        pool_done, in_done = m.sem("f_pool_done"), m.sem("f_in_done")
        turned, copied, products, met_done, placed, step = (m.sem("f_" + n) for n in
                                                            ("turned", "copied", "products", "met_done", "placed", "step"))
        loads = []
        with nc.Block() as block:

            @block.sync
            def _(eng):
                eng.wait_ge(pool_done, 1)

                def load(dst, src):
                    eng.dma_start(dst, src).then_inc(in_done, 16)
                    loads.append(src)

                row = lambda v: v.rearrange("(o n) -> o n", o=1)
                heads = lambda t: t.rearrange("p h d -> p (h d)")
                load(heads(uq[0:DC, :, :]), a["L1_attn_W_UQ"])
                load(heads(uq[DC:DC + 1, :, :]), row(a["L1_attn_b_UQ"]))
                load(heads(uk[:, :, :]), a["L1_attn_W_UK"])
                load(heads(uv[:, :, :]), a["L1_attn_W_UV"])
                load(heads(qr[0:DC, :, :]), a["L1_attn_W_QR"])
                load(heads(qr[DC:DC + 1, :, :]), row(a["L1_attn_b_QR"]))
                load(wo[:, :, :], a["L1_attn_W_O"].rearrange("(h d) n -> d h n", h=H1))
                load(b_uv_rows[:, :], a["L1_attn_b_UV"].rearrange("(h d) -> h d", h=H1))
                load(b_o[:, :], a["L1_attn_b_O"].partition_broadcast(P))
                load(w.kv_bias[:, :], a["L1_attn_b_DKV"].partition_broadcast(P))
                for copy in range(3):
                    load(w.q_lat[:, copy * DC:(copy + 1) * DC], a["L1_attn_W_DQ"])
                    load(bias2[:, 0, copy * DC:(copy + 1) * DC], a["L1_attn_b_DQ"].partition_broadcast(2))
                for copy in range(4):
                    which = "DKV" if copy % 2 == 0 else "KR"
                    load(w.kv_lat[:, copy * DC:(copy + 1) * DC], a[f"L1_attn_W_{which}"])
                    load(bias2[:, 1, copy * DC:(copy + 1) * DC], a[f"L1_attn_b_{which}"].partition_broadcast(2))
                load(place[:, :], a["place"])
                load(low_w[:, :], a["low_w"])
                load(low2[:, :], a["low_rows"][31:33, :])
                load(w.q_low[:, :], a["q_low"])
                load(w.upper_low[:, :], a["upper_low"])
            IN = 16 * len(loads)

            @block.gpsimd
            def _(eng):
                eng.memset(w.q_lat[:, :], 0.0)
                eng.memset(w.ones2[:, :].bitcast(F32), 1.0)
                eng.memset(bias2[:, :, :], 1.0).then_inc(pool_done, 1)

            @block.tensor
            def _(eng):
                eng.wait_ge(in_done, IN)
                for name, src, rows in (("uq", uq, DC + 1), ("uk", uk, DC), ("uv", uv, DC)):
                    for h in range(H1):
                        last = eng.transpose(ps[name][:, h * rows:(h + 1) * rows], src[:, h, :], k.ident[0:rows, 0:rows])
                    last.then_inc(turned, 1)
                eng.transpose(ps["const"][:, 0:H1], b_uv_rows[:, :], k.ident[0:H1, 0:H1]).then_inc(turned, 1)
                eng.wait_ge(copied, 4)
                for h in range(H1):
                    last = eng.matmul(ps["met"][0:DC + 1, h * DC:(h + 1) * DC], uqT[:, h, :], ukT[:, h, :], start=True, stop=True)
                last.then_inc(products, 1)
                for h in range(H1):
                    g, j = divmod(h, 4)
                    last = eng.matmul(ps["out"][32 * j:32 * j + 32, g * D:(g + 1) * D], uvT[:, h, :], wo[:, h, :],
                                      start=True, stop=True, skip_group_check=True)
                last.then_inc(products, 1)
                eng.wait_ge(met_done, 1)
                eng.matmul(ps["query"][:, :], place[:, :], met[:, :, :].rearrange("p h c -> p (h c)"), start=True, stop=True).then_inc(placed, 1)
                for h in range(H1):
                    last = eng.matmul(ps["const"][:, 0:D], b_uv_wide[:, h, :], wo[:, h, :], start=(h == 0), stop=(h == H1 - 1))
                last.then_inc(placed, 1)

            @block.scalar
            def _(eng):
                for n, (name, dst) in enumerate((("uq", uqT), ("uk", ukT), ("uv", uvT), ("const", b_uv))):
                    flat = dst[:, :] if name == "const" else dst[:, :, :].rearrange("p h c -> p (h c)")
                    eng.wait_ge(turned, n + 1)
                    eng.activation(flat, ps[name][:, 0:flat.shape[1]], ACT.Copy).then_inc(copied, 1)

            @block.vector
            def _(eng):
                eng.wait_ge(in_done, IN)
                eng.tensor_copy(met[:, :, DC:DKV], qr[:, :, :])
                eng.tensor_copy(bias2_hi[:, :, :], bias2[:, :, :]).then_inc(step, 1)
                eng.wait_ge(copied, 4)
                eng.tensor_copy(b_uv_wide[:, :, :], b_uv[:, :].unsqueeze(2).to_broadcast([P, H1, P]))
                eng.wait_ge(products, 1)
                eng.tensor_copy(met[:, :, 0:DC], ps["met"][0:DC + 1, 0:H1 * DC].rearrange("p (h c) -> p h c", h=H1)).then_inc(met_done, 1)
                eng.wait_ge(step, 1)
                eng.scalar_tensor_tensor(w.bias[:, :, :], bias2_hi[:, :, :].bitcast(F32), low2[:, :], bias2[:, :, :], ALU.mult, ALU.add)
                eng.wait_ge(products, 2)
                eng.tensor_copy(w.out[:, :, :].rearrange("p g n -> p (g n)"), ps["out"][:, 0:2 * D])
                eng.wait_ge(placed, 1)
                eng.tensor_copy(rounded[:, :], ps["query"][:, :]).then_inc(step, 1)
                eng.wait_ge(step, 2)
                for copy in range(2):
                    eng.scalar_tensor_tensor(w.query[:, :, copy, :], rounded[:, :].bitcast(F32).rearrange("p (h c) -> p h c", h=H1), low_w[:, :],
                                             ps["query"][:, :].rearrange("p (h c) -> p h c", h=H1), ALU.mult, ALU.add)
                eng.wait_ge(placed, 2)
                eng.tensor_tensor(w.const[:, :], ps["const"][:, 0:D], b_o[:, :], ALU.add)


def latent_attention(nc, a, k, w):
    with ExitStack() as stack:
        m = Memory(nc, stack)
        norm = Norm(m, k, 1, SA, CA)
        hT = m.sb("a_hT", [P, 2, N])
        q_lat_hi, q_lat = m.sb("a_q_lat_hi", [P, N], F32R), m.sb("a_q_lat", [P, N], F32R)
        key_hi, key_lo = m.sb("a_key_hi", [P, 2, N], F32R), m.sb("a_key_lo", [P, 2, N], F32R)
        value = m.sb("a_value", [P, 2, T, 2 * DC])
        q_hi, q_both = m.sb("a_q_hi", [P, 2, H1, N], F32R), m.sb("a_q_both", [P, 2, H1, N], F32R)
        top, shift = m.sb("a_top", [P, H1 * T]), m.sb("a_shift", [H1 * T, P])
        expo = m.sb("a_expo", [P, 2, 2, T, N])
        weighted = m.sb("a_weighted", [P, H1 // 2, N])
        inverse, mixed = m.sb("a_inverse", [P, T, H1]), m.sb("a_mixed", [P, T, H1, DC])
        mixedT = m.sb("a_mixedT", [P, 2, N])
        out_w, const_g = m.sb("a_out_w", [P, 2, D]), m.sb("a_const_g", [P, D])
        ps_f, ps_m, ps_s = ([m.ps(f"a_ps_{n}{i}") for i in (0, 1)] for n in "fms")
        ps_v, ps_y = m.ps("a_ps_v"), m.ps("a_ps_y")
        S = m.sem
        filled, emptied = [S("a_filled0"), S("a_filled1")], [S("a_emptied0"), S("a_emptied1")]
        pool_ready, h_done = S("a_pool_ready"), S("a_h_done")
        lat_hi_done, key_hi_done, q_hi_done = S("a_lat_hi_done"), S("a_key_hi_done"), S("a_q_hi_done")
        rough, top_done, shift_in = S("a_rough"), S("a_top_done"), S("a_shift_in")
        scores_done, expo_done, pv_done, weighted_done = S("a_scores_done"), S("a_expo_done"), S("a_pv_done"), S("a_weighted_done")
        w_turned, inverse_done, mixed_done, m_turned, mixedT_done = (
            S("a_w_turned"), S("a_inverse_done"), S("a_mixed_done"), S("a_m_turned"), S("a_mixedT_done"))
        const_done, pre_done, out_w_done, y_done, x_done = S("a_const_done"), S("a_pre_done"), S("a_out_w_done"), S("a_y_done"), S("a_x_done")
        LAT, KEY, VALUE, QUERY, TOP = 0, 1, 2, 3, 3 + H1
        USES = (TOP + 1) // 2
        HT = H1 * T

        def nth(n, s):
            return s * USES + n // 2 + 1

        with nc.Block() as block:

            @block.gpsimd
            def _(eng):
                norm.pool_setup(eng)
                eng.memset(value[:, :, :, :].rearrange("p a t n -> p (a t n)"), 1.0).then_inc(pool_ready, 1)
                eng.wait_ge(pool_ready, 1)
                eng.memset(key_lo[DKV:P, :, :].bitcast(F32), 0.0).then_inc(pool_ready, 1)
                eng.wait_ge(pool_ready, 2)
                eng.memset(key_lo[DKV:DKV + 1, :, :].bitcast(F32), 1.0).then_inc(pool_ready, 1)
                norm.pool_rstd(eng, 0, 0)

                def body(front, back, nxt, p):
                    if back is not None:
                        eng.tensor_tensor(out_w[:, :, :], w.out[:, :, :],
                                          k.gates[:, back, 2, :].unsqueeze(1).to_broadcast([P, 2, D]), ALU.mult).then_inc(out_w_done, 1)
                        eng.tensor_tensor(const_g[:, :], w.const[:, :], k.gates[:, back, 2, :], ALU.mult).then_inc(const_done, 1)
                        eng.wait_ge(const_done, back + 1)
                        eng.wait_ge(norm.xn_done, back + 1)
                        eng.tensor_tensor(k.x[:, back, :, :], k.x[:, back, :, :],
                                          const_g[:, :].unsqueeze(1).to_broadcast([P, T, D]), ALU.add).then_inc(pre_done, 1)
                    if nxt is not None:
                        norm.pool_rstd(eng, nxt, 1 - p)
                    if front is not None:
                        eng.wait_ge(emptied[TOP % 2], nth(TOP, front))
                        apart(eng, k.passed)
                        eng.dma_start(q_hi[DKV:DKV + 1, p, :, :].rearrange("o h (t n) -> o (h t) n", t=T),
                                      shift[:, :]).then_inc(shift_in, 16)
                    if back is not None:
                        eng.wait_ge(y_done, back + 1)
                        eng.wait_ge(pre_done, back + 1)

                rounds(eng, body)

            @block.tensor
            def _(eng):
                eng.wait_ge(pool_ready, 3)
                norm.tensor_turn(eng, ps_y, 0, 0)

                def latent(s, p, n):
                    weights = (w.q_lat, w.kv_lat)[n]
                    eng.wait_ge(h_done, s + 1)
                    eng.wait_ge(emptied[n % 2], nth(n, s) - 1)
                    eng.matmul(ps_f[n % 2][:, :], weights[:, :], hT[:, p, :], start=True, stop=False)
                    eng.matmul(ps_f[n % 2][:, :], w.bias[:, n, :], w.ones2[:, :], start=False, stop=True).then_inc(filled[n % 2], 1)

                def latent_values(s, p):
                    eng.wait_ge(emptied[VALUE % 2], nth(VALUE, s) - 1)
                    for t in range(T):
                        last = eng.matmul(ps_f[VALUE % 2][:, t * DC:(t + 1) * DC], hT[:, p, t * P:(t + 1) * P], w.kv_lat[:, 0:DC],
                                          start=True, stop=True)
                    last.then_inc(filled[VALUE % 2], 1)

                def queries(s, p, h):
                    n = QUERY + h
                    if h == 0:
                        eng.wait_ge(emptied[LAT % 2], nth(LAT, s))
                    eng.wait_ge(emptied[n % 2], nth(n, s) - 1)
                    eng.matmul(ps_f[n % 2][:, :], w.query[:, h, :, :].rearrange("p c n -> p (c n)"), q_lat[:, :],
                               start=True, stop=True).then_inc(filled[n % 2], 1)

                def rough_scores(s, p, h, t):
                    n = h * T + t
                    if t == 0:
                        eng.wait_ge(q_hi_done, s * H1 + h + 1)
                    if n == 0:
                        eng.wait_ge(emptied[KEY % 2], nth(KEY, s))
                    eng.wait_ge(top_done, s * HT + max(n - 1, 0))
                    eng.matmul(ps_m[n % 2][:, :], q_hi[0:DKV, p, h, t * P:(t + 1) * P], key_hi[0:DKV, p, :],
                               start=True, stop=True).then_inc(rough, 1)

                def scores(s, p, h, t):
                    n = h * T + t
                    if n == 0:
                        eng.wait_ge(shift_in, s * 16 + 16)
                    if n >= 2:
                        eng.wait_ge(expo_done, s * HT + n - 1)
                    eng.matmul(ps_s[n % 2][:, :], key_hi[:, p, t * P:(t + 1) * P], q_both[:, p, h, :], start=True, stop=False)
                    eng.matmul(ps_s[n % 2][:, :], key_lo[:, p, t * P:(t + 1) * P], q_hi[:, p, h, :],
                               start=False, stop=True).then_inc(scores_done, 1)

                def pair_values(s, p, pair, t):
                    if t == 0:
                        eng.wait_ge(expo_done, s * HT + 2 * T * (pair + 1))
                    if t == 0 and pair > 0:
                        eng.wait_ge(weighted_done, s * 4 + pair)
                    for h in range(2):
                        last = eng.matmul(ps_v[DKV * h:DKV * (h + 1), :], value[:, p, t, :], expo[:, pair % 2, h, t, :],
                                          start=(t == 0), stop=(t == T - 1), skip_group_check=True)
                    if t == T - 1:
                        last.then_inc(pv_done, 1)

                def tail(s, p):
                    eng.wait_ge(weighted_done, s * 4 + 4)
                    for t in range(T):
                        if t >= 2:
                            eng.wait_ge(mixed_done, s * T + t - 1)
                        for pair in range(H1 // 2):
                            last = eng.transpose(ps_m[t % 2][:, pair * P:(pair + 1) * P], weighted[:, pair, t * P:(t + 1) * P], k.ident[:, :])
                        last.then_inc(w_turned, 1)
                    for g in range(2):
                        eng.wait_ge(mixed_done, s * T + T)
                        for t in range(T):
                            last = eng.transpose(ps_m[g][:, t * P:(t + 1) * P],
                                                 mixed[:, t, 4 * g:4 * g + 4, :].rearrange("p h c -> p (h c)"), k.ident[:, :])
                        last.then_inc(m_turned, 1)
                    eng.wait_ge(mixedT_done, s * 2 + 2)
                    eng.wait_ge(out_w_done, s + 1)
                    for t in range(T):
                        for g in range(2):
                            last = eng.matmul(ps_y[:, t * P:(t + 1) * P], mixedT[:, g, t * P:(t + 1) * P], out_w[:, g, :],
                                              start=(g == 0), stop=(g == 1))
                    last.then_inc(y_done, 1)

                def body(front, back, nxt, p):
                    if front is not None:
                        queries(front, p, 0)
                    for h in range(H1):
                        for t in range(T):
                            if back is not None:
                                scores(back, 1 - p, h, t)
                            if front is not None:
                                rough_scores(front, p, h, t)
                            if front is not None and t == 0 and h + 1 < H1:
                                queries(front, p, h + 1)
                            if back is not None and h >= 2 and t % 2 == 0:
                                pair_values(back, 1 - p, h // 2 - 1, (h % 2) * 2 + t // 2)
                        if nxt is not None and h == 5:
                            norm.tensor_turn(eng, ps_y, nxt, 1 - p)
                    if nxt is not None:
                        latent(nxt, 1 - p, LAT)
                    if back is not None:
                        for t in range(T):
                            pair_values(back, 1 - p, 3, t)
                    if front is not None:
                        eng.wait_ge(top_done, front * HT + HT)
                        eng.wait_ge(emptied[TOP % 2], nth(TOP, front) - 1)
                        eng.transpose(ps_f[TOP % 2][0:HT, 0:P], top[:, :], k.ident[:, :]).then_inc(filled[TOP % 2], 1)
                    if nxt is not None:
                        latent(nxt, 1 - p, KEY)
                        latent_values(nxt, 1 - p)
                    if back is not None:
                        tail(back, 1 - p)

                latent(0, 0, LAT)
                latent(0, 0, KEY)
                latent_values(0, 0)
                rounds(eng, body)

            @block.scalar
            def _(eng):
                norm.scalar_modulate(eng, ps_y, hT[:, 0, :], 0).then_inc(h_done, 1)

                def latent_hi(s, p):
                    eng.wait_ge(filled[LAT % 2], nth(LAT, s))
                    eng.activation(q_lat_hi[:, :], ps_f[LAT % 2][:, :], ACT.Copy).then_inc(lat_hi_done, 1)

                def key_high(s, p):
                    eng.wait_ge(filled[KEY % 2], nth(KEY, s))
                    eng.activation(key_hi[:, p, :], ps_f[KEY % 2][:, :], ACT.Copy).then_inc(key_hi_done, 1)

                def query_hi(s, p, h):
                    n = QUERY + h
                    eng.wait_ge(filled[n % 2], nth(n, s))
                    eng.activation(q_hi[:, p, h, :], ps_f[n % 2][:, :], ACT.Copy).then_inc(q_hi_done, 1)

                def read_values(s, pair):
                    eng.wait_ge(pv_done, s * 4 + pair + 1)
                    eng.activation(weighted[:, pair, :], ps_v[:, :], ACT.Copy).then_inc(weighted_done, 1)

                def body(front, back, nxt, p):
                    if front is not None:
                        query_hi(front, p, 0)
                    for h in range(H1):
                        for t in range(T):
                            if back is not None:
                                n = h * T + t
                                eng.wait_ge(scores_done, back * HT + n + 1)
                                eng.activation(expo[:, (h // 2) % 2, h % 2, t, :], ps_s[n % 2][:, :], ACT.Exp, scale=SCALE).then_inc(expo_done, 1)
                            if front is not None and t == 1 and h + 1 < H1:
                                query_hi(front, p, h + 1)
                        if back is not None and h in (3, 5, 7):
                            read_values(back, h // 2 - 1)
                        if nxt is not None and h == 6:
                            norm.scalar_modulate(eng, ps_y, hT[:, 1 - p, :], nxt).then_inc(h_done, 1)
                    if nxt is not None:
                        latent_hi(nxt, 1 - p)
                    if back is not None:
                        read_values(back, 3)
                    if nxt is not None:
                        key_high(nxt, 1 - p)
                    if back is not None:
                        for g in range(2):
                            eng.wait_ge(m_turned, back * 2 + g + 1)
                            eng.activation(mixedT[:, g, :], ps_m[g][:, :], ACT.Copy).then_inc(mixedT_done, 1)

                latent_hi(0, 0)
                key_high(0, 0)
                rounds(eng, body)

            @block.vector
            def _(eng):
                eng.wait_ge(pool_ready, 3)
                norm.vector_stats(eng, 0, 0)
                norm.vector_normalise(eng, 0, 0)

                def latent_low(s, p):
                    eng.wait_ge(lat_hi_done, s + 1)
                    eng.scalar_tensor_tensor(q_lat[:, :], q_lat_hi[:, :].bitcast(F32), w.q_low[:, :], ps_f[LAT % 2][:, :],
                                             ALU.mult, ALU.add).then_inc(emptied[LAT % 2], 1)

                def key_low(s, p):
                    eng.wait_ge(key_hi_done, s + 1)
                    eng.tensor_tensor(key_lo[0:DKV, p, :], ps_f[KEY % 2][0:DKV, :], key_hi[0:DKV, p, :].bitcast(F32),
                                      ALU.subtract).then_inc(emptied[KEY % 2], 1)
                    eng.wait_ge(filled[VALUE % 2], nth(VALUE, s))
                    eng.tensor_tensor(value[:, p, :, 0:DC], ps_f[VALUE % 2][:, 0:T * DC].rearrange("p (t c) -> p t c", t=T),
                                      w.kv_bias[:, :].unsqueeze(1).to_broadcast([P, T, DC]), ALU.add).then_inc(emptied[VALUE % 2], 1)

                def query_low(s, p, h):
                    n = QUERY + h
                    eng.wait_ge(q_hi_done, s * H1 + h + 1)
                    eng.scalar_tensor_tensor(q_both[:, p, h, :], q_hi[:, p, h, :].bitcast(F32), w.upper_low[:, :],
                                             ps_f[n % 2][:, :], ALU.mult, ALU.add).then_inc(emptied[n % 2], 1)

                def body(front, back, nxt, p):
                    if front is not None:
                        query_low(front, p, 0)
                    for h in range(H1):
                        if front is not None:
                            for t in range(T):
                                n = h * T + t
                                eng.wait_ge(rough, front * HT + n + 1)
                                eng.tensor_reduce(top[:, n:n + 1], ps_m[n % 2][:, :], AX.X, ALU.max).then_inc(top_done, 1)
                                if t == 2 and h + 1 < H1:
                                    query_low(front, p, h + 1)
                        if nxt is not None and h == 2:
                            norm.vector_stats(eng, nxt, 1 - p)
                        if nxt is not None and h == 4:
                            norm.vector_normalise(eng, nxt, 1 - p)
                    if nxt is not None:
                        latent_low(nxt, 1 - p)
                    if front is not None:
                        eng.wait_ge(filled[TOP % 2], nth(TOP, front))
                        eng.wait_ge(shift_in, front * 16)
                        eng.tensor_scalar(shift[:, :], ps_f[TOP % 2][0:HT, 0:P], -1.0, None, ALU.mult).then_inc(emptied[TOP % 2], 1)
                    if nxt is not None:
                        key_low(nxt, 1 - p)
                    if back is not None:
                        s = back
                        for t in range(T):
                            eng.wait_ge(w_turned, s * T + t + 1)
                            by_head = ps_m[t % 2][:, :].rearrange("p (h c) -> p h c", h=H1)
                            eng.reciprocal(inverse[:, t, :], by_head[:, :, DC]).then_inc(inverse_done, 1)
                            eng.wait_ge(inverse_done, s * T + t + 1)
                            eng.tensor_tensor(mixed[:, t, :, :], by_head[:, :, 0:DC],
                                              inverse[:, t, :].unsqueeze(2).to_broadcast([P, H1, DC]), ALU.mult).then_inc(mixed_done, 1)
                        eng.wait_ge(y_done, s + 1)
                        eng.wait_ge(pre_done, s + 1)
                        xs = k.x[:, s, :, :].rearrange("p t d -> p (t d)")
                        eng.tensor_tensor(xs, ps_y[:, :], xs, ALU.add).then_inc(x_done, 1)

                latent_low(0, 0)
                key_low(0, 0)
                rounds(eng, body)


HID = 512
Q1 = HID // P


def one_ahead(eng, body):
    body(0, 1, 0)
    with eng.Fori(0, (B - 2) // 2) as i:
        body(2 * i + 1, 2 * i + 2, 1)
        body(2 * i + 2, 2 * i + 3, 0)
    body(B - 1, None, 1)


class Binary:

    def __init__(self, m):
        self.sign1T = m.sb("b_sign1T", [P, Q1, P], F32R)
        self.sign2T = m.sb("b_sign2T", [P, Q1, D])
        self.alpha1, self.b1 = m.sb("b_alpha1", [P, Q1]), m.sb("b_b1", [P, Q1])
        self.alpha2, self.b2 = m.sb("b_alpha2", [P, D]), m.sb("b_b2", [P, D])


def binarise(nc, a, k, w):
    with ExitStack() as stack:
        m = Memory(nc, stack)
        w1, w2, b1_rows = m.sb("z_w1", [P, Q1, D]), m.sb("z_w2", [P, HID]), m.sb("z_b1_rows", [Q1, P])
        sign1, sign2 = m.sb("z_sign1", [P, Q1, D]), m.sb("z_sign2", [P, HID])
        size1, size2 = m.sb("z_size1", [P, Q1, D]), m.sb("z_size2", [P, HID])
        sum1, sum2, diag = m.sb("z_sum1", [P, Q1]), m.sb("z_sum2", [P, 1]), m.sb("z_diag", [P, P])
        ones = m.sb("z_ones", [P, P])
        ps_1, ps_2, ps_b, ps_a = (m.ps("z_ps_" + n) for n in ("1", "2", "b", "a"))
        in_done, ones_done, signs_done, sizes_done, sums_done, diag_done, turned, spread = (
            m.sem("z_" + n) for n in ("in", "ones", "signs", "sizes", "sums", "diag", "turned", "spread"))
        with nc.Block() as block:

            @block.sync
            def _(eng):
                eng.dma_start(w1[:, :, :], a["L1_ffn_w1"].rearrange("(q p) d -> p q d", p=P)).then_inc(in_done, 16)
                eng.dma_start(w2[:, :], a["L1_ffn_w2"]).then_inc(in_done, 16)
                eng.dma_start(b1_rows[:, :], a["L1_ffn_b1"].rearrange("(q p) -> q p", p=P)).then_inc(in_done, 16)
                eng.dma_start(w.b2[:, :], a["L1_ffn_b2"].partition_broadcast(P)).then_inc(in_done, 16)

            @block.gpsimd
            def _(eng):
                eng.memset(ones[:, :], 1.0).then_inc(ones_done, 1)

            @block.tensor
            def _(eng):
                eng.wait_ge(in_done, 64)
                eng.transpose(ps_b[:, 0:Q1], b1_rows[:, :], k.ident[0:Q1, 0:Q1]).then_inc(turned, 1)
                eng.wait_ge(signs_done, 2)
                for q in range(Q1):
                    last = eng.transpose(ps_1[:, q * P:(q + 1) * P], sign1[:, q, :], k.ident[:, :])
                last.then_inc(turned, 1)
                for q in range(Q1):
                    last = eng.transpose(ps_2[:, q * P:(q + 1) * P], sign2[:, q * P:(q + 1) * P], k.ident[:, :])
                last.then_inc(turned, 1)
                eng.wait_ge(diag_done, 1)
                eng.wait_ge(ones_done, 1)
                eng.matmul(ps_a[:, 0:D], ones[:, :], diag[:, :], start=True, stop=True).then_inc(spread, 1)

            @block.scalar
            def _(eng):
                flat = lambda t: t[:, :, :].rearrange("p q d -> p (q d)")
                eng.wait_ge(in_done, 64)
                eng.activation(flat(sign1), flat(w1), ACT.Sign).then_inc(signs_done, 1)
                eng.activation(sign2[:, :], w2[:, :], ACT.Sign).then_inc(signs_done, 1)
                eng.activation(flat(size1), flat(w1), ACT.Abs).then_inc(sizes_done, 1)
                eng.activation(size2[:, :], w2[:, :], ACT.Abs).then_inc(sizes_done, 1)
                eng.wait_ge(turned, 1)
                eng.activation(w.b1[:, :], ps_b[:, 0:Q1], ACT.Copy)
                eng.wait_ge(turned, 2)
                eng.activation(flat(w.sign1T), ps_1[:, :], ACT.Copy)
                eng.wait_ge(turned, 3)
                eng.activation(flat(w.sign2T), ps_2[:, :], ACT.Copy)

            @block.vector
            def _(eng):
                eng.wait_ge(sizes_done, 1)
                eng.tensor_reduce(sum1[:, :], size1[:, :, :], AX.X, ALU.add).then_inc(sums_done, 1)
                eng.wait_ge(sizes_done, 2)
                eng.tensor_reduce(sum2[:, :], size2[:, :], AX.X, ALU.add).then_inc(sums_done, 1)
                eng.wait_ge(sums_done, 2)
                eng.tensor_scalar(w.alpha1[:, :], sum1[:, :], 1.0 / D, None, ALU.mult)
                eng.tensor_scalar(diag[:, :], k.ident[:, :], sum2[:, :], 1.0 / HID, ALU.mult, ALU.mult).then_inc(diag_done, 1)
                eng.wait_ge(spread, 1)
                eng.tensor_copy(w.alpha2[:, :], ps_a[:, 0:D])


def feed_forward(nc, a, k, w, out):
    with ExitStack() as stack:
        m = Memory(nc, stack)
        norm = Norm(m, k, 1, SB, CB)
        hT = m.sb("d_hT", [P, 2, N])
        h_hi, h_lo = m.sb("d_h_hi", [P, 2, N], F32R), m.sb("d_h_lo", [P, 2, N], F32R)
        hidden, scaled = m.sb("d_hidden", [P, 2, Q1, N]), m.sb("d_scaled", [P, 2, N])
        gate_alpha, gate_b2 = m.sb("d_gate_alpha", [P, 2, D]), m.sb("d_gate_b2", [P, 2, D])
        ps_up, ps_y, ps_h = [m.ps(f"d_ps_up{q}") for q in range(Q1)], [m.ps(f"d_ps_y{p}") for p in (0, 1)], m.ps("d_ps_h")
        S = m.sem
        h_done, hi_done, lo_done, up_done, gelu_done = S("d_h_done"), S("d_hi_done"), S("d_lo_done"), S("d_up_done"), S("d_gelu_done")
        gates_done, pre_done, y_done, scaled_done, x_done, stored = (
            S("d_gates_done"), S("d_pre_done"), S("d_y_done"), S("d_scaled_done"), S("d_x_done"), S("d_stored"))
        with nc.Block() as block:

            @block.sync
            def _(eng):
                with eng.Fori(0, B) as s:
                    eng.wait_ge(x_done, s + 1)
                    eng.dma_start(out[s, :, :].rearrange("(t p) d -> p t d", p=P), k.x[:, s, :, :]).then_inc(stored, 16)
                eng.wait_ge(stored, 16 * B)

            @block.gpsimd
            def _(eng):
                norm.pool_setup(eng)
                norm.pool_rstd(eng, 0, 0)

                def body(s, nxt, p):
                    eng.wait_ge(scaled_done, s)
                    eng.tensor_tensor(gate_alpha[:, p, :], w.alpha2[:, :], k.gates[:, s, 3, :], ALU.mult)
                    eng.tensor_tensor(gate_b2[:, p, :], w.b2[:, :], k.gates[:, s, 3, :], ALU.mult).then_inc(gates_done, 1)
                    if nxt is not None:
                        norm.pool_rstd(eng, nxt, 1 - p)
                    eng.wait_ge(gates_done, s + 1)
                    eng.wait_ge(norm.xn_done, s + 1)
                    eng.tensor_tensor(k.x[:, s, :, :], k.x[:, s, :, :],
                                      gate_b2[:, p, :].unsqueeze(1).to_broadcast([P, T, D]), ALU.add).then_inc(pre_done, 1)

                one_ahead(eng, body)

            @block.tensor
            def _(eng):
                norm.tensor_turn(eng, ps_h, 0, 0)

                def body(s, nxt, p):
                    eng.wait_ge(hi_done, s + 1)
                    eng.wait_ge(lo_done, s + 1)
                    for q in range(Q1):
                        eng.matmul(ps_up[q][:, :], w.sign1T[:, q, :], h_hi[:, p, :], start=True, stop=False)
                        eng.matmul(ps_up[q][:, :], w.sign1T[:, q, :], h_lo[:, p, :], start=False, stop=True).then_inc(up_done, 1)
                    for q in range(Q1):
                        eng.wait_ge(gelu_done, s * Q1 + q + 1)
                        for t in range(T):
                            last = eng.matmul(ps_y[p][:, t * P:(t + 1) * P], hidden[:, p, q, t * P:(t + 1) * P], w.sign2T[:, q, :],
                                              start=(q == 0 and t == 0), stop=(q == Q1 - 1), skip_group_check=True)
                        if q == 0 and nxt is not None:
                            norm.tensor_turn(eng, ps_h, nxt, 1 - p)
                    last.then_inc(y_done, 1)

                one_ahead(eng, body)

            @block.scalar
            def _(eng):
                def modulate(s, p):
                    norm.scalar_modulate(eng, ps_h, hT[:, p, :], s).then_inc(h_done, 1)
                    eng.wait_ge(h_done, s + 1)
                    eng.activation(h_hi[:, p, :], hT[:, p, :], ACT.Copy).then_inc(hi_done, 1)

                modulate(0, 0)

                def body(s, nxt, p):
                    for q in range(Q1):
                        eng.wait_ge(up_done, s * Q1 + q + 1)
                        eng.activation(hidden[:, p, q, :], ps_up[q][:, :], ACT.Gelu, scale=w.alpha1[:, q:q + 1],
                                       bias=w.b1[:, q:q + 1]).then_inc(gelu_done, 1)
                    if nxt is not None:
                        modulate(nxt, 1 - p)

                one_ahead(eng, body)

            @block.vector
            def _(eng):
                def low(s, p):
                    eng.wait_ge(hi_done, s + 1)
                    eng.tensor_tensor(h_lo[:, p, :], hT[:, p, :], h_hi[:, p, :].bitcast(F32), ALU.subtract).then_inc(lo_done, 1)

                norm.vector_stats(eng, 0, 0)
                norm.vector_normalise(eng, 0, 0)
                low(0, 0)

                def body(s, nxt, p):
                    if nxt is not None:
                        norm.vector_stats(eng, nxt, 1 - p)
                        norm.vector_normalise(eng, nxt, 1 - p)
                        low(nxt, 1 - p)
                    eng.wait_ge(y_done, s + 1)
                    eng.wait_ge(gates_done, s + 1)
                    eng.tensor_tensor(scaled[:, p, :].rearrange("p (t d) -> p t d", t=T), ps_y[p][:, :].rearrange("p (t d) -> p t d", t=T),
                                      gate_alpha[:, p, :].unsqueeze(1).to_broadcast([P, T, D]), ALU.mult).then_inc(scaled_done, 1)
                    eng.wait_ge(scaled_done, s + 1)
                    eng.wait_ge(pre_done, s + 1)
                    xs = k.x[:, s, :, :].rearrange("p t d -> p (t d)")
                    eng.tensor_tensor(xs, scaled[:, p, :], xs, ALU.add).then_inc(x_done, 1)

                one_ahead(eng, body)


class Kept:

    def __init__(self, nc, m):
        self.x = m.sb("x", [P, B, T, D])
        self.ident = m.sb("ident", [P, P])
        self.spread = m.sb("spread", [P, 4, G0, P], F32R)
        self.mods = m.sb("mods", [P, 2, 4, B])
        self.gates = m.sb("gates", [P, B, 4, D])
        self.passed = m.sem("passed")
        self.scratch = nc.dram_tensor("gate_scratch", [B, 4 * D], F32, kind="Internal").ap()


def two_blocks(nc, a, out):
    with ExitStack() as stack:
        m = Memory(nc, stack)
        k = Kept(nc, m)
        prepare(nc, a, k)
        linear_attention(nc, a, k)
        with ExitStack() as moe_stack:
            r = Router(Memory(nc, moe_stack))
            routing(nc, a, k, r)
            expert_layers(nc, a, k, r)
        with ExitStack() as latent_stack:
            w = Latent(Memory(nc, latent_stack))
            fold_latent(nc, a, k, w)
            latent_attention(nc, a, k, w)
        with ExitStack() as binary_stack:
            w = Binary(Memory(nc, binary_stack))
            binarise(nc, a, k, w)
            feed_forward(nc, a, k, w, out)


def shape_constants():
    c = np.arange(P)
    inv_freq = (1.0 / 10000.0 ** (np.arange(0, HD0, 2, dtype=np.float32) / HD0)).astype(np.float32)
    angle = np.arange(N, dtype=np.float32)[None, :] * inv_freq[c % (HD0 // 2)][:, None]
    sign = np.where(c % HD0 < HD0 // 2, -1.0, 1.0).astype(np.float32)[:, None]
    spread = np.zeros((P, 4, G0, P), np.float32)
    for g in range(G0):
        for quadrant in range(4):
            rows, cols = 32 * g + np.arange(32), 32 * quadrant + np.arange(32)
            spread[rows, 0 if quadrant % 2 == 0 else 1, g, cols] = 1.0
            spread[rows, 2 if quadrant < 2 else 3, g, cols] = 1.0
    f = np.float32
    pick = np.zeros((64, DYN_UNITS + 1, P), f)
    for u in range(DYN_UNITS + 1):
        expert = np.where(u < DYN_UNITS, 2 * u + c // I_DYN, E_DYN)
        pick[expert, u, c] = pick[32 + expert, u, c] = 1.0
    place = np.zeros((DC + 1, P), f)
    for copy in range(3):
        place[np.arange(DC), copy * DC + np.arange(DC)] = 1.0
    place[DC, 3 * DC:3 * DC + 2] = 1.0
    column = lambda mask: np.where(mask, -1.0, 0.0).astype(f)[:, None]
    return {
        "place": place, "low_w": column(((c >= 2 * DC) & (c < 3 * DC)) | (c == 3 * DC + 1)),
        "q_low": column((c >= DC) & (c < 2 * DC)), "upper_low": column(c >= DKV),
        "experts": np.tile(np.arange(E_DYN, dtype=f), (P, 1)),
        "pick": pick.reshape(64, -1), "low_rows": np.where(np.arange(64) < 32, 0.0, -1.0).astype(f)[:, None],
        "ident": np.eye(P, dtype=f),
        "cos": np.cos(angle).astype(f), "sin": (np.sin(angle) * sign).astype(f),
        "causal": (c[:, None] <= c[None, :]).astype(f),
        "own_head": (c[:, None] // HD0 == c[None, :] // HD0).astype(f),
        "head_rows": ((c[:, None] % 32) // HD0 == np.arange(J0)[None, :]).astype(f),
        "spread": spread.reshape(P, -1),
    }


_INS = ["L0_attn_x", "L0_attn_Wq", "L0_attn_Wk", "L0_attn_Wv", "L0_attn_Wo", "L0_attn_Wg1", "L0_attn_Wg2", "L0_attn_ln_w",
        "L0_attn_ln_b", "L0_ffn_gate_w", "L0_ffn_dyn_gate_w", "L0_ffn_dyn_up_w", "L0_ffn_dyn_down_w", "L0_ffn_sh_gate_w",
        "L0_ffn_sh_up_w", "L0_ffn_sh_down_w", "L0_c", "L0_wmod", "L1_attn_W_DQ", "L1_attn_b_DQ", "L1_attn_W_UQ",
        "L1_attn_b_UQ", "L1_attn_W_DKV", "L1_attn_b_DKV", "L1_attn_W_UK", "L1_attn_b_UK", "L1_attn_W_UV", "L1_attn_b_UV",
        "L1_attn_W_QR", "L1_attn_b_QR", "L1_attn_W_KR", "L1_attn_b_KR", "L1_attn_W_O", "L1_attn_b_O", "L1_ffn_w1",
        "L1_ffn_b1", "L1_ffn_w2", "L1_ffn_b2", "L1_c", "L1_wmod"]


def kernel(**inputs):
    import concourse.bacc as _bacc
    from concourse.bass_utils import run_bass_kernel_spmd as _run

    nc = _bacc.Bacc("TRN2", target_bir_lowering=False, num_devices=1)
    arrays, args = {}, {}
    tables = shape_constants()
    for name in [*_INS, *tables]:
        array = np.ascontiguousarray(tables[name] if name in tables else inputs[name])
        arrays[f"in_{name}_dram"] = array
        args[name] = nc.dram_tensor(f"in_{name}_dram", array.shape, mybir.dt.from_np(array.dtype), kind="ExternalInput").ap()
    out = nc.dram_tensor("out_0_dram", (B, N, D), F32, kind="ExternalOutput").ap()
    two_blocks(nc, args, out)
    result = _run(nc, [arrays], core_ids=[0])
    return result.results[0]["out_0_dram"]
```

```python
from contextlib import ExitStack

import numpy as np

import concourse.bass as bass
from concourse import mybir

F32 = mybir.dt.float32
F32R = mybir.dt.float32r
ALU = mybir.AluOpType
ACT = mybir.ActivationFunctionType
AX = mybir.AxisListType

P = 128
B, N, D = 8, 512, 128
T = N // P
HEADS0, HD0 = 16, 8
G0, J0 = 4, 4
EPS = 1e-5
SA, CA, SB, CB = range(4)


def steps(eng, step, late):
    step(0, 1, None, 0)
    with eng.Fori(0, (B - 2) // 2) as i:
        step(2 * i + 1, 2 * i + 2, 2 * i, 1)
        step(2 * i + 2, 2 * i + 3, 2 * i + 1, 0)
    step(B - 1, None, B - 2, 1)
    late(B - 1)


def apart(eng, passed):
    eng.sem_inc(passed, 1)


class Memory:

    def __init__(self, nc, stack):
        self.nc, self.stack = nc, stack

    def sb(self, name, shape, dt=F32):
        return self.stack.enter_context(self.nc.sbuf_tensor(name, shape, dt))

    def ps(self, name):
        return self.stack.enter_context(self.nc.psum_tensor(name, [P, 512], F32))

    def sem(self, name):
        handle = self.nc.alloc_semaphore(name=name)

        def give_back():
            self.nc.gpsimd.sem_clear(handle)
            self.nc.release_semaphore(handle)

        self.stack.callback(give_back)
        return handle


class Linear:

    def __init__(self, m):
        self.wq, self.wk, self.wv, self.wo = (m.sb(n, [P, D]) for n in ("wq", "wk", "wv", "wo"))
        self.wg1, self.wg2 = m.sb("wg1", [P, 8]), m.sb("wg2", [8, D])
        self.lnw, self.lnb = m.sb("lnw", [P, 1]), m.sb("lnb", [P, 1])
        self.cos, self.sin = m.sb("cos", [P, N]), m.sb("sin", [P, N])
        self.causal, self.own_head = m.sb("causal", [P, P]), m.sb("own_head", [P, P])
        self.head_rows = m.sb("head_rows", [P, J0])
        self.spread = m.sb("spread", [P, 4, G0, P], F32R)
        self.minus_half = m.sb("minus_half", [P, T])
        self.v_heads = m.sb("v_heads", [P, 2, T, J0, D])
        self.w_in, self.x_in = m.sem("w_in"), m.sem("x_in")
        self.W_IN = 13 * 16

    def load(self, eng, a):
        for dst, name in ((self.wq, "L0_attn_Wq"), (self.wk, "L0_attn_Wk"), (self.wv, "L0_attn_Wv"), (self.wo, "L0_attn_Wo"),
                          (self.wg1, "L0_attn_Wg1"), (self.wg2, "L0_attn_Wg2"), (self.cos, "cos"), (self.sin, "sin"),
                          (self.causal, "causal"), (self.own_head, "own_head"), (self.head_rows, "head_rows")):
            eng.dma_start(dst[:, :], a[name]).then_inc(self.w_in, 16)
        for dst, name in ((self.lnw, "L0_attn_ln_w"), (self.lnb, "L0_attn_ln_b")):
            eng.dma_start(dst[:, :], a[name].rearrange("(d o) -> d o", o=1)).then_inc(self.w_in, 16)

    def load_x(self, eng, a, k, s):
        eng.dma_start(k.x[:, s, :, :], a["L0_attn_x"][s, :, :].rearrange("(t p) d -> p t d", p=P)).then_inc(self.x_in, 16)


def prepare(nc, a, k, w):
    with ExitStack() as stack:
        m = Memory(nc, stack)
        c_rows = m.sb("c_rows", [B, 2, D])
        cT = m.sb("cT", [P, 2, B])
        silu_cT = m.sb("silu_cT", [P, 2, B])
        wmod = m.sb("wmod", [P, 2, 6 * D])
        gate_raw = m.sb("gate_raw", [B, 4, D])
        gate_sign = m.sb("gate_sign", [B, 4, D])
        gate_neg = m.sb("gate_neg", [B, 4, D])
        gate_abs = m.sb("gate_abs", [B, 4, D])
        gate_rows = m.sb("gate_rows", [B, 4, D])
        spread_raw = m.sb("spread_raw", [P, 4, G0, P])
        spread_in = m.sem("spread_in")
        ps_c, ps_col, ps_row = m.ps("ps_c"), m.ps("ps_col"), m.ps("ps_row")
        ident_in, c_in, wmod_in = m.sem("ident_in"), m.sem("c_in"), m.sem("wmod_in")
        c_turned, c_copied, silu_done = m.sem("c_turned"), m.sem("c_copied"), m.sem("silu_done")
        cols_done, rows_done = m.sem("cols_done"), m.sem("rows_done")
        step, rows_ready = m.sem("gate_step"), m.sem("rows_ready")
        rows_stored = m.sem("rows_stored")
        with nc.Block() as block:

            @block.sync
            def _(eng):
                eng.dma_start(k.ident[:, :], a["ident"]).then_inc(ident_in, 16)
                for l in range(2):
                    eng.dma_start(c_rows[:, l, :], a[f"L{l}_c"]).then_inc(c_in, 16)
                for l in range(2):
                    eng.dma_start(wmod[:, l, :], a[f"L{l}_wmod"]).then_inc(wmod_in, 16)
                eng.dma_start(spread_raw[:, :, :, :].rearrange("p a g n -> p (a g n)"), a["spread"]).then_inc(spread_in, 16)
                w.load_x(eng, a, k, 0)
                w.load(eng, a)
                eng.wait_ge(rows_ready, 1)
                eng.dma_start(k.scratch, gate_rows[:, :, :].rearrange("b k d -> b (k d)")).then_inc(rows_stored, 16)
                eng.wait_ge(rows_stored, 16)
                eng.dma_start(k.gates[:, :, :, :].rearrange("p b k d -> p (b k d)"),
                              k.scratch.rearrange("b n -> (b n)").partition_broadcast(P)).then_inc(k.gates_in, 16)

            @block.gpsimd
            def _(eng):
                eng.memset(w.minus_half[:, :], -0.5)
                eng.memset(w.v_heads[:, :, :, :, :].rearrange("p a t j d -> p (a t j d)"), 0.0)

            @block.tensor
            def _(eng):
                eng.wait_ge(ident_in, 16)
                eng.wait_ge(c_in, 32)
                for l in range(2):
                    last = eng.transpose(ps_c[:, B * l:B * l + B], c_rows[:, l, :], k.ident[0:B, 0:B])
                last.then_inc(c_turned, 1)
                eng.wait_ge(silu_done, 1)
                eng.wait_ge(wmod_in, 32)
                for l in range(2):
                    for n, chunk in enumerate((0, 1, 3, 4)):
                        at = (4 * l + n) * B
                        last = eng.matmul(ps_col[:, at:at + B], wmod[:, l, chunk * D:(chunk + 1) * D],
                                          silu_cT[:, l, :], start=True, stop=True)
                last.then_inc(cols_done, 1)
                for l in range(2):
                    for n, chunk in enumerate((2, 5)):
                        at = (2 * l + n) * D
                        last = eng.matmul(ps_row[0:B, at:at + D], silu_cT[:, l, :],
                                          wmod[:, l, chunk * D:(chunk + 1) * D], start=True, stop=True)
                last.then_inc(rows_done, 1)

            @block.scalar
            def _(eng):
                eng.wait_ge(c_turned, 1)
                eng.activation(silu_cT[:, :, :].rearrange("p l b -> p (l b)"), ps_c[:, 0:2 * B], ACT.Silu).then_inc(silu_done, 1)

            @block.vector
            def _(eng):
                cols = ps_col[:, 0:8 * B].rearrange("p (l c b) -> p l c b", l=2, c=4)
                eng.wait_ge(cols_done, 1)
                for n, plus in ((SA, 0.0), (CA, 1.0), (SB, 0.0), (CB, 1.0)):
                    eng.tensor_scalar(k.mods[:, :, n, :], cols[:, :, n, :], plus, None, ALU.add)
                eng.wait_ge(rows_done, 1)
                rows = ps_row[0:B, :].rearrange("b (k d) -> b k d", k=4)
                eng.tensor_scalar(gate_sign[:, :, :], rows, 0.0, 2.0, ALU.is_ge, ALU.mult)
                eng.tensor_scalar(gate_neg[:, :, :], rows, -1.0, None, ALU.mult).then_inc(step, 1)
                eng.wait_ge(step, 1)
                eng.scalar_tensor_tensor(gate_abs[:, :, :], rows, 0.25, gate_neg[:, :, :], ALU.max, ALU.max).then_inc(step, 1)
                eng.wait_ge(step, 2)
                eng.scalar_tensor_tensor(gate_rows[:, :, :], gate_sign[:, :, :], -1.0, gate_abs[:, :, :],
                                         ALU.add, ALU.mult).then_inc(rows_ready, 1)
                eng.wait_ge(spread_in, 16)
                eng.tensor_copy(w.spread[:, :, :, :], spread_raw[:, :, :, :])


def layer_norm_stats(eng, rows, stats, moments, stats_done, moments_done, passed, s):
    for t in range(T):
        last = eng.bn_stats(stats[:, t, :], rows(t))
    last.then_inc(stats_done, 1)
    eng.wait_ge(stats_done, s + 1)
    apart(eng, passed)
    for t in range(T):
        last = eng.bn_aggr(moments[:, t, :], stats[:, t, :])
    last.then_inc(moments_done, 1)


def linear_attention(nc, a, k, w):
    with ExitStack() as stack:
        m = Memory(nc, stack)
        wq, wk, wv, wo, wg1, wg2, lnw, lnb = w.wq, w.wk, w.wv, w.wo, w.wg1, w.wg2, w.lnw, w.lnb
        cos, sin, causal, own_head, head_rows, spread = w.cos, w.sin, w.causal, w.own_head, w.head_rows, w.spread
        minus_half, v_heads, w_in, x_in, W_IN = w.minus_half, w.v_heads, w.w_in, w.x_in, w.W_IN
        wq_rot, wk_rot = m.sb("wq_rot", [P, D]), m.sb("wk_rot", [P, D])
        wg1T, wg = m.sb("wg1T", [8, P]), m.sb("wg", [P, D])
        stats, moments = m.sb("stats", [P, T, 6]), m.sb("moments", [P, T, 2])
        var_eps, rstd = m.sb("var_eps", [P, T]), m.sb("rstd", [P, T])
        xn, hT = m.sb("xn", [P, T, D]), m.sb("hT", [P, N])
        act = {n: m.sb("act_" + n, [P, N]) for n in ("q", "q_rot", "k", "k_rot")}
        qr = [m.sb(f"qr{p}", [P, N]) for p in (0, 1)]
        kr = m.sb("kr", [P, N])
        hi = {n: m.sb("hi_" + n, [P, N], F32R) for n in "qk"}
        lo = {n: m.sb("lo_" + n, [P, N], F32R) for n in "qk"}
        q_stack = m.sb("q_stack", [P, G0, N])
        q_heads = m.sb("q_heads", [P, 2, G0, J0, N // 1], F32R)
        k_stack = m.sb("k_stack", [P, 2, G0, N], F32R)
        k_tok, v_tok = m.sb("k_tok", [P, 2, T, D]), m.sb("v_tok", [P, 2, T, D])
        gate = m.sb("gate", [P, 2, N])
        masked = m.sb("masked", [P, 4, 4 * P])
        state = m.sb("state", [P, D])
        gated = m.sb("gated", [P, N])
        stats2, moments2 = m.sb("stats2", [P, T, 6]), m.sb("moments2", [P, T, 2])
        var_eps2, rstd2, shift2 = m.sb("var_eps2", [P, T]), m.sb("rstd2", [P, T]), m.sb("shift2", [P, T])
        on, oT, wo_g = m.sb("on", [P, T, D]), m.sb("oT", [P, N]), m.sb("wo_g", [P, D])
        ps_t, ps_e, ps_o, ps_s, ps_y = m.ps("ps_t"), [m.ps("ps_e0"), m.ps("ps_e1")], m.ps("ps_o"), m.ps("ps_s"), m.ps("ps_y")
        ps_p = [m.ps("ps_p0"), m.ps("ps_p1")]
        S = m.sem
        wg_t, wg_c, wg_m, w_ready = S("wg_t"), S("wg_c"), S("wg_m"), S("w_ready")
        stats_done, moments_done, ve_done, rstd_done = S("stats_done"), S("moments_done"), S("ve_done"), S("rstd_done")
        xn_done, turned, hT_done, kT_turned, k_tok_done = S("xn_done"), S("turned"), S("hT_done"), S("kT_turned"), S("k_tok_done")
        filled, emptied = [S("filled0"), S("filled1")], [S("emptied0"), S("emptied1")]
        cos_done, sin_done, rot_done, hi_done, lo_done = S("cos_done"), S("sin_done"), S("rot_done"), S("hi_done"), S("lo_done")
        q_heads_v, q_heads_a, v_heads_done = S("q_heads_v"), S("q_heads_a"), S("v_heads_done")
        energy_done, masked_done, av_done = S("energy_done"), S("masked_done"), S("av_done")
        state_sum, state_done, o_done, gated_done = S("state_sum"), S("state_done"), S("o_done"), S("gated_done")
        o_turned, stats2_done, moments2_done, ve2_done, rstd2_done, shift2_done = (
            S("o_turned"), S("stats2_done"), S("moments2_done"), S("ve2_done"), S("rstd2_done"), S("shift2_done"))
        on_done, on_turned, oT_done, wo_g_done, y_done, x_done = (
            S("on_done"), S("on_turned"), S("oT_done"), S("wo_g_done"), S("y_done"), S("x_done"))
        USES = (6 + 2 * G0) // 2
        Q, Q_ROT, K, K_ROT, V, GATE, QS, KS = 0, 1, 2, 3, 4, 5, 6, 6 + G0

        def nth(n, s):
            return s * USES + n // 2 + 1

        with nc.Block() as block:

            @block.sync
            def _(eng):
                with eng.Fori(1, B) as s:
                    eng.wait_ge(x_in, s * 16)
                    w.load_x(eng, a, k, s)

            @block.gpsimd
            def _(eng):
                eng.wait_ge(w_in, W_IN)

                def norm_rstd(s):
                    eng.wait_ge(moments_done, s + 1)
                    apart(eng, k.passed)
                    eng.tensor_scalar(var_eps[:, :], moments[:, :, 1], EPS, None, ALU.add).then_inc(ve_done, 1)
                    eng.wait_ge(ve_done, s + 1)
                    eng.tensor_tensor(rstd[:, :], var_eps[:, :], minus_half[:, :], ALU.pow).then_inc(rstd_done, 1)

                def front(s, p):
                    norm_rstd(s)
                    for i, n in enumerate("qk"):
                        bank = 2 * i
                        eng.wait_ge(emptied[0], nth(bank, s))
                        eng.tensor_tensor(act[n][:, :], act[n][:, :], cos[:, :], ALU.mult).then_inc(cos_done, 1)
                    for i, n in enumerate("qk"):
                        eng.wait_ge(hi_done, 2 * s + i + 1)
                        rot = qr[p] if n == "q" else kr
                        eng.tensor_tensor(lo[n][:, :], rot[:, :], hi[n][:, :].bitcast(F32), ALU.subtract).then_inc(lo_done, 1)
                    eng.wait_ge(emptied[0], nth(V, s))
                    apart(eng, k.passed)
                    for j in range(J0):
                        cols = lambda t: t.rearrange("p t (g j c) -> p t g j c", g=G0, j=J0)[:, :, :, j, :]
                        last = eng.tensor_copy(cols(v_heads[:, p, :, j, :]), cols(v_tok[:, p, :, :]))
                    last.then_inc(v_heads_done, 1)

                def step(s, front_of, late_of, p):
                    if front_of is not None:
                        front(front_of, 1 - p)
                    eng.wait_ge(y_done, s)
                    eng.tensor_tensor(wo_g[:, :], wo[:, :], k.gates[:, s, 0, :], ALU.mult).then_inc(wo_g_done, 1)
                    eng.wait_ge(moments2_done, s + 1)
                    apart(eng, k.passed)
                    eng.tensor_scalar(var_eps2[:, :], moments2[:, :, 1], 4 * EPS, None, ALU.add).then_inc(ve2_done, 1)
                    eng.wait_ge(ve2_done, s + 1)
                    eng.tensor_tensor(rstd2[:, :], var_eps2[:, :], minus_half[:, :], ALU.pow).then_inc(rstd2_done, 1)

                front(0, 0)
                eng.wait_ge(k.gates_in, 16)
                steps(eng, step, lambda s: None)

            @block.tensor
            def _(eng):
                eng.wait_ge(w_in, W_IN)
                eng.transpose(ps_t[0:8, 0:P], wg1[:, :], k.ident[:, :]).then_inc(wg_t, 1)
                eng.wait_ge(wg_c, 1)
                eng.matmul(ps_t[:, 0:D], wg1T[:, :], wg2[:, :], start=True, stop=True).then_inc(wg_m, 1)
                eng.wait_ge(w_ready, 2)

                def turn(s):
                    eng.wait_ge(xn_done, s + 1)
                    eng.wait_ge(k_tok_done, s)
                    for t in range(T):
                        last = eng.transpose(ps_t[:, t * P:(t + 1) * P], xn[:, t, :], k.ident[:, :])
                    last.then_inc(turned, 1)

                def project(s, n):
                    eng.wait_ge(hT_done, s + 1)
                    eng.wait_ge(emptied[n % 2], s * USES + n // 2)
                    if n == V:
                        for t in range(T):
                            last = eng.matmul(ps_p[0][:, t * P:(t + 1) * P], hT[:, t * P:(t + 1) * P], wv[:, :], start=True, stop=True)
                    else:
                        last = eng.matmul(ps_p[n % 2][:, :], {Q: wq, Q_ROT: wq_rot, K: wk, K_ROT: wk_rot, GATE: wg}[n][:, :], hT[:, :],
                                          start=True, stop=True)
                    last.then_inc(filled[n % 2], 1)

                def spread_parts(s, i):
                    name, first = (("q", QS), ("k", KS))[i]
                    eng.wait_ge(lo_done, 2 * s + i + 1)
                    for g in range(G0):
                        n = first + g
                        eng.wait_ge(emptied[n % 2], s * USES + n // 2)
                        eng.matmul(ps_p[n % 2][:, :], spread[:, 2 * i, g, :], hi[name][:, :], start=True, stop=False)
                        eng.matmul(ps_p[n % 2][:, :], spread[:, 2 * i + 1, g, :], lo[name][:, :],
                                   start=False, stop=True).then_inc(filled[n % 2], 1)

                def turn_k(s):
                    for t in range(T):
                        last = eng.transpose(ps_t[:, t * P:(t + 1) * P], kr[:, t * P:(t + 1) * P], k.ident[:, :])
                    last.then_inc(kT_turned, 1)

                def energy(s, p, n):
                    c, g = divmod(n, G0)
                    if c == 0:
                        if g < 3:
                            eng.wait_ge(q_heads_v, 3 * s + g + 1)
                        else:
                            eng.wait_ge(q_heads_a, s + 1)
                        eng.wait_ge(emptied[(KS + g) % 2], nth(KS + g, s))
                    eng.wait_ge(masked_done, s * 16 + max(n - 1, 0))
                    eng.matmul(ps_e[n % 2][:, :], k_stack[:, p, g, c * P:(c + 1) * P],
                               q_heads[:, p, g, :, c * P:(c + 1) * P],
                               start=True, stop=True).then_inc(energy_done, 1)

                def values(s, p, n):
                    c, g = divmod(n, G0)
                    out = slice(c * P, (c + 1) * P)
                    if n == 0:
                        eng.wait_ge(gated_done, s)
                        eng.wait_ge(v_heads_done, s + 1)
                        eng.wait_ge(k_tok_done, s + 1)
                    if g == 0 and c > 0:
                        eng.wait_ge(state_done, s * 3 + c)
                        eng.matmul(ps_o[:, out], state[:, :], qr[p][:, out], start=True, stop=False,
                                   skip_group_check=True)
                    if g == 0 and c < T - 1:
                        eng.wait_ge(state_done, s * 3 + c)
                        eng.matmul(ps_s[:, 0:D], k_tok[:, p, c, :], v_tok[:, p, c, :], start=(c == 0),
                                   stop=(c == T - 2), skip_group_check=True).then_inc(state_sum, 1)
                    eng.wait_ge(masked_done, s * 16 + n + 1)
                    for j in range(J0):
                        last = eng.matmul(ps_o[32 * g:32 * g + 32, out], v_heads[:, p, c, j, 32 * g:32 * g + 32],
                                          masked[:, n % 4, j * P:(j + 1) * P], start=(c == 0 and j == 0),
                                          stop=(j == J0 - 1), skip_group_check=True)
                    last.then_inc(av_done, 1)

                def turn_gated(s):
                    eng.wait_ge(gated_done, s + 1)
                    eng.wait_ge(x_done, s)
                    for t in range(T):
                        last = eng.transpose(ps_y[:, t * P:(t + 1) * P], gated[:, t * P:(t + 1) * P], k.ident[:, :])
                    last.then_inc(o_turned, 1)

                def turn_normed(s):
                    eng.wait_ge(on_done, s + 1)
                    for t in range(T):
                        last = eng.transpose(ps_y[:, t * P:(t + 1) * P], on[:, t, :], k.ident[:, :])
                    last.then_inc(on_turned, 1)

                def product_out(s):
                    eng.wait_ge(oT_done, s + 1)
                    eng.wait_ge(wo_g_done, s + 1)
                    for t in range(T):
                        last = eng.matmul(ps_y[:, t * P:(t + 1) * P], oT[:, t * P:(t + 1) * P], wo_g[:, :],
                                          start=True, stop=True)
                    last.then_inc(y_done, 1)

                def step(s, front, late, p):
                    energy(s, p, 0)
                    energy(s, p, 1)
                    for n in range(16):
                        if n < 2:
                            values(s, p, n)
                        if n + 2 < 16:
                            energy(s, p, n + 2)
                        if n >= 2:
                            values(s, p, n)
                        if late is not None and n == 4:
                            turn_normed(late)
                        if late is not None and n == 6:
                            product_out(late)
                        if front is not None and n == 5:
                            turn(front)
                        if front is not None and 7 <= n < 13:
                            project(front, n - 7)
                    if front is not None:
                        spread_parts(front, 0)
                    turn_gated(s)
                    if front is not None:
                        spread_parts(front, 1)
                        turn_k(front)

                def late(s):
                    turn_normed(s)
                    product_out(s)

                turn(0)
                for n in range(6):
                    project(0, n)
                spread_parts(0, 0)
                spread_parts(0, 1)
                turn_k(0)
                steps(eng, step, late)

            @block.scalar
            def _(eng):
                eng.wait_ge(wg_t, 1)
                eng.activation(wg1T[:, :], ps_t[0:8, 0:P], ACT.Copy).then_inc(wg_c, 1)
                eng.wait_ge(wg_m, 1)
                eng.activation(wg[:, :], ps_t[:, 0:D], ACT.Copy).then_inc(w_ready, 1)

                def front(s, p):
                    eng.wait_ge(turned, s + 1)
                    eng.wait_ge(filled[1], s * USES)
                    eng.activation(hT[:, :], ps_t[:, :], ACT.Identity,
                                   scale=k.mods[:, 0, CA, bass.ds(s, 1)], bias=k.mods[:, 0, SA, bass.ds(s, 1)]).then_inc(hT_done, 1)

                    def split(i):
                        eng.wait_ge(rot_done, 2 * s + i + 1)
                        rot = (qr[p], kr)[i]
                        eng.activation(hi["qk"[i]][:, :], rot[:, :], ACT.Copy).then_inc(hi_done, 1)

                    for n, name in enumerate(("q", "q_rot", "k", "k_rot")):
                        eng.wait_ge(filled[n % 2], nth(n, s))
                        eng.wait_ge(rot_done, 2 * s)
                        eng.activation(act[name][:, :], ps_p[n % 2][:, :], ACT.Silu).then_inc(emptied[n % 2], 1)
                    eng.wait_ge(filled[0], nth(V, s))
                    eng.activation(v_tok[:, p, :, :].rearrange("p t d -> p (t d)"), ps_p[0][:, :], ACT.Copy).then_inc(emptied[0], 1)
                    split(0)
                    eng.wait_ge(filled[1], nth(GATE, s))
                    eng.activation(gate[:, p, :], ps_p[1][:, :], ACT.Tanh, scale=0.5).then_inc(emptied[1], 1)
                    split(1)
                    eng.wait_ge(q_heads_v, 3 * s)
                    for g in range(G0):
                        n = QS + g
                        eng.wait_ge(filled[n % 2], nth(n, s))
                        if g == 3:
                            eng.wait_ge(q_heads_a, s)
                        eng.activation(q_stack[:, g, :], ps_p[n % 2][:, :], ACT.Copy).then_inc(emptied[n % 2], 1)
                    for g in range(G0):
                        n = KS + g
                        eng.wait_ge(filled[n % 2], nth(n, s))
                        eng.activation(k_stack[:, p, g, :], ps_p[n % 2][:, :], ACT.Copy).then_inc(emptied[n % 2], 1)
                    eng.wait_ge(kT_turned, s + 1)
                    eng.activation(k_tok[:, p, :, :].rearrange("p t d -> p (t d)"), ps_t[:, :], ACT.Copy).then_inc(k_tok_done, 1)
                    eng.wait_ge(emptied[1], nth(QS + 3, s))
                    eng.wait_ge(emptied[1], nth(QS + 3, s))
                    for j in range(J0):
                        last = eng.activation(q_heads[:, p, 3, j, :], q_stack[:, 3, :], ACT.Copy, scale=head_rows[:, j:j + 1])
                    last.then_inc(q_heads_a, 1)

                def late(s):
                    eng.wait_ge(shift2_done, s + 1)
                    eng.wait_ge(rstd2_done, s + 1)
                    for t in range(T):
                        last = eng.activation(on[:, t, :], ps_y[:, t * P:(t + 1) * P], ACT.Identity,
                                              scale=rstd2[:, t:t + 1], bias=shift2[:, t:t + 1])
                    last.then_inc(on_done, 1)
                    eng.wait_ge(on_turned, s + 1)
                    eng.activation(oT[:, :], ps_y[:, :], ACT.Identity, scale=lnw[:, :], bias=lnb[:, :]).then_inc(oT_done, 1)

                def step(s, front_of, late_of, p):
                    if late_of is not None:
                        late(late_of)
                    if front_of is not None:
                        front(front_of, 1 - p)

                front(0, 0)
                steps(eng, step, late)

            @block.vector
            def _(eng):
                eng.wait_ge(w_in, W_IN)
                for src, rot in ((wq, wq_rot), (wk, wk_rot)):
                    for half in (0, 1):
                        of = lambda t, h: t[:, :].rearrange("p (n h r) -> p n h r", h=2, r=4)[:, :, h, :]
                        last = eng.tensor_copy(of(rot, half), of(src, 1 - half))
                last.then_inc(w_ready, 1)

                def norm_stats(s):
                    eng.wait_ge(x_in, s * 16 + 16)
                    layer_norm_stats(eng, lambda t: k.x[:, s, t, :], stats, moments, stats_done, moments_done, k.passed, s)

                def normalise(s):
                    eng.wait_ge(rstd_done, s + 1)
                    eng.wait_ge(turned, s)
                    for t in range(T):
                        last = eng.tensor_scalar(xn[:, t, :], k.x[:, s, t, :], moments[:, t, 0:1], rstd[:, t:t + 1],
                                                 ALU.subtract, ALU.mult)
                    last.then_inc(xn_done, 1)

                def times_sine(s, i):
                    name = "qk"[i]
                    eng.wait_ge(emptied[1], nth(2 * i + 1, s))
                    eng.tensor_tensor(act[name + "_rot"][:, :], act[name + "_rot"][:, :], sin[:, :], ALU.mult).then_inc(sin_done, 1)

                def rotate(s, p, i):
                    name = "qk"[i]
                    eng.wait_ge(sin_done, 2 * s + i + 1)
                    eng.wait_ge(cos_done, 2 * s + i + 1)
                    if name == "k":
                        eng.wait_ge(kT_turned, s)
                        eng.wait_ge(lo_done, 2 * s)
                    rot = qr[p] if name == "q" else kr
                    eng.tensor_tensor(rot[:, :], act[name][:, :], act[name + "_rot"][:, :], ALU.add).then_inc(rot_done, 1)

                def split_heads(s, p):
                    for g in range(3):
                        eng.wait_ge(emptied[g % 2], nth(QS + g, s))
                        for j in range(J0):
                            last = eng.tensor_scalar(q_heads[:, p, g, j, :], q_stack[:, g, :], head_rows[:, j:j + 1],
                                                     None, ALU.mult)
                        last.then_inc(q_heads_v, 1)

                def mask(s, n):
                    c, g = divmod(n, G0)
                    eng.wait_ge(energy_done, s * 16 + n + 1)
                    if n >= 4:
                        eng.wait_ge(av_done, s * 16 + n - 3)
                    eng.tensor_tensor(masked[:, n % 4, :].rearrange("p (j n) -> p j n", j=J0),
                                      ps_e[n % 2][:, :].rearrange("p (j n) -> p j n", j=J0),
                                      causal[:, :].unsqueeze(1).to_broadcast([P, J0, P]), ALU.mult).then_inc(masked_done, 1)
                    if g == 1 and c < T - 1:
                        eng.wait_ge(state_sum, s * 3 + c + 1)
                        eng.tensor_tensor(state[:, :], ps_s[:, 0:D], own_head[:, :], ALU.mult).then_inc(state_done, 1)

                def gate_out(s, p):
                    eng.wait_ge(av_done, s * 16 + 16)
                    eng.wait_ge(o_turned, s)
                    eng.scalar_tensor_tensor(gated[:, :], gate[:, p, :], 1.0, ps_o[:, :], ALU.add, ALU.mult).then_inc(gated_done, 1)

                def late_shift(s):
                    eng.wait_ge(rstd2_done, s + 1)
                    eng.scalar_tensor_tensor(shift2[:, :], moments2[:, :, 0], -1.0, rstd2[:, :], ALU.mult, ALU.mult).then_inc(shift2_done, 1)

                def add_out(s):
                    eng.wait_ge(y_done, s + 1)
                    xs = k.x[:, s, :, :].rearrange("p t d -> p (t d)")
                    eng.tensor_tensor(xs, ps_y[:, :], xs, ALU.add).then_inc(x_done, 1)

                def step(s, front, late, p):
                    for n in range(16):
                        mask(s, n)
                        if late is not None and n == 0:
                            late_shift(late)
                        if front is not None and n == 1:
                            norm_stats(front)
                        if front is not None and n == 4:
                            normalise(front)
                        if late is not None and n == 8:
                            add_out(late)
                        if front is not None and n in (10, 13):
                            times_sine(front, n // 13)
                        if front is not None and n in (12, 15):
                            rotate(front, 1 - p, n // 15)
                    gate_out(s, p)
                    if front is not None:
                        split_heads(front, 1 - p)
                    eng.wait_ge(o_turned, s + 1)
                    layer_norm_stats(eng, lambda t: ps_y[:, t * P:(t + 1) * P], stats2, moments2, stats2_done, moments2_done, k.passed, s)

                def late(s):
                    late_shift(s)
                    add_out(s)

                norm_stats(0)
                normalise(0)
                for i in range(2):
                    times_sine(0, i)
                    rotate(0, 0, i)
                split_heads(0, 0)
                steps(eng, step, late)


def pairs_of(eng, body):
    body(0, 0)
    with eng.Fori(0, (B - 2) // 2) as i:
        body(2 * i + 1, 1)
        body(2 * i + 2, 0)
    body(B - 1, 1)


def one_ahead(eng, body):
    body(0, 1, 0)
    with eng.Fori(0, (B - 2) // 2) as i:
        body(2 * i + 1, 2 * i + 2, 1)
        body(2 * i + 2, 2 * i + 3, 0)
    body(B - 1, None, 1)


def neighbours(eng, body):
    body(0, 1, 0, None)
    with eng.Fori(0, (B - 2) // 2) as i:
        body(2 * i + 1, 2 * i + 2, 1, 2 * i)
        body(2 * i + 2, 2 * i + 3, 0, 2 * i + 1)
    body(B - 1, None, 1, B - 2)


class Norm:

    def __init__(self, m, k, layer, shift, scale):
        tag = f"n{layer}{shift}_"
        self.k, self.layer, self.shift, self.scale = k, layer, shift, scale
        self.stats, self.moments = m.sb(tag + "stats", [P, 2, T, 6]), m.sb(tag + "moments", [P, 2, T, 2])
        self.var_eps, self.rstd = m.sb(tag + "var_eps", [P, 2, T]), m.sb(tag + "rstd", [P, 2, T])
        self.minus_half = m.sb(tag + "minus_half", [P, T])
        self.xn = m.sb(tag + "xn", [P, 2, T, D])
        self.power_ready = m.sem(tag + "power_ready")
        self.stats_done, self.moments_done = m.sem(tag + "stats_done"), m.sem(tag + "moments_done")
        self.ve_done, self.rstd_done = m.sem(tag + "ve_done"), m.sem(tag + "rstd_done")
        self.xn_done, self.turned, self.h_done = m.sem(tag + "xn_done"), m.sem(tag + "turned"), m.sem(tag + "h_done")

    def pool_setup(self, eng):
        eng.memset(self.minus_half[:, :], -0.5).then_inc(self.power_ready, 1)
        eng.wait_ge(self.power_ready, 1)

    def pool_rstd(self, eng, s, p):
        eng.wait_ge(self.moments_done, s + 1)
        apart(eng, self.k.passed)
        eng.tensor_scalar(self.var_eps[:, p, :], self.moments[:, p, :, 1], EPS, None, ALU.add).then_inc(self.ve_done, 1)
        eng.wait_ge(self.ve_done, s + 1)
        eng.tensor_tensor(self.rstd[:, p, :], self.var_eps[:, p, :], self.minus_half[:, :], ALU.pow).then_inc(self.rstd_done, 1)

    def vector_stats(self, eng, s, p):
        for t in range(T):
            last = eng.bn_stats(self.stats[:, p, t, :], self.k.x[:, s, t, :])
        last.then_inc(self.stats_done, 1)
        eng.wait_ge(self.stats_done, s + 1)
        apart(eng, self.k.passed)
        for t in range(T):
            last = eng.bn_aggr(self.moments[:, p, t, :], self.stats[:, p, t, :])
        last.then_inc(self.moments_done, 1)

    def vector_normalise(self, eng, s, p):
        eng.wait_ge(self.rstd_done, s + 1)
        for t in range(T):
            last = eng.tensor_scalar(self.xn[:, p, t, :], self.k.x[:, s, t, :], self.moments[:, p, t, 0:1],
                                     self.rstd[:, p, t:t + 1], ALU.subtract, ALU.mult)
        last.then_inc(self.xn_done, 1)

    def tensor_turn(self, eng, bank, s, p):
        eng.wait_ge(self.xn_done, s + 1)
        for t in range(T):
            last = eng.transpose(bank[:, t * P:(t + 1) * P], self.xn[:, p, t, :], self.k.ident[:, :])
        last.then_inc(self.turned, 1)

    def scalar_modulate(self, eng, bank, out, s):
        eng.wait_ge(self.turned, s + 1)
        return eng.activation(out, bank[:, :], ACT.Identity,
                              scale=self.k.mods[:, self.layer, self.scale, bass.ds(s, 1)],
                              bias=self.k.mods[:, self.layer, self.shift, bass.ds(s, 1)])


E_DYN, I_DYN, I_FIX = 8, 64, 256
E_ALL = E_DYN + 1
TOP_K, TOP_P, JITTER = 4, 0.75, 0.1
TILES = B * T
CAPACITY = max(int(np.ceil(B * N / E_DYN * 1.25)), 4)
UNITS = (E_DYN * I_DYN + I_FIX) // P
DYN_UNITS = E_DYN * I_DYN // P


def routing(nc, a, k, r):
    with ExitStack() as stack:
        m = Memory(nc, stack)
        norm = Norm(m, k, 0, SB, CB)
        gate_rows, gateT = m.sb("r_gate_rows", [E_ALL, D]), m.sb("r_gateT", [P, E_ALL])
        hT = m.sb("r_hT", [P, 2, N])
        raw = {n: m.sb("r_raw_" + n, [P, UNITS, P]) for n in ("gate", "up", "down")}
        ps_t, ps_l, ps_w = [m.ps("r_ps_t0"), m.ps("r_ps_t1")], m.ps("r_ps_l"), [m.ps("r_ps_w0"), m.ps("r_ps_w1")]
        g_in, w_in, g_turned, g_done = m.sem("r_g_in"), m.sem("r_w_in"), m.sem("r_g_turned"), m.sem("r_g_done")
        w_turned, w_done, w_low = m.sem("r_w_turned"), m.sem("r_w_done"), m.sem("r_w_low")
        h_done, h_kept, logits_done = m.sem("r_h_done"), m.sem("r_h_kept"), m.sem("r_logits_done")
        logits = m.sb("r_logits", [P, TILES, E_ALL])
        batches = [(raw[n], dst, u, min(u + 4, UNITS)) for n, dst in (("gate", r.gate_hi), ("up", r.up_hi), ("down", r.down)) for u in (0, 4)]
        with nc.Block() as block:

            @block.sync
            def _(eng):
                eng.dma_start(gate_rows[:, :], a["L0_ffn_gate_w"]).then_inc(g_in, 16)
                for n in ("gate", "up"):
                    eng.dma_start(raw[n][:, 0:DYN_UNITS, :],
                                  a[f"L0_ffn_dyn_{n}_w"].rearrange("e i h -> (e i) h").rearrange("(u p) h -> p u h", p=P)).then_inc(w_in, 16)
                    eng.dma_start(raw[n][:, DYN_UNITS:UNITS, :],
                                  a[f"L0_ffn_sh_{n}_w"].rearrange("f i h -> (f i) h").rearrange("(u p) h -> p u h", p=P)).then_inc(w_in, 16)
                eng.dma_start(raw["down"][:, 0:DYN_UNITS, :].rearrange("p u i -> p (u i)").rearrange("p (e i) -> p e i", e=E_DYN),
                              a["L0_ffn_dyn_down_w"].rearrange("e h i -> h e i")).then_inc(w_in, 16)
                eng.dma_start(raw["down"][:, DYN_UNITS:UNITS, :].rearrange("p u i -> p (u i)"),
                              a["L0_ffn_sh_down_w"].rearrange("f h i -> (f h) i")).then_inc(w_in, 16)

            @block.gpsimd
            def _(eng):
                norm.pool_setup(eng)
                norm.pool_rstd(eng, 0, 0)

                def body(s, nxt, p):
                    if nxt is not None:
                        norm.pool_rstd(eng, nxt, 1 - p)
                    eng.wait_ge(h_kept, s + 1)
                    eng.tensor_tensor(r.h_lo[:, s, :], hT[:, p, :], r.h_hi[:, s, :].bitcast(F32), ALU.subtract)

                one_ahead(eng, body)

            @block.tensor
            def _(eng):
                eng.wait_ge(g_in, 16)
                eng.transpose(ps_l[:, 0:E_ALL], gate_rows[:, :], k.ident[0:E_ALL, 0:E_ALL]).then_inc(g_turned, 1)
                eng.wait_ge(g_done, 1)
                norm.tensor_turn(eng, ps_t[0], 0, 0)

                def body(s, nxt, p):
                    if nxt is not None:
                        eng.wait_ge(h_done, s)
                        norm.tensor_turn(eng, ps_t[1 - p], nxt, 1 - p)
                    eng.wait_ge(h_done, s + 1)
                    for t in range(T):
                        last = eng.matmul(ps_l[:, bass.ds((s * T + t) * E_ALL, E_ALL)], hT[:, p, t * P:(t + 1) * P], gateT[:, :],
                                          start=True, stop=True)
                    last.then_inc(logits_done, 1)

                one_ahead(eng, body)

            @block.scalar
            def _(eng):
                eng.wait_ge(g_turned, 1)
                eng.activation(gateT[:, :], ps_l[:, 0:E_ALL], ACT.Copy).then_inc(g_done, 1)

                def body(s, p):
                    eng.wait_ge(logits_done, s)
                    norm.scalar_modulate(eng, ps_t[p], hT[:, p, :], s).then_inc(h_done, 1)
                    eng.wait_ge(h_done, s + 1)
                    eng.activation(r.h_hi[:, s, :], hT[:, p, :], ACT.Copy).then_inc(h_kept, 1)

                pairs_of(eng, body)

            @block.vector
            def _(eng):
                norm.vector_stats(eng, 0, 0)

                def body(s, nxt, p):
                    if nxt is not None:
                        norm.vector_stats(eng, nxt, 1 - p)
                    eng.wait_ge(norm.turned, s)
                    norm.vector_normalise(eng, s, p)

                one_ahead(eng, body)
                eng.wait_ge(logits_done, B)
                eng.tensor_copy(logits[:, :, :].rearrange("p t e -> p (t e)"), ps_l[:, 0:TILES * E_ALL])

        route(nc, a, k, r, m, logits, (batches, ps_w, w_in, w_turned, w_done, w_low))


def route(nc, a, k, r, m, logits, weights):
    batches, ps_w, w_in, w_turned, w_done, w_low = weights
    S8 = [P, TILES, E_DYN]
    SKJ = [P, TILES, TOP_K, E_DYN]
    best, index, index_f = m.sb("r_best", S8), m.sb("r_index", S8, mybir.dt.uint32), m.sb("r_index_f", S8)
    negated, size = m.sb("r_negated", S8), m.sb("r_size", S8)
    apart, larger, close, expo = (m.sb(n, SKJ) for n in ("r_apart", "r_larger", "r_close", "r_expo"))
    kept_sum, slot_w = m.sb("r_kept_sum", [P, TILES, TOP_K]), m.sb("r_slot_w", [P, TILES, TOP_K])
    head_sum, whole, valid = m.sb("r_head_sum", [P, TILES, 3]), m.sb("r_whole", [P, TILES]), m.sb("r_valid", [P, TILES, 3])
    total, total_inv = m.sb("r_total", [P, TILES]), m.sb("r_total_inv", [P, TILES])
    experts = m.sb("r_experts", [P, E_DYN])
    chosen, weighed, rw = m.sb("r_chosen", SKJ), m.sb("r_weighed", SKJ), m.sb("r_rw", S8)
    mask, causal, ones = m.sb("r_mask", S8), m.sb("r_causal", [P, P]), m.sb("r_ones", [P, P])
    before = [m.sb("r_before0", [P, TILES + 1, E_DYN]), m.sb("r_before1", [P, TILES + 1, E_DYN])]
    count, fits, masked_l, penalty = m.sb("r_count", S8), m.sb("r_fits", S8), m.sb("r_masked_l", S8), m.sb("r_penalty", S8)
    top, shifted, expo9 = m.sb("r_top", [P, TILES]), m.sb("r_shifted", [P, TILES, E_ALL]), m.sb("r_expo9", [P, TILES, E_ALL])
    dyn_sum, all_sum, all_inv, dyn_share = (m.sb(n, [P, TILES]) for n in ("r_dyn_sum", "r_all_sum", "r_all_inv", "r_dyn_share"))
    ps_in, ps_all = m.ps("r_ps_in"), m.ps("r_ps_all")
    consts_in, pool_done = m.sem("r_consts_in"), m.sem("r_pool_done")
    step = m.sem("r_step")
    apart_done, expo_done, mask_done, counted = m.sem("r_apart_done"), m.sem("r_expo_done"), m.sem("r_mask_done"), m.sem("r_counted")
    shifted_done, expo9_done = m.sem("r_shifted_done"), m.sem("r_expo9_done")

    def over_j(t):
        return t.unsqueeze(3).to_broadcast([P, TILES, TOP_K, E_DYN])

    def over_k(t):
        return t.unsqueeze(2).to_broadcast([P, TILES, TOP_K, E_DYN])

    def over_e(t, n=E_DYN):
        return t.unsqueeze(2).to_broadcast([P, TILES, n])

    with nc.Block() as block:

        @block.sync
        def _(eng):
            eng.dma_start(causal[:, :], a["causal"]).then_inc(consts_in, 16)
            eng.dma_start(experts[:, :], a["experts"]).then_inc(consts_in, 16)

        @block.gpsimd
        def _(eng):
            eng.memset(ones[:, :], 1.0)
            for b in before:
                last = eng.memset(b[:, :, :].rearrange("p t e -> p (t e)"), 0.0)
            last.then_inc(pool_done, 1)

        @block.tensor
        def _(eng):
            eng.wait_ge(w_in, 6 * 16)
            for b, (src, _dst, u0, u1) in enumerate(batches):
                if b >= 2:
                    eng.wait_ge(w_done, b - 1)
                    eng.wait_ge(w_low, min(b - 1, 4))
                for u in range(u0, u1):
                    last = eng.transpose(ps_w[b % 2][:, (u - u0) * P:(u - u0 + 1) * P], src[:, u, :], k.ident[:, :])
                last.then_inc(w_turned, 1)
            eng.wait_ge(consts_in, 32)
            eng.wait_ge(pool_done, 1)
            eng.wait_ge(mask_done, 1)
            flat = mask[:, :, :].rearrange("p t e -> p (t e)")
            eng.matmul(ps_in[:, 0:TILES * E_DYN], causal[:, :], flat, start=True, stop=True)
            eng.matmul(ps_all[:, 0:TILES * E_DYN], ones[:, :], flat, start=True, stop=True).then_inc(counted, 1)

        @block.scalar
        def _(eng):
            eng.wait_ge(apart_done, 1)
            eng.activation(expo[:, :, :, :].rearrange("p t k j -> p (t k j)"),
                           apart[:, :, :, :].rearrange("p t k j -> p (t k j)"), ACT.Exp).then_inc(expo_done, 1)
            for b, (_src, dst, u0, u1) in enumerate(batches):
                eng.wait_ge(w_turned, b + 1)
                eng.activation(dst[:, u0:u1, :].rearrange("p u i -> p (u i)"), ps_w[b % 2][:, 0:(u1 - u0) * P],
                               ACT.Copy).then_inc(w_done, 1)
            eng.wait_ge(shifted_done, 1)
            eng.activation(expo9[:, :, :].rearrange("p t e -> p (t e)"),
                           shifted[:, :, :].rearrange("p t e -> p (t e)"), ACT.Exp).then_inc(expo9_done, 1)

        @block.vector
        def _(eng):
            steps = [0]

            def then(ins):
                steps[0] += 1
                ins.then_inc(step, 1)
                eng.wait_ge(step, steps[0])

            for t in range(TILES):
                last = eng.max(best[:, t, :], logits[:, t, 0:E_DYN])
            then(last)
            eng.tensor_tensor(apart[:, :, :, :], over_k(best[:, :, :]), over_j(best[:, :, 0:TOP_K]), ALU.subtract).then_inc(apart_done, 1)
            for t in range(TILES):
                last = eng.max_index(index[:, t, :], best[:, t, :], logits[:, t, 0:E_DYN])
            then(last)
            for b, (dst, low) in enumerate(((r.gate_hi, r.gate_lo), (r.up_hi, r.up_lo))):
                for half, (u0, u1) in enumerate(((0, 4), (4, UNITS))):
                    n = 2 * b + half
                    eng.wait_ge(w_done, n + 1)
                    eng.tensor_tensor(low[:, u0:u1, :].rearrange("p u i -> p (u i)"), ps_w[n % 2][:, 0:(u1 - u0) * P],
                                      dst[:, u0:u1, :].rearrange("p u i -> p (u i)").bitcast(F32), ALU.subtract).then_inc(w_low, 1)
            eng.tensor_copy(index_f[:, :, :], index[:, :, :])
            then(eng.tensor_scalar(negated[:, :, :], best[:, :, :], -1.0, None, ALU.mult))
            then(eng.tensor_tensor(size[:, :, :], best[:, :, :], negated[:, :, :], ALU.max))
            then(eng.tensor_tensor(larger[:, :, :, :], over_k(size[:, :, :]), over_j(size[:, :, 0:TOP_K]), ALU.max))
            flat4 = lambda t: t[:, :, :, :].rearrange("p t k j -> p (t k j)")
            then(eng.scalar_tensor_tensor(flat4(close), flat4(larger), 2.0 * JITTER, flat4(apart), ALU.mult, ALU.add))
            eng.wait_ge(expo_done, 1)
            then(eng.scalar_tensor_tensor(flat4(larger), flat4(close), 0.0, flat4(expo), ALU.is_ge, ALU.mult))
            for j in range(TOP_K):
                last = eng.tensor_reduce(kept_sum[:, :, j], larger[:, :, j, j:E_DYN], AX.X, ALU.add)
            eng.tensor_reduce(whole[:, :], expo[:, :, 0, :], AX.X, ALU.add)
            for j in range(3):
                last = eng.tensor_reduce(head_sum[:, :, j], expo[:, :, 0, 0:j + 1], AX.X, ALU.add)
            then(last)
            eng.reciprocal(slot_w[:, :, :], kept_sum[:, :, :])
            then(eng.scalar_tensor_tensor(valid[:, :, :], over_e(whole[:, :], 3), TOP_P, head_sum[:, :, :], ALU.mult, ALU.is_gt))
            then(eng.tensor_tensor(slot_w[:, :, 1:TOP_K], slot_w[:, :, 1:TOP_K], valid[:, :, :], ALU.mult))
            then(eng.tensor_reduce(total[:, :], slot_w[:, :, :], AX.X, ALU.add))
            then(eng.reciprocal(total_inv[:, :], total[:, :]))
            then(eng.tensor_tensor(slot_w[:, :, :], slot_w[:, :, :], over_e(total_inv[:, :], TOP_K), ALU.mult))
            eng.wait_ge(consts_in, 32)
            then(eng.tensor_tensor(chosen[:, :, :, :], over_j(index_f[:, :, 0:TOP_K]),
                                   experts[:, :].unsqueeze(1).unsqueeze(1).to_broadcast(SKJ), ALU.is_equal))
            then(eng.tensor_tensor(weighed[:, :, :, :], chosen[:, :, :, :], over_j(slot_w[:, :, :]), ALU.mult))
            then(eng.tensor_reduce(rw[:, :, :], weighed[:, :, :, :].rearrange("p t k e -> p t e k"), AX.X, ALU.add))
            eng.tensor_scalar(mask[:, :, :], rw[:, :, :], 0.0, None, ALU.is_gt).then_inc(mask_done, 1)
            eng.wait_ge(counted, 1)
            eng.wait_ge(pool_done, 1)
            then(eng.tensor_copy(before[0][:, 1:TILES + 1, :], ps_all[:, 0:TILES * E_DYN].rearrange("p (t e) -> p t e", e=E_DYN)))
            reach, cur = 1, 0
            while reach < TILES:
                src, dst = before[cur], before[1 - cur]
                eng.tensor_copy(dst[:, 1:reach + 1, :], src[:, 1:reach + 1, :])
                then(eng.tensor_tensor(dst[:, reach + 1:TILES + 1, :], src[:, reach + 1:TILES + 1, :],
                                       src[:, 1:TILES + 1 - reach, :], ALU.add))
                reach, cur = 2 * reach, 1 - cur
            then(eng.tensor_tensor(count[:, :, :], ps_in[:, 0:TILES * E_DYN].rearrange("p (t e) -> p t e", e=E_DYN),
                                   before[cur][:, 0:TILES, :], ALU.add))
            then(eng.scalar_tensor_tensor(fits[:, :, :], count[:, :, :], float(CAPACITY), mask[:, :, :], ALU.is_le, ALU.mult))
            eng.tensor_tensor(masked_l[:, :, :], logits[:, :, 0:E_DYN], fits[:, :, :], ALU.mult)
            then(eng.tensor_scalar(penalty[:, :, :], fits[:, :, :], -1.0, 1e30, ALU.add, ALU.mult))
            then(eng.tensor_tensor(masked_l[:, :, :], masked_l[:, :, :], penalty[:, :, :], ALU.add))
            then(eng.tensor_reduce(top[:, :], masked_l[:, :, :], AX.X, ALU.max))
            then(eng.tensor_tensor(top[:, :], top[:, :], logits[:, :, E_DYN], ALU.max))
            eng.tensor_tensor(shifted[:, :, 0:E_DYN], masked_l[:, :, :], over_e(top[:, :]), ALU.subtract)
            eng.tensor_tensor(shifted[:, :, E_DYN], logits[:, :, E_DYN], top[:, :], ALU.subtract).then_inc(shifted_done, 1)
            eng.wait_ge(expo9_done, 1)
            eng.tensor_reduce(dyn_sum[:, :], expo9[:, :, 0:E_DYN], AX.X, ALU.add)
            then(eng.tensor_reduce(all_sum[:, :], expo9[:, :, :], AX.X, ALU.add))
            then(eng.reciprocal(all_inv[:, :], all_sum[:, :]))
            then(eng.tensor_tensor(dyn_share[:, :], dyn_sum[:, :], all_inv[:, :], ALU.mult))
            then(eng.tensor_tensor(rw[:, :, :], rw[:, :, :], fits[:, :, :], ALU.mult))
            eng.tensor_tensor(r.weights[:, :, 0:E_DYN], rw[:, :, :], over_e(dyn_share[:, :]), ALU.mult)
            eng.tensor_tensor(r.weights[:, :, E_DYN], expo9[:, :, E_DYN], all_inv[:, :], ALU.mult)


class Router:

    def __init__(self, m):
        self.h_hi, self.h_lo = m.sb("moe_h_hi", [P, B, N], F32R), m.sb("moe_h_lo", [P, B, N], F32R)
        self.weights = m.sb("moe_weights", [P, TILES, E_ALL])
        self.gate_hi, self.gate_lo, self.up_hi, self.up_lo = (
            m.sb("moe_" + n, [P, UNITS, P], F32R) for n in ("gate_hi", "gate_lo", "up_hi", "up_lo"))
        self.down = m.sb("moe_down", [P, UNITS, P])


def expert_layers(nc, a, k, r, raw):
    with ExitStack() as stack:
        m = Memory(nc, stack)
        pair = m.sb("e_pair", [P, 2, T, 64])
        rounded = m.sb("e_rounded", [64, 2, N], F32R)
        stacked = m.sb("e_stacked", [64, 2, N], F32R)
        low_rows = m.sb("e_low_rows", [64, 1])
        pick_raw, pick = m.sb("e_pick_raw", [64, DYN_UNITS + 1, P]), m.sb("e_pick", [64, DYN_UNITS + 1, P], F32R)
        silu_g, product, hidden = m.sb("e_silu_g", [P, 2, N]), m.sb("e_product", [P, 2, N]), m.sb("e_hidden", [P, 2, N])
        scaled = m.sb("e_scaled", [P, 2, N])
        ps_g, ps_u, ps_w = ([m.ps(f"e_ps_{n}{i}") for i in (0, 1)] for n in "guw")
        ps_y, ps_t = m.ps("e_ps_y"), m.ps("e_ps_t")
        S = m.sem
        consts_in, pool_ready, ready = S("e_consts_in"), S("e_pool_ready"), S("e_ready")
        pair_done, turned, rounded_done, stacked_done = S("e_pair_done"), S("e_turned"), S("e_rounded_done"), S("e_stacked_done")
        g_done, u_done, w_done, silu_done = S("e_g_done"), S("e_u_done"), S("e_w_done"), S("e_silu_done")
        product_done, hidden_done, down_done = S("e_product_done"), S("e_hidden_done"), S("e_down_done")
        scaled_done, x_done = S("e_scaled_done"), S("e_x_done")
        with nc.Block() as block:

            @block.sync
            def _(eng):
                eng.dma_start(pick_raw[:, :, :].rearrange("p u n -> p (u n)"), a["pick"]).then_inc(consts_in, 16)
                eng.dma_start(low_rows[:, :], a["low_rows"]).then_inc(consts_in, 16)
                raw.load(eng, a)

            @block.gpsimd
            def _(eng):
                raw.pool_setup(eng)
                eng.memset(pair[:, :, :, :].rearrange("p a t n -> p (a t n)"), 0.0).then_inc(pool_ready, 1)
                eng.wait_ge(pool_ready, 1)

                def copy_pair(s, p):
                    for at in (0, 32):
                        last = eng.tensor_copy(pair[:, p, :, at:at + E_ALL], r.weights[:, bass.ds(s * T, T), :])
                    last.then_inc(pair_done, 1)

                def body(s, nxt, p):
                    if nxt is not None:
                        eng.wait_ge(turned, s)
                        copy_pair(nxt, 1 - p)
                    eng.wait_ge(scaled_done, s + 1)
                    xs = k.x[:, s, :, :].rearrange("p t d -> p (t d)")
                    eng.tensor_tensor(xs, scaled[:, p, :], xs, ALU.add).then_inc(x_done, 1)

                copy_pair(0, 0)
                one_ahead(eng, body)

            @block.tensor
            def _(eng):
                eng.wait_ge(ready, 1)

                def product3(bank, hi, lo, s):
                    eng.matmul(bank[:, :], hi, r.h_hi[:, s, :], start=True, stop=False)
                    eng.matmul(bank[:, :], hi, r.h_lo[:, s, :], start=False, stop=False)
                    return eng.matmul(bank[:, :], lo, r.h_hi[:, s, :], start=False, stop=True)

                def gate_up(s, u, first=False):
                    if not first:
                        eng.wait_ge(silu_done, s * UNITS + u - 1)
                    product3(ps_g[u % 2], r.gate_hi[:, u, :], r.gate_lo[:, u, :], s).then_inc(g_done, 1)
                    if not first:
                        eng.wait_ge(product_done, s * UNITS + u - 1)
                    product3(ps_u[u % 2], r.up_hi[:, u, :], r.up_lo[:, u, :], s).then_inc(u_done, 1)

                def turn_weights(s, p):
                    eng.wait_ge(pair_done, s + 1)
                    eng.wait_ge(stacked_done, s)
                    apart(eng, k.passed)
                    for t in range(T):
                        last = eng.transpose(ps_t[0:64, t * P:(t + 1) * P], pair[:, p, t, :], k.ident[:, :])
                    last.then_inc(turned, 1)

                def weigh(s, p, u):
                    if u == 0:
                        eng.wait_ge(stacked_done, s + 1)
                    eng.wait_ge(hidden_done, s * UNITS + max(u - 1, 0))
                    eng.matmul(ps_w[u % 2][:, :], pick[:, u, :], stacked[:, p, :], start=True, stop=True).then_inc(w_done, 1)

                def down(s, u):
                    eng.wait_ge(hidden_done, s * UNITS + u + 1)
                    if u == 0:
                        eng.wait_ge(scaled_done, s)
                    for t in range(T):
                        last = eng.matmul(ps_y[:, t * P:(t + 1) * P], hidden[:, u % 2, t * P:(t + 1) * P], r.down[:, u, :],
                                          start=(u == 0 and t == 0), stop=(u == UNITS - 1), skip_group_check=True)
                    last.then_inc(down_done, 1)

                def body(s, nxt, p):
                    for u in range(UNITS):
                        if u + 2 < UNITS:
                            gate_up(s, u + 2)
                        elif nxt is not None:
                            gate_up(nxt, u + 2 - UNITS)
                        if u < DYN_UNITS:
                            weigh(s, p, u + 1)
                        if nxt is not None and u == 3:
                            turn_weights(nxt, 1 - p)
                        down(s, u)
                    if nxt is not None:
                        weigh(nxt, 1 - p, 0)

                gate_up(0, 0, first=True)
                gate_up(0, 1, first=True)
                turn_weights(0, 0)
                weigh(0, 0, 0)
                one_ahead(eng, body)

            @block.scalar
            def _(eng):
                def round_weights(s, p):
                    eng.wait_ge(turned, s + 1)
                    eng.activation(rounded[:, p, :], ps_t[0:64, :], ACT.Copy).then_inc(rounded_done, 1)

                round_weights(0, 0)

                def body(s, nxt, p):
                    for u in range(UNITS):
                        eng.wait_ge(g_done, s * UNITS + u + 1)
                        eng.wait_ge(product_done, s * UNITS + max(u - 1, 0))
                        eng.activation(silu_g[:, u % 2, :], ps_g[u % 2][:, :], ACT.Silu).then_inc(silu_done, 1)
                        if nxt is not None and u == 5:
                            round_weights(nxt, 1 - p)

                one_ahead(eng, body)

            @block.vector
            def _(eng):
                eng.wait_ge(consts_in, 32)
                eng.tensor_copy(pick[:, :, :], pick_raw[:, :, :]).then_inc(ready, 1)

                def stack_parts(s, p):
                    eng.wait_ge(rounded_done, s + 1)
                    eng.scalar_tensor_tensor(stacked[:, p, :], rounded[:, p, :].bitcast(F32), low_rows[:, :], ps_t[0:64, :],
                                             ALU.mult, ALU.add).then_inc(stacked_done, 1)

                def multiply(s, u):
                    eng.wait_ge(silu_done, s * UNITS + u + 1)
                    eng.wait_ge(u_done, s * UNITS + u + 1)
                    eng.wait_ge(hidden_done, s * UNITS + max(u - 1, 0))
                    eng.tensor_tensor(product[:, u % 2, :], silu_g[:, u % 2, :], ps_u[u % 2][:, :], ALU.mult).then_inc(product_done, 1)

                def weigh(s, u):
                    eng.wait_ge(product_done, s * UNITS + u + 1)
                    eng.wait_ge(w_done, s * (DYN_UNITS + 1) + min(u, DYN_UNITS) + 1)
                    eng.wait_ge(down_done, s * UNITS + max(u - 1, 0))
                    eng.tensor_tensor(hidden[:, u % 2, :], product[:, u % 2, :], ps_w[min(u, DYN_UNITS) % 2][:, :],
                                      ALU.mult).then_inc(hidden_done, 1)

                def scale(s, p):
                    eng.wait_ge(down_done, s * UNITS + UNITS)
                    eng.tensor_tensor(scaled[:, p, :].rearrange("p (t d) -> p t d", t=T), ps_y[:, :].rearrange("p (t d) -> p t d", t=T),
                                      k.gates[:, s, 1, :].unsqueeze(1).to_broadcast([P, T, D]), ALU.mult).then_inc(scaled_done, 1)

                def body(s, nxt, p, last):
                    for u in range(UNITS):
                        multiply(s, u)
                        if u == 0 and last is not None:
                            scale(last, 1 - p)
                        weigh(s, u)
                    if nxt is not None:
                        stack_parts(nxt, 1 - p)

                stack_parts(0, 0)
                neighbours(eng, body)
                scale(B - 1, 1)


H1, DK, DC = 8, 128, 32
DKV = 2 * DC
SCALE = float(1.0 / np.sqrt(DK + DC))


def rounds(eng, body):
    body(0, None, None, 1, 0)
    body(1, 0, None, 2, 1)
    with eng.Fori(0, (B - 4) // 2) as i:
        body(2 * i + 2, 2 * i + 1, 2 * i, 2 * i + 3, 0)
        body(2 * i + 3, 2 * i + 2, 2 * i + 1, 2 * i + 4, 1)
    body(B - 2, B - 3, B - 4, B - 1, 0)
    body(B - 1, B - 2, B - 3, None, 1)
    body(None, B - 1, B - 2, None, 0)
    body(None, None, B - 1, None, 1)


class Latent:

    def __init__(self, m):
        self.q_lat = m.sb("l_q_lat", [P, P])
        self.kv_lat = m.sb("l_kv_lat", [P, P])
        self.bias = m.sb("l_bias", [2, 2, P], F32R)
        self.ones2 = m.sb("l_ones2", [2, N], F32R)
        self.query = m.sb("l_query", [P, H1, 2, DKV], F32R)
        self.out = m.sb("l_out", [P, 2, D])
        self.const = m.sb("l_const", [P, D])
        self.kv_bias = m.sb("l_kv_bias", [P, DC])
        self.q_low, self.upper_low = m.sb("l_q_low", [P, 1]), m.sb("l_upper_low", [P, 1])
        self.minus_upper = m.sb("l_minus_upper", [P, P], F32R)


class LatentRaw:

    def __init__(self, m, w):
        self.w = w
        self.uq, self.uk, self.uv = m.sb("f_uq", [DC + 1, H1, DK]), m.sb("f_uk", [DC, H1, DK]), m.sb("f_uv", [DC, H1, DK])
        self.qr, self.wo = m.sb("f_qr", [DC + 1, H1, DC]), m.sb("f_wo", [P, H1, D])
        self.b_uv_rows, self.b_o = m.sb("f_b_uv_rows", [H1, DK]), m.sb("f_b_o", [P, D])
        self.place, self.low_w, self.low2 = m.sb("f_place", [DC + 1, P]), m.sb("f_low_w", [P, 1]), m.sb("f_low2", [2, 1])
        self.bias2 = m.sb("f_bias2", [2, 2, P])
        self.pool_done, self.in_done = m.sem("f_pool_done"), m.sem("f_in_done")
        self.IN = 16 * (10 + 2 * 3 + 2 * 4 + 5)

    def pool_setup(self, eng):
        eng.memset(self.w.q_lat[:, :], 0.0)
        eng.memset(self.w.ones2[:, :].bitcast(F32), 1.0)
        eng.memset(self.bias2[:, :, :], 1.0).then_inc(self.pool_done, 1)

    def load(self, eng, a):
        eng.wait_ge(self.pool_done, 1)

        def load(dst, src):
            eng.dma_start(dst, src).then_inc(self.in_done, 16)

        row = lambda v: v.rearrange("(o n) -> o n", o=1)
        heads = lambda t: t.rearrange("p h d -> p (h d)")
        load(heads(self.uq[0:DC, :, :]), a["L1_attn_W_UQ"])
        load(heads(self.uq[DC:DC + 1, :, :]), row(a["L1_attn_b_UQ"]))
        load(heads(self.uk[:, :, :]), a["L1_attn_W_UK"])
        load(heads(self.uv[:, :, :]), a["L1_attn_W_UV"])
        load(heads(self.qr[0:DC, :, :]), a["L1_attn_W_QR"])
        load(heads(self.qr[DC:DC + 1, :, :]), row(a["L1_attn_b_QR"]))
        load(self.wo[:, :, :], a["L1_attn_W_O"].rearrange("(h d) n -> d h n", h=H1))
        load(self.b_uv_rows[:, :], a["L1_attn_b_UV"].rearrange("(h d) -> h d", h=H1))
        load(self.b_o[:, :], a["L1_attn_b_O"].partition_broadcast(P))
        load(self.w.kv_bias[:, :], a["L1_attn_b_DKV"].partition_broadcast(P))
        for copy in range(3):
            load(self.w.q_lat[:, copy * DC:(copy + 1) * DC], a["L1_attn_W_DQ"])
            load(self.bias2[:, 0, copy * DC:(copy + 1) * DC], a["L1_attn_b_DQ"].partition_broadcast(2))
        for copy in range(4):
            which = "DKV" if copy % 2 == 0 else "KR"
            load(self.w.kv_lat[:, copy * DC:(copy + 1) * DC], a[f"L1_attn_W_{which}"])
            load(self.bias2[:, 1, copy * DC:(copy + 1) * DC], a[f"L1_attn_b_{which}"].partition_broadcast(2))
        load(self.place[:, :], a["place"])
        load(self.low_w[:, :], a["low_w"])
        load(self.low2[:, :], a["low_rows"][31:33, :])
        load(self.w.q_low[:, :], a["q_low"])
        load(self.w.upper_low[:, :], a["upper_low"])


def fold_latent(nc, a, k, w, raw):
    with ExitStack() as stack:
        m = Memory(nc, stack)
        uq, uk, uv, qr, wo, b_o, bias2 = raw.uq, raw.uk, raw.uv, raw.qr, raw.wo, raw.b_o, raw.bias2
        b_uv_rows, place, low_w, low2, in_done, IN = raw.b_uv_rows, raw.place, raw.low_w, raw.low2, raw.in_done, raw.IN
        b_uv, b_uv_wide = m.sb("f_b_uv", [P, H1]), m.sb("f_b_uv_wide", [P, H1, P])
        uqT, ukT, uvT = m.sb("f_uqT", [P, H1, DC + 1]), m.sb("f_ukT", [P, H1, DC]), m.sb("f_uvT", [P, H1, DC])
        met = m.sb("f_met", [DC + 1, H1, DKV])
        rounded = m.sb("f_rounded", [P, H1 * DKV], F32R)
        bias2_hi = m.sb("f_bias2_hi", [2, 2, P], F32R)
        ps = {n: m.ps("f_ps_" + n) for n in ("uq", "uk", "uv", "met", "query", "out", "const")}
        turned, copied, products, met_done, placed, step = (m.sem("f_" + n) for n in
                                                            ("turned", "copied", "products", "met_done", "placed", "step"))
        with nc.Block() as block:

            @block.tensor
            def _(eng):
                eng.wait_ge(in_done, IN)
                for name, src, rows in (("uq", uq, DC + 1), ("uk", uk, DC), ("uv", uv, DC)):
                    for h in range(H1):
                        last = eng.transpose(ps[name][:, h * rows:(h + 1) * rows], src[:, h, :], k.ident[0:rows, 0:rows])
                    last.then_inc(turned, 1)
                eng.transpose(ps["const"][:, 0:H1], b_uv_rows[:, :], k.ident[0:H1, 0:H1]).then_inc(turned, 1)
                eng.wait_ge(copied, 4)
                for h in range(H1):
                    last = eng.matmul(ps["met"][0:DC + 1, h * DC:(h + 1) * DC], uqT[:, h, :], ukT[:, h, :], start=True, stop=True)
                last.then_inc(products, 1)
                for h in range(H1):
                    g, j = divmod(h, 4)
                    last = eng.matmul(ps["out"][32 * j:32 * j + 32, g * D:(g + 1) * D], uvT[:, h, :], wo[:, h, :],
                                      start=True, stop=True, skip_group_check=True)
                last.then_inc(products, 1)
                eng.wait_ge(met_done, 1)
                eng.matmul(ps["query"][:, :], place[:, :], met[:, :, :].rearrange("p h c -> p (h c)"), start=True, stop=True).then_inc(placed, 1)
                for h in range(H1):
                    last = eng.matmul(ps["const"][:, 0:D], b_uv_wide[:, h, :], wo[:, h, :], start=(h == 0), stop=(h == H1 - 1))
                last.then_inc(placed, 1)

            @block.scalar
            def _(eng):
                for n, (name, dst) in enumerate((("uq", uqT), ("uk", ukT), ("uv", uvT), ("const", b_uv))):
                    flat = dst[:, :] if name == "const" else dst[:, :, :].rearrange("p h c -> p (h c)")
                    eng.wait_ge(turned, n + 1)
                    eng.activation(flat, ps[name][:, 0:flat.shape[1]], ACT.Copy).then_inc(copied, 1)

            @block.vector
            def _(eng):
                eng.wait_ge(in_done, IN)
                eng.tensor_copy(met[:, :, DC:DKV], qr[:, :, :])
                eng.tensor_scalar(w.minus_upper[:, :], k.ident[:, :], w.upper_low[:, :], None, ALU.mult)
                eng.tensor_copy(bias2_hi[:, :, :], bias2[:, :, :]).then_inc(step, 1)
                eng.wait_ge(copied, 4)
                eng.tensor_copy(b_uv_wide[:, :, :], b_uv[:, :].unsqueeze(2).to_broadcast([P, H1, P]))
                eng.wait_ge(products, 1)
                eng.tensor_copy(met[:, :, 0:DC], ps["met"][0:DC + 1, 0:H1 * DC].rearrange("p (h c) -> p h c", h=H1)).then_inc(met_done, 1)
                eng.wait_ge(step, 1)
                eng.scalar_tensor_tensor(w.bias[:, :, :], bias2_hi[:, :, :].bitcast(F32), low2[:, :], bias2[:, :, :], ALU.mult, ALU.add)
                eng.wait_ge(products, 2)
                eng.tensor_copy(w.out[:, :, :].rearrange("p g n -> p (g n)"), ps["out"][:, 0:2 * D])
                eng.wait_ge(placed, 1)
                eng.tensor_copy(rounded[:, :], ps["query"][:, :]).then_inc(step, 1)
                eng.wait_ge(step, 2)
                for copy in range(2):
                    eng.scalar_tensor_tensor(w.query[:, :, copy, :], rounded[:, :].bitcast(F32).rearrange("p (h c) -> p h c", h=H1), low_w[:, :],
                                             ps["query"][:, :].rearrange("p (h c) -> p h c", h=H1), ALU.mult, ALU.add)
                eng.wait_ge(placed, 2)
                eng.tensor_tensor(w.const[:, :], ps["const"][:, 0:D], b_o[:, :], ALU.add)


def latent_attention(nc, a, k, w):
    with ExitStack() as stack:
        m = Memory(nc, stack)
        norm = Norm(m, k, 1, SA, CA)
        hT = m.sb("a_hT", [P, N])
        q_lat_hi, q_lat = m.sb("a_q_lat_hi", [P, N], F32R), m.sb("a_q_lat", [P, N], F32R)
        key_hi, key_lo = m.sb("a_key_hi", [P, 2, N], F32R), m.sb("a_key_lo", [P, 2, N], F32R)
        value, ones = m.sb("a_value", [P, 2, T, DC]), m.sb("a_ones", [P, DC])
        q_hi, q_both = m.sb("a_q_hi", [P, 2, H1, N], F32R), m.sb("a_q_both", [P, 2, H1, N], F32R)
        top, shift = m.sb("a_top", [P, H1 * T]), m.sb("a_shift", [H1 * T, P])
        RING = 6
        expo, expo_sum = m.sb("a_expo", [P, RING, T, N]), m.sb("a_expo_sum", [P, RING, N])
        mixedT = m.sb("a_mixedT", [P, 2, N])
        out_w, const_g = m.sb("a_out_w", [P, 2, D]), m.sb("a_const_g", [P, D])
        ps_f, ps_m, ps_s = ([m.ps(f"a_ps_{n}{i}") for i in (0, 1)] for n in "fms")
        ps_v, ps_y = m.ps("a_ps_v"), m.ps("a_ps_y")
        S = m.sem
        filled, emptied = [S("a_filled0"), S("a_filled1")], [S("a_emptied0"), S("a_emptied1")]
        pool_ready, h_done = S("a_pool_ready"), S("a_h_done")
        lat_hi_done, key_hi_done, q_hi_done = S("a_lat_hi_done"), S("a_key_hi_done"), S("a_q_hi_done")
        q_split = S("a_q_split")
        rough, top_done, shift_in = S("a_rough"), S("a_top_done"), S("a_shift_in")
        scores_done, expo_done, pv_done = S("a_scores_done"), S("a_expo_done"), S("a_pv_done")
        added, summed, totals_done, mixed_done = S("a_added"), S("a_summed"), S("a_totals_done"), S("a_mixed_done")
        total, inverse = m.sb("a_total", [P, 2, N]), m.sb("a_inverse", [P, N])
        total_kept, inverse_done = S("a_total_kept"), S("a_inverse_done")
        weighted, weighted_done = m.sb("a_weighted", [P, 2, N]), S("a_weighted_done")
        last_added, last_summed = S("a_last_added"), S("a_last_summed")
        const_done, pre_done, out_w_done, y_done, x_done = S("a_const_done"), S("a_pre_done"), S("a_out_w_done"), S("a_y_done"), S("a_x_done")
        LAT, KEY, VALUE, QUERY, TOP = 0, 1, 2, 3, 3 + H1
        USES = (TOP + 1) // 2
        HT = H1 * T

        def nth(n, s):
            return s * USES + n // 2 + 1

        with nc.Block() as block:

            @block.gpsimd
            def _(eng):
                norm.pool_setup(eng)
                eng.memset(ones[:, :], 1.0).then_inc(pool_ready, 1)
                eng.wait_ge(pool_ready, 1)
                eng.memset(key_lo[DKV:P, :, :].bitcast(F32), 0.0).then_inc(pool_ready, 1)
                eng.wait_ge(pool_ready, 2)
                eng.memset(key_lo[DKV:DKV + 1, :, :].bitcast(F32), 1.0).then_inc(pool_ready, 1)
                norm.pool_rstd(eng, 0, 0)

                def body(front, back, late, nxt, p):
                    if late is not None:
                        eng.tensor_tensor(out_w[:, :, :], w.out[:, :, :],
                                          k.gates[:, late, 2, :].unsqueeze(1).to_broadcast([P, 2, D]), ALU.mult).then_inc(out_w_done, 1)
                        eng.tensor_tensor(const_g[:, :], w.const[:, :], k.gates[:, late, 2, :], ALU.mult).then_inc(const_done, 1)
                        eng.wait_ge(const_done, late + 1)
                        eng.wait_ge(norm.xn_done, late + 1)
                        eng.tensor_tensor(k.x[:, late, :, :], k.x[:, late, :, :],
                                          const_g[:, :].unsqueeze(1).to_broadcast([P, T, D]), ALU.add).then_inc(pre_done, 1)
                    for h in range(H1):
                        if h == 4 and nxt is not None:
                            norm.pool_rstd(eng, nxt, 1 - p)
                        if h == 7 and front is not None:
                            eng.wait_ge(emptied[TOP % 2], nth(TOP, front))
                            apart(eng, k.passed)
                            eng.dma_start(q_hi[DKV:DKV + 1, p, :, :].rearrange("o h (t n) -> o (h t) n", t=T),
                                          shift[:, :]).then_inc(shift_in, 16)
                        if back is not None and h < H1 - 1:
                            if h == RING:
                                eng.wait_ge(totals_done, back * 2 + 1)
                            for t in range(1, T):
                                eng.wait_ge(expo_done, back * HT + h * T + t + 1)
                                if t > 1:
                                    eng.wait_ge(added, (back * (H1 - 1) + h) * 2 + t - 1)
                                eng.tensor_tensor(expo_sum[:, h % RING, :], expo[:, h % RING, 0, :] if t == 1 else expo_sum[:, h % RING, :], expo[:, h % RING, t, :],
                                                  ALU.add).then_inc(added if t < T - 1 else summed, 1)
                    if late is not None:
                        eng.wait_ge(y_done, late + 1)
                        eng.wait_ge(pre_done, late + 1)

                rounds(eng, body)

            @block.tensor
            def _(eng):
                eng.wait_ge(pool_ready, 3)
                norm.tensor_turn(eng, ps_y, 0, 0)

                def latent(s, p, n):
                    weights = (w.q_lat, w.kv_lat)[n]
                    eng.wait_ge(h_done, s + 1)
                    eng.wait_ge(emptied[n % 2], nth(n, s) - 1)
                    eng.matmul(ps_f[n % 2][:, :], weights[:, :], hT[:, :], start=True, stop=False)
                    eng.matmul(ps_f[n % 2][:, :], w.bias[:, n, :], w.ones2[:, :], start=False, stop=True).then_inc(filled[n % 2], 1)

                def latent_values(s, p):
                    eng.wait_ge(emptied[VALUE % 2], nth(VALUE, s) - 1)
                    for t in range(T):
                        last = eng.matmul(ps_f[VALUE % 2][:, t * DC:(t + 1) * DC], hT[:, t * P:(t + 1) * P], w.kv_lat[:, 0:DC],
                                          start=True, stop=True)
                    last.then_inc(filled[VALUE % 2], 1)

                def queries(s, p, h):
                    n = QUERY + h
                    if h == 0:
                        eng.wait_ge(emptied[LAT % 2], nth(LAT, s))
                    eng.wait_ge(emptied[n % 2], nth(n, s) - 1)
                    eng.matmul(ps_f[n % 2][:, :], w.query[:, h, :, :].rearrange("p c n -> p (c n)"), q_lat[:, :],
                               start=True, stop=True, skip_group_check=True).then_inc(filled[n % 2], 1)

                def take_hi(s, p, h):
                    eng.wait_ge(q_hi_done, s * H1 + h + 1)
                    eng.matmul(ps_f[(QUERY + h) % 2][:, :], w.minus_upper[:, :], q_hi[:, p, h, :], start=False, stop=True,
                               skip_group_check=True).then_inc(q_split, 1)

                def rough_scores(s, p, h, t):
                    n = h * T + t
                    if t == 0:
                        eng.wait_ge(q_hi_done, s * H1 + h + 1)
                    if n == 0:
                        eng.wait_ge(emptied[KEY % 2], nth(KEY, s))
                    eng.wait_ge(top_done, s * HT + max(n - 1, 0))
                    eng.matmul(ps_m[n % 2][:, :], q_hi[0:DKV, p, h, t * P:(t + 1) * P], key_hi[0:DKV, p, :],
                               start=True, stop=True).then_inc(rough, 1)

                def scores(s, p, h, t):
                    n = h * T + t
                    if n == 0:
                        eng.wait_ge(shift_in, s * 16 + 16)
                    if n >= 2:
                        eng.wait_ge(expo_done, s * HT + n - 1)
                    eng.matmul(ps_s[n % 2][:, :], key_hi[:, p, t * P:(t + 1) * P], q_both[:, p, h, :], start=True, stop=False)
                    eng.matmul(ps_s[n % 2][:, :], key_lo[:, p, t * P:(t + 1) * P], q_hi[:, p, h, :],
                               start=False, stop=True).then_inc(scores_done, 1)

                def quad_values(s, p, quad, t):
                    if t == 0:
                        eng.wait_ge(expo_done, s * HT + 4 * T * (quad + 1))
                    if t == 0 and quad > 0:
                        eng.wait_ge(weighted_done, s * 2 + quad)
                    for j in range(4):
                        last = eng.matmul(ps_v[DC * j:DC * (j + 1), :], value[:, p, t, :], expo[:, (4 * quad + j) % RING, t, :],
                                          start=(t == 0), stop=(t == T - 1), skip_group_check=True)
                    if t == T - 1:
                        last.then_inc(pv_done, 1)

                def totals(s, quad):
                    eng.wait_ge(summed, s * (H1 - 1) + (4, H1 - 1)[quad])
                    if quad == 1:
                        eng.wait_ge(last_summed, s + 1)
                    for j in range(4):
                        last = eng.matmul(ps_y[DC * j:DC * (j + 1), :], ones[:, :], expo_sum[:, (4 * quad + j) % RING, :],
                                          start=True, stop=True, skip_group_check=True)
                    last.then_inc(totals_done, 1)

                def output(s):
                    eng.wait_ge(mixed_done, s * 2 + 2)
                    eng.wait_ge(out_w_done, s + 1)
                    for t in range(T):
                        for g in range(2):
                            last = eng.matmul(ps_y[:, t * P:(t + 1) * P], mixedT[:, g, t * P:(t + 1) * P], out_w[:, g, :],
                                              start=(g == 0), stop=(g == 1))
                    last.then_inc(y_done, 1)

                def body(front, back, late, nxt, p):
                    if front is not None:
                        queries(front, p, 0)
                    for h in range(H1):
                        for t in range(T):
                            if back is not None:
                                scores(back, 1 - p, h, t)
                            if front is not None:
                                rough_scores(front, p, h, t)
                            if front is not None and t == 0:
                                take_hi(front, p, h)
                            if front is not None and t == 0 and h + 1 < H1:
                                queries(front, p, h + 1)
                            if back is not None and h in (4, 5) and t % 2 == 0:
                                quad_values(back, 1 - p, 0, (h % 2) * 2 + t // 2)
                            if nxt is not None and (h, t) == (6, 2):
                                if late is not None:
                                    eng.wait_ge(x_done, late + 1)
                                elif back is not None:
                                    eng.wait_ge(total_kept, back * 2 + 1)
                                norm.tensor_turn(eng, ps_y, nxt, 1 - p)
                        if back is not None and h == 4:
                            if late is not None:
                                eng.wait_ge(total_kept, late * 2 + 2)
                            totals(back, 0)
                        if late is not None and h == 5:
                            eng.wait_ge(total_kept, late * 2 + 2 if back is None else back * 2 + 1)
                            output(late)
                    if back is not None:
                        quad_values(back, 1 - p, 1, 0)
                    if front is not None:
                        eng.wait_ge(top_done, front * HT + HT)
                        eng.wait_ge(emptied[TOP % 2], nth(TOP, front) - 1)
                        eng.transpose(ps_f[TOP % 2][0:HT, 0:P], top[:, :], k.ident[:, :]).then_inc(filled[TOP % 2], 1)
                    if nxt is not None:
                        latent(nxt, 1 - p, LAT)
                    if back is not None:
                        for t in range(1, T):
                            quad_values(back, 1 - p, 1, t)
                    if nxt is not None:
                        latent(nxt, 1 - p, KEY)
                    if back is not None:
                        if nxt is None:
                            eng.wait_ge(x_done, late + 1)
                        totals(back, 1)
                    if nxt is not None:
                        latent_values(nxt, 1 - p)

                latent(0, 0, LAT)
                latent(0, 0, KEY)
                latent_values(0, 0)
                rounds(eng, body)

            @block.scalar
            def _(eng):
                norm.scalar_modulate(eng, ps_y, hT[:, :], 0).then_inc(h_done, 1)

                def latent_hi(s, p):
                    eng.wait_ge(filled[LAT % 2], nth(LAT, s))
                    eng.activation(q_lat_hi[:, :], ps_f[LAT % 2][:, :], ACT.Copy).then_inc(lat_hi_done, 1)

                def key_high(s, p):
                    eng.wait_ge(filled[KEY % 2], nth(KEY, s))
                    eng.activation(key_hi[:, p, :], ps_f[KEY % 2][:, :], ACT.Copy).then_inc(key_hi_done, 1)

                def query_hi(s, p, h):
                    n = QUERY + h
                    eng.wait_ge(filled[n % 2], nth(n, s))
                    eng.activation(q_hi[:, p, h, :], ps_f[n % 2][:, :], ACT.Copy).then_inc(q_hi_done, 1)

                def query_both(s, p, h):
                    n = QUERY + h
                    eng.wait_ge(q_split, s * H1 + h + 1)
                    eng.activation(q_both[:, p, h, :], ps_f[n % 2][:, :], ACT.Copy).then_inc(emptied[n % 2], 1)

                def read_values(s, quad):
                    eng.wait_ge(pv_done, s * 2 + quad + 1)
                    eng.activation(weighted[:, quad, :], ps_v[:, :], ACT.Copy).then_inc(weighted_done, 1)

                def keep_total(s, quad):
                    eng.wait_ge(totals_done, s * 2 + quad + 1)
                    eng.activation(total[:, quad, :], ps_y[:, :], ACT.Copy).then_inc(total_kept, 1)

                def body(front, back, late, nxt, p):
                    if front is not None:
                        query_hi(front, p, 0)
                    for h in range(H1):
                        for t in range(T):
                            if back is not None:
                                n = h * T + t
                                eng.wait_ge(scores_done, back * HT + n + 1)
                                eng.activation(expo[:, h % RING, t, :], ps_s[n % 2][:, :], ACT.Exp, scale=SCALE).then_inc(expo_done, 1)
                                if n == 6 * T - 1:
                                    read_values(back, 0)
                                if n == 5 * T + 1:
                                    keep_total(back, 0)
                            if front is not None and t == 0:
                                query_both(front, p, h)
                            if front is not None and t == 1 and h + 1 < H1:
                                query_hi(front, p, h + 1)
                            if nxt is not None and h == 7 and t == 1:
                                norm.scalar_modulate(eng, ps_y, hT[:, :], nxt).then_inc(h_done, 1)
                    if nxt is not None:
                        latent_hi(nxt, 1 - p)
                    if back is not None:
                        read_values(back, 1)
                    if nxt is not None:
                        key_high(nxt, 1 - p)
                    if back is not None:
                        keep_total(back, 1)

                latent_hi(0, 0)
                key_high(0, 0)
                rounds(eng, body)

            @block.vector
            def _(eng):
                eng.wait_ge(pool_ready, 3)
                norm.vector_stats(eng, 0, 0)
                norm.vector_normalise(eng, 0, 0)

                def latent_low(s, p):
                    eng.wait_ge(lat_hi_done, s + 1)
                    eng.scalar_tensor_tensor(q_lat[:, :], q_lat_hi[:, :].bitcast(F32), w.q_low[:, :], ps_f[LAT % 2][:, :],
                                             ALU.mult, ALU.add).then_inc(emptied[LAT % 2], 1)

                def key_low(s, p):
                    eng.wait_ge(key_hi_done, s + 1)
                    eng.tensor_tensor(key_lo[0:DKV, p, :], ps_f[KEY % 2][0:DKV, :], key_hi[0:DKV, p, :].bitcast(F32),
                                      ALU.subtract).then_inc(emptied[KEY % 2], 1)

                def add_value_bias(s, p):
                    eng.wait_ge(filled[VALUE % 2], nth(VALUE, s))
                    eng.tensor_tensor(value[:, p, :, :], ps_f[VALUE % 2][:, 0:T * DC].rearrange("p (t c) -> p t c", t=T),
                                      w.kv_bias[:, :].unsqueeze(1).to_broadcast([P, T, DC]), ALU.add).then_inc(emptied[VALUE % 2], 1)

                def invert(s, quad, part):
                    eng.wait_ge(total_kept, s * 2 + quad + 1)
                    eng.wait_ge(mixed_done, s * 2 + quad)
                    at = slice(part * N // 8, (part + 1) * N // 8)
                    eng.reciprocal(inverse[:, at], total[:, quad, at]).then_inc(inverse_done, 1)

                INVERT_0 = [(5, 3), (6, 1), (6, 2), (6, 3), (7, 0), (7, 1), (7, 2), (7, 3)]

                def mix(s, quad):
                    eng.wait_ge(inverse_done, (s * 2 + quad + 1) * 8)
                    eng.wait_ge(weighted_done, s * 2 + quad + 1)
                    eng.tensor_tensor(mixedT[:, quad, :], weighted[:, quad, :], inverse[:, :], ALU.mult).then_inc(mixed_done, 1)

                def add_output(s):
                    eng.wait_ge(y_done, s + 1)
                    eng.wait_ge(pre_done, s + 1)
                    xs = k.x[:, s, :, :].rearrange("p t d -> p (t d)")
                    eng.tensor_tensor(xs, ps_y[:, :], xs, ALU.add).then_inc(x_done, 1)

                def add_last(s):
                    h = H1 - 1
                    for t in range(1, T):
                        if t == 1:
                            eng.wait_ge(expo_done, s * HT + HT)
                        else:
                            eng.wait_ge(last_added, s * 2 + t - 1)
                        eng.tensor_tensor(expo_sum[:, h % RING, :], expo[:, h % RING, 0, :] if t == 1 else expo_sum[:, h % RING, :],
                                          expo[:, h % RING, t, :], ALU.add).then_inc(last_added if t < T - 1 else last_summed, 1)

                def body(front, back, late, nxt, p):
                    for h in range(H1):
                        for t in range(T):
                            if front is not None:
                                n = h * T + t
                                eng.wait_ge(rough, front * HT + n + 1)
                                eng.tensor_reduce(top[:, n:n + 1], ps_m[n % 2][:, :], AX.X, ALU.max).then_inc(top_done, 1)
                            if late is not None and h < 4 and t % 2 == 1:
                                invert(late, 1, h * 2 + t // 2)
                            if late is not None and (h, t) == (6, 0):
                                add_output(late)
                            if back is not None and (h, t) in INVERT_0:
                                invert(back, 0, INVERT_0.index((h, t)))
                        if late is not None and h == 4:
                            mix(late, 1)
                        if nxt is not None and h == 3:
                            norm.vector_stats(eng, nxt, 1 - p)
                        if nxt is not None and h == 5:
                            norm.vector_normalise(eng, nxt, 1 - p)
                    if front is not None:
                        eng.wait_ge(filled[TOP % 2], nth(TOP, front))
                        eng.wait_ge(shift_in, front * 16)
                        eng.tensor_scalar(shift[:, :], ps_f[TOP % 2][0:HT, 0:P], -1.0, None, ALU.mult).then_inc(emptied[TOP % 2], 1)
                    if back is not None:
                        mix(back, 0)
                    if nxt is not None:
                        latent_low(nxt, 1 - p)
                    if back is not None:
                        add_last(back)
                    if nxt is not None:
                        key_low(nxt, 1 - p)
                        add_value_bias(nxt, 1 - p)

                latent_low(0, 0)
                key_low(0, 0)
                add_value_bias(0, 0)
                rounds(eng, body)


HID = 512
Q1 = HID // P


class Binary:

    def __init__(self, m):
        self.sign1T = m.sb("b_sign1T", [P, Q1, P], F32R)
        self.sign2T = m.sb("b_sign2T", [P, Q1, D])
        self.alpha1, self.b1 = m.sb("b_alpha1", [P, Q1]), m.sb("b_b1", [P, Q1])
        self.alpha2, self.b2 = m.sb("b_alpha2", [P, D]), m.sb("b_b2", [P, D])


def binarise(nc, a, k, w):
    with ExitStack() as stack:
        m = Memory(nc, stack)
        w1, w2, b1_rows = m.sb("z_w1", [P, Q1, D]), m.sb("z_w2", [P, HID]), m.sb("z_b1_rows", [Q1, P])
        sign1, sign2 = m.sb("z_sign1", [P, Q1, D]), m.sb("z_sign2", [P, HID])
        size1, size2 = m.sb("z_size1", [P, Q1, D]), m.sb("z_size2", [P, HID])
        sum1, sum2, diag = m.sb("z_sum1", [P, Q1]), m.sb("z_sum2", [P, 1]), m.sb("z_diag", [P, P])
        ones = m.sb("z_ones", [P, P])
        ps_1, ps_2, ps_b, ps_a = (m.ps("z_ps_" + n) for n in ("1", "2", "b", "a"))
        in_done, ones_done, signs_done, sizes_done, sums_done, diag_done, turned, spread = (
            m.sem("z_" + n) for n in ("in", "ones", "signs", "sizes", "sums", "diag", "turned", "spread"))
        with nc.Block() as block:

            @block.sync
            def _(eng):
                eng.dma_start(w1[:, :, :], a["L1_ffn_w1"].rearrange("(q p) d -> p q d", p=P)).then_inc(in_done, 16)
                eng.dma_start(w2[:, :], a["L1_ffn_w2"]).then_inc(in_done, 16)
                eng.dma_start(b1_rows[:, :], a["L1_ffn_b1"].rearrange("(q p) -> q p", p=P)).then_inc(in_done, 16)
                eng.dma_start(w.b2[:, :], a["L1_ffn_b2"].partition_broadcast(P)).then_inc(in_done, 16)

            @block.gpsimd
            def _(eng):
                eng.memset(ones[:, :], 1.0).then_inc(ones_done, 1)

            @block.tensor
            def _(eng):
                eng.wait_ge(in_done, 64)
                eng.transpose(ps_b[:, 0:Q1], b1_rows[:, :], k.ident[0:Q1, 0:Q1]).then_inc(turned, 1)
                eng.wait_ge(signs_done, 2)
                for q in range(Q1):
                    last = eng.transpose(ps_1[:, q * P:(q + 1) * P], sign1[:, q, :], k.ident[:, :])
                last.then_inc(turned, 1)
                for q in range(Q1):
                    last = eng.transpose(ps_2[:, q * P:(q + 1) * P], sign2[:, q * P:(q + 1) * P], k.ident[:, :])
                last.then_inc(turned, 1)
                eng.wait_ge(diag_done, 1)
                eng.wait_ge(ones_done, 1)
                eng.matmul(ps_a[:, 0:D], ones[:, :], diag[:, :], start=True, stop=True).then_inc(spread, 1)

            @block.scalar
            def _(eng):
                flat = lambda t: t[:, :, :].rearrange("p q d -> p (q d)")
                eng.wait_ge(in_done, 64)
                eng.activation(flat(sign1), flat(w1), ACT.Sign).then_inc(signs_done, 1)
                eng.activation(sign2[:, :], w2[:, :], ACT.Sign).then_inc(signs_done, 1)
                eng.activation(flat(size1), flat(w1), ACT.Abs).then_inc(sizes_done, 1)
                eng.activation(size2[:, :], w2[:, :], ACT.Abs).then_inc(sizes_done, 1)
                eng.wait_ge(turned, 1)
                eng.activation(w.b1[:, :], ps_b[:, 0:Q1], ACT.Copy)
                eng.wait_ge(turned, 2)
                eng.activation(flat(w.sign1T), ps_1[:, :], ACT.Copy)
                eng.wait_ge(turned, 3)
                eng.activation(flat(w.sign2T), ps_2[:, :], ACT.Copy)

            @block.vector
            def _(eng):
                eng.wait_ge(sizes_done, 1)
                eng.tensor_reduce(sum1[:, :], size1[:, :, :], AX.X, ALU.add).then_inc(sums_done, 1)
                eng.wait_ge(sizes_done, 2)
                eng.tensor_reduce(sum2[:, :], size2[:, :], AX.X, ALU.add).then_inc(sums_done, 1)
                eng.wait_ge(sums_done, 2)
                eng.tensor_scalar(w.alpha1[:, :], sum1[:, :], 1.0 / D, None, ALU.mult)
                eng.tensor_scalar(diag[:, :], k.ident[:, :], sum2[:, :], 1.0 / HID, ALU.mult, ALU.mult).then_inc(diag_done, 1)
                eng.wait_ge(spread, 1)
                eng.tensor_copy(w.alpha2[:, :], ps_a[:, 0:D])


def feed_forward(nc, a, k, w, out):
    with ExitStack() as stack:
        m = Memory(nc, stack)
        norm = Norm(m, k, 1, SB, CB)
        hT = m.sb("d_hT", [P, 2, N])
        h_hi, h_lo = m.sb("d_h_hi", [P, 2, N], F32R), m.sb("d_h_lo", [P, 2, N], F32R)
        hidden, scaled = m.sb("d_hidden", [P, 2, Q1, N]), m.sb("d_scaled", [P, 2, N])
        gate_alpha, gate_b2 = m.sb("d_gate_alpha", [P, 2, D]), m.sb("d_gate_b2", [P, 2, D])
        ps_up, ps_y, ps_h = [m.ps(f"d_ps_up{q}") for q in range(Q1)], [m.ps(f"d_ps_y{p}") for p in (0, 1)], m.ps("d_ps_h")
        S = m.sem
        h_done, hi_done, lo_done, up_done, gelu_done = S("d_h_done"), S("d_hi_done"), S("d_lo_done"), S("d_up_done"), S("d_gelu_done")
        gates_done, pre_done, y_done, scaled_done, x_done, stored = (
            S("d_gates_done"), S("d_pre_done"), S("d_y_done"), S("d_scaled_done"), S("d_x_done"), S("d_stored"))
        with nc.Block() as block:

            @block.sync
            def _(eng):
                with eng.Fori(0, B) as s:
                    eng.wait_ge(x_done, s + 1)
                    eng.dma_start(out[s, :, :].rearrange("(t p) d -> p t d", p=P), k.x[:, s, :, :]).then_inc(stored, 16)
                eng.wait_ge(stored, 16 * B)

            @block.gpsimd
            def _(eng):
                norm.pool_setup(eng)
                norm.pool_rstd(eng, 0, 0)

                def body(s, nxt, p):
                    if nxt is not None:
                        norm.pool_rstd(eng, nxt, 1 - p)
                    eng.wait_ge(scaled_done, s)
                    eng.tensor_tensor(gate_alpha[:, p, :], w.alpha2[:, :], k.gates[:, s, 3, :], ALU.mult)
                    eng.tensor_tensor(gate_b2[:, p, :], w.b2[:, :], k.gates[:, s, 3, :], ALU.mult).then_inc(gates_done, 1)
                    eng.wait_ge(gates_done, s + 1)
                    eng.wait_ge(norm.xn_done, s + 1)
                    eng.tensor_tensor(k.x[:, s, :, :], k.x[:, s, :, :],
                                      gate_b2[:, p, :].unsqueeze(1).to_broadcast([P, T, D]), ALU.add).then_inc(pre_done, 1)

                one_ahead(eng, body)

            @block.tensor
            def _(eng):
                norm.tensor_turn(eng, ps_h, 0, 0)

                def body(s, nxt, p):
                    eng.wait_ge(hi_done, s + 1)
                    eng.wait_ge(lo_done, s + 1)
                    for q in range(Q1):
                        eng.matmul(ps_up[q][:, :], w.sign1T[:, q, :], h_hi[:, p, :], start=True, stop=False)
                        eng.matmul(ps_up[q][:, :], w.sign1T[:, q, :], h_lo[:, p, :], start=False, stop=True).then_inc(up_done, 1)
                    for q in range(Q1):
                        eng.wait_ge(gelu_done, s * Q1 + q + 1)
                        for t in range(T):
                            last = eng.matmul(ps_y[p][:, t * P:(t + 1) * P], hidden[:, p, q, t * P:(t + 1) * P], w.sign2T[:, q, :],
                                              start=(q == 0 and t == 0), stop=(q == Q1 - 1), skip_group_check=True)
                        if q == 0 and nxt is not None:
                            norm.tensor_turn(eng, ps_h, nxt, 1 - p)
                    last.then_inc(y_done, 1)

                one_ahead(eng, body)

            @block.scalar
            def _(eng):
                def modulate(s, p):
                    norm.scalar_modulate(eng, ps_h, hT[:, p, :], s).then_inc(h_done, 1)
                    eng.wait_ge(h_done, s + 1)
                    eng.activation(h_hi[:, p, :], hT[:, p, :], ACT.Copy).then_inc(hi_done, 1)

                modulate(0, 0)

                def body(s, nxt, p):
                    for q in range(Q1):
                        eng.wait_ge(up_done, s * Q1 + q + 1)
                        eng.activation(hidden[:, p, q, :], ps_up[q][:, :], ACT.Gelu, scale=w.alpha1[:, q:q + 1],
                                       bias=w.b1[:, q:q + 1]).then_inc(gelu_done, 1)
                    if nxt is not None:
                        modulate(nxt, 1 - p)

                one_ahead(eng, body)

            @block.vector
            def _(eng):
                def low(s, p):
                    eng.wait_ge(hi_done, s + 1)
                    eng.tensor_tensor(h_lo[:, p, :], hT[:, p, :], h_hi[:, p, :].bitcast(F32), ALU.subtract).then_inc(lo_done, 1)

                norm.vector_stats(eng, 0, 0)
                norm.vector_normalise(eng, 0, 0)
                low(0, 0)

                def finish(s, p):
                    eng.wait_ge(y_done, s + 1)
                    eng.wait_ge(gates_done, s + 1)
                    eng.tensor_tensor(scaled[:, p, :].rearrange("p (t d) -> p t d", t=T), ps_y[p][:, :].rearrange("p (t d) -> p t d", t=T),
                                      gate_alpha[:, p, :].unsqueeze(1).to_broadcast([P, T, D]), ALU.mult).then_inc(scaled_done, 1)
                    eng.wait_ge(scaled_done, s + 1)
                    eng.wait_ge(pre_done, s + 1)
                    xs = k.x[:, s, :, :].rearrange("p t d -> p (t d)")
                    eng.tensor_tensor(xs, scaled[:, p, :], xs, ALU.add).then_inc(x_done, 1)

                def body(s, nxt, p, last):
                    if nxt is not None:
                        norm.vector_stats(eng, nxt, 1 - p)
                        norm.vector_normalise(eng, nxt, 1 - p)
                    if last is not None:
                        finish(last, 1 - p)
                    if nxt is not None:
                        low(nxt, 1 - p)

                neighbours(eng, body)
                finish(B - 1, 1)


class Kept:

    def __init__(self, nc, m):
        self.x = m.sb("x", [P, B, T, D])
        self.ident = m.sb("ident", [P, P])
        self.mods = m.sb("mods", [P, 2, 4, B])
        self.gates = m.sb("gates", [P, B, 4, D])
        self.passed, self.gates_in = m.sem("passed"), m.sem("gates_in")
        self.scratch = nc.dram_tensor("gate_scratch", [B, 4 * D], F32, kind="Internal").ap()


def two_blocks(nc, a, out):
    with ExitStack() as stack:
        m = Memory(nc, stack)
        k = Kept(nc, m)
        with ExitStack() as linear_stack:
            w = Linear(Memory(nc, linear_stack))
            prepare(nc, a, k, w)
            linear_attention(nc, a, k, w)
        with ExitStack() as latent_stack:
            w = Latent(Memory(nc, latent_stack))
            with ExitStack() as raw_stack:
                raw = LatentRaw(Memory(nc, raw_stack), w)
                with ExitStack() as moe_stack:
                    r = Router(Memory(nc, moe_stack))
                    routing(nc, a, k, r)
                    expert_layers(nc, a, k, r, raw)
                fold_latent(nc, a, k, w, raw)
            latent_attention(nc, a, k, w)
        with ExitStack() as binary_stack:
            w = Binary(Memory(nc, binary_stack))
            binarise(nc, a, k, w)
            feed_forward(nc, a, k, w, out)


def shape_constants():
    c = np.arange(P)
    inv_freq = (1.0 / 10000.0 ** (np.arange(0, HD0, 2, dtype=np.float32) / HD0)).astype(np.float32)
    angle = np.arange(N, dtype=np.float32)[None, :] * inv_freq[c % (HD0 // 2)][:, None]
    sign = np.where(c % HD0 < HD0 // 2, -1.0, 1.0).astype(np.float32)[:, None]
    spread = np.zeros((P, 4, G0, P), np.float32)
    for g in range(G0):
        for quadrant in range(4):
            rows, cols = 32 * g + np.arange(32), 32 * quadrant + np.arange(32)
            spread[rows, 0 if quadrant % 2 == 0 else 1, g, cols] = 1.0
            spread[rows, 2 if quadrant < 2 else 3, g, cols] = 1.0
    f = np.float32
    pick = np.zeros((64, DYN_UNITS + 1, P), f)
    for u in range(DYN_UNITS + 1):
        expert = np.where(u < DYN_UNITS, 2 * u + c // I_DYN, E_DYN)
        pick[expert, u, c] = pick[32 + expert, u, c] = 1.0
    place = np.zeros((DC + 1, P), f)
    for copy in range(3):
        place[np.arange(DC), copy * DC + np.arange(DC)] = 1.0
    place[DC, 3 * DC:3 * DC + 2] = 1.0
    column = lambda mask: np.where(mask, -1.0, 0.0).astype(f)[:, None]
    return {
        "place": place, "low_w": column(((c >= 2 * DC) & (c < 3 * DC)) | (c == 3 * DC + 1)),
        "q_low": column((c >= DC) & (c < 2 * DC)), "upper_low": column(c >= DKV),
        "experts": np.tile(np.arange(E_DYN, dtype=f), (P, 1)),
        "pick": pick.reshape(64, -1), "low_rows": np.where(np.arange(64) < 32, 0.0, -1.0).astype(f)[:, None],
        "ident": np.eye(P, dtype=f),
        "cos": np.cos(angle).astype(f), "sin": (np.sin(angle) * sign).astype(f),
        "causal": (c[:, None] <= c[None, :]).astype(f),
        "own_head": (c[:, None] // HD0 == c[None, :] // HD0).astype(f),
        "head_rows": ((c[:, None] % 32) // HD0 == np.arange(J0)[None, :]).astype(f),
        "spread": spread.reshape(P, -1),
    }


_INS = ["L0_attn_x", "L0_attn_Wq", "L0_attn_Wk", "L0_attn_Wv", "L0_attn_Wo", "L0_attn_Wg1", "L0_attn_Wg2", "L0_attn_ln_w",
        "L0_attn_ln_b", "L0_ffn_gate_w", "L0_ffn_dyn_gate_w", "L0_ffn_dyn_up_w", "L0_ffn_dyn_down_w", "L0_ffn_sh_gate_w",
        "L0_ffn_sh_up_w", "L0_ffn_sh_down_w", "L0_c", "L0_wmod", "L1_attn_W_DQ", "L1_attn_b_DQ", "L1_attn_W_UQ",
        "L1_attn_b_UQ", "L1_attn_W_DKV", "L1_attn_b_DKV", "L1_attn_W_UK", "L1_attn_b_UK", "L1_attn_W_UV", "L1_attn_b_UV",
        "L1_attn_W_QR", "L1_attn_b_QR", "L1_attn_W_KR", "L1_attn_b_KR", "L1_attn_W_O", "L1_attn_b_O", "L1_ffn_w1",
        "L1_ffn_b1", "L1_ffn_w2", "L1_ffn_b2", "L1_c", "L1_wmod"]


def kernel(**inputs):
    import concourse.bacc as _bacc
    from concourse.bass_utils import run_bass_kernel_spmd as _run

    nc = _bacc.Bacc("TRN2", target_bir_lowering=False, num_devices=1)
    arrays, args = {}, {}
    tables = shape_constants()
    for name in [*_INS, *tables]:
        array = np.ascontiguousarray(tables[name] if name in tables else inputs[name])
        arrays[f"in_{name}_dram"] = array
        args[name] = nc.dram_tensor(f"in_{name}_dram", array.shape, mybir.dt.from_np(array.dtype), kind="ExternalInput").ap()
    out = nc.dram_tensor("out_0_dram", (B, N, D), F32, kind="ExternalOutput").ap()
    two_blocks(nc, args, out)
    result = _run(nc, [arrays], core_ids=[0])
    return result.results[0]["out_0_dram"]
```
